# Optimizing a Trainium2 kernel written in Bass

```python
import numpy as np
import jax
import jax.numpy as jnp

def _softmax(x, axis=-1):
    return jax.nn.softmax(x, axis=axis)

def _gelu(x):
    return jax.nn.gelu(x, approximate=True)

def _silu(x):
    return jax.nn.silu(x)

def _sigmoid(x):
    return jax.nn.sigmoid(x)

def _layernorm(x, axis=-1, eps=1e-05):
    m = jnp.mean(x, axis=axis, keepdims=True)
    v = jnp.var(x, axis=axis, keepdims=True)
    return (x - m) / jnp.sqrt(v + eps)

def _scatter_add(tgt, idx, src, axis=0):
    return tgt.at[idx].add(src)

def _segment_sum(src, seg, n):
    return jax.ops.segment_sum(src, seg, n)
kernel_name = 'mk_gps_d1_gnn_r8_19f23a'

def setup_inputs(seed: int=0):
    np.random.seed(seed)
    _w = jnp.asarray

    def _rec_inputs():
        import jax
        import jax.numpy as jnp
        _gk = jax.random.key(seed)
        x = -0.0003929 + 0.9999 * jax.random.normal(jax.random.fold_in(_gk, 1), (1250, 1024), jnp.float32)
        src = jax.random.randint(jax.random.fold_in(_gk, 2), (20000,), 0, 1250, jnp.int32)
        dst = jax.random.randint(jax.random.fold_in(_gk, 3), (20000,), 0, 1250, jnp.int32)
        _o = jnp.argsort(dst, stable=True)
        src = src[_o]
        dst = dst[_o]
        edge_weight = jax.random.uniform(jax.random.fold_in(_gk, 12), (20000,), jnp.float32, 0.0, 0.999994)
        return (x, src, dst, edge_weight)
    x, src, dst, edge_weight = _rec_inputs()

    def _L0_gnn_setup():
        import jax, jax.numpy as jnp
        import numpy as np
        N_NODES = 2048
        N_EDGES = 16384
        D = 1024
        key = jax.random.key(seed)
        k_x, k_w, k_W, k_s, k_d = jax.random.split(key, 5)
        x = jax.random.normal(k_x, (N_NODES, D), dtype=jnp.float32)
        edge_w = jax.random.uniform(k_w, (N_EDGES,), dtype=jnp.float32)
        W = jax.random.normal(k_W, (D, D), dtype=jnp.float32) * (1.0 / np.sqrt(D))
        b = jnp.zeros((D,), dtype=jnp.float32)
        src = jax.random.randint(k_s, (N_EDGES,), 0, N_NODES)
        dst = jax.random.randint(k_d, (N_EDGES,), 0, N_NODES)
        return {'x': x, 'edge_w': edge_w, 'W': W, 'b': b, 'src': src, 'dst': dst}
    _L0_gnn_all = _L0_gnn_setup()
    _L0_gnn_in = {k: v for k, v in _L0_gnn_all.items() if k in ('W', 'b')}
    del _L0_gnn_all

    def _L0_mix_setup():
        import math
        import jax, jax.numpy as jnp
        import numpy as np
        N_HEADS = 16

        def _phi(x, rf, m):
            norms_sq = jnp.sum(x * x, axis=-1, keepdims=True)
            proj = jnp.einsum('bhtd,md->bhtm', x, rf)
            scale = jnp.exp(-norms_sq * 0.5) / math.sqrt(m)
            return jnp.concatenate([jnp.cos(proj), jnp.sin(proj)], axis=-1) * scale
        key = jax.random.key(seed)
        ks = jax.random.split(key, 6)
        B, T, D = (2, 512, 1024)
        m, dh = (256, D // N_HEADS)
        x = jax.random.normal(ks[0], (B, T, D), dtype=jnp.float32)
        s = 1.0 / math.sqrt(D)
        wq = jax.random.normal(ks[1], (D, D), dtype=jnp.float32) * s
        wk = jax.random.normal(ks[2], (D, D), dtype=jnp.float32) * s
        wv = jax.random.normal(ks[3], (D, D), dtype=jnp.float32) * s
        wo = jax.random.normal(ks[4], (D, D), dtype=jnp.float32) * s
        rf = jax.random.normal(ks[5], (m, dh), dtype=jnp.float32) / math.sqrt(dh)
        return {'x': x, 'wq': wq, 'wk': wk, 'wv': wv, 'wo': wo, 'rf': rf}
    _L0_mix_all = _L0_mix_setup()
    _L0_mix_in = {k: v for k, v in _L0_mix_all.items() if k in ('wq', 'wk', 'wv', 'wo', 'rf')}
    del _L0_mix_all

    def _L0_ffn_setup():
        import jax, jax.numpy as jnp
        import numpy as np
        HIDDEN = 1024
        INNER = 512

        def _weight_quant(w):
            scale = 1.0 / jnp.clip(jnp.mean(jnp.abs(w)), 1e-05)
            wq = jnp.clip(jnp.round(w * scale), -1.0, 1.0) / scale
            return w + jax.lax.stop_gradient(wq - w)

        def _act_quant(x):
            scale = 127.0 / jnp.clip(jnp.max(jnp.abs(x), axis=-1, keepdims=True), 1e-05)
            xq = jnp.clip(jnp.round(x * scale), -128.0, 127.0) / scale
            return x + jax.lax.stop_gradient(xq - x)

        def _bitlinear(x, w):
            return jnp.einsum('bsi,oi->bso', _act_quant(x), _weight_quant(w))
        key = jax.random.key(seed)
        k0, k1, k2, k3 = jax.random.split(key, 4)
        x = jax.random.normal(k0, (4, 256, HIDDEN), dtype=jnp.float32)
        w_gate = jax.random.normal(k1, (INNER, HIDDEN), dtype=jnp.float32) / np.sqrt(HIDDEN)
        w_up = jax.random.normal(k2, (INNER, HIDDEN), dtype=jnp.float32) / np.sqrt(HIDDEN)
        w_down = jax.random.normal(k3, (HIDDEN, INNER), dtype=jnp.float32) / np.sqrt(INNER)
        return {'x': x, 'w_gate': w_gate, 'w_up': w_up, 'w_down': w_down}
    _L0_ffn_all = _L0_ffn_setup()
    _L0_ffn_in = {k: v for k, v in _L0_ffn_all.items() if k in ('w_gate', 'w_up', 'w_down')}
    del _L0_ffn_all
    return {'x': x, 'src': src, 'dst': dst, 'edge_weight': edge_weight, 'L0_gnn_W': _L0_gnn_in['W'], 'L0_gnn_b': _L0_gnn_in['b'], 'L0_mix_wq': _L0_mix_in['wq'], 'L0_mix_wk': _L0_mix_in['wk'], 'L0_mix_wv': _L0_mix_in['wv'], 'L0_mix_wo': _L0_mix_in['wo'], 'L0_mix_rf': _L0_mix_in['rf'], 'L0_ffn_w_gate': _L0_ffn_in['w_gate'], 'L0_ffn_w_up': _L0_ffn_in['w_up'], 'L0_ffn_w_down': _L0_ffn_in['w_down']}

def reference(x, src, dst, edge_weight, L0_gnn_W, L0_gnn_b, L0_mix_wq, L0_mix_wk, L0_mix_wv, L0_mix_wo, L0_mix_rf, L0_ffn_w_gate, L0_ffn_w_up, L0_ffn_w_down):
    import jax
    import jax.numpy as jnp

    def _L0_gnn_ref(x, edge_w, W, b, src, dst):
        import jax, jax.numpy as jnp
        import numpy as np
        N_NODES = 2048
        N_EDGES = 16384
        D = 1024
        "EdgeWeightNorm(norm='both') -> GraphConv(norm='both', weight, bias) -> ReLU.\n\n            Matches DGL semantics:\n              c_ij   = w_ij / sqrt(sum_out_w[src] * sum_in_w[dst])   (EdgeWeightNorm 'both')\n              h_j    = relu( D_in[j]^-1/2 * sum_i c_ij * D_out[i]^-1/2 * x_i  @ W + b )\n            where D_out/D_in are structural degrees clamped to >= 1.\n            "
        n = x.shape[0]
        ones = jnp.ones_like(edge_w)
        w_out = jax.ops.segment_sum(edge_w, src, num_segments=n)
        w_in = jax.ops.segment_sum(edge_w, dst, num_segments=n)
        c = edge_w * jax.lax.rsqrt(w_out[src] * w_in[dst])
        deg_out = jnp.clip(jax.ops.segment_sum(ones, src, num_segments=n), 1.0)
        deg_in = jnp.clip(jax.ops.segment_sum(ones, dst, num_segments=n), 1.0)
        xs = x * jax.lax.rsqrt(deg_out)[:, None]
        msg = xs[src] * c[:, None]
        agg = jax.ops.segment_sum(msg, dst, num_segments=n)
        agg = agg * jax.lax.rsqrt(deg_in)[:, None]
        return jax.nn.relu(agg @ W + b)

    def _L0_mix_ref(x, wq, wk, wv, wo, rf):
        import math
        import jax, jax.numpy as jnp
        import numpy as np
        N_HEADS = 16

        def _phi(x, rf, m):
            norms_sq = jnp.sum(x * x, axis=-1, keepdims=True)
            proj = jnp.einsum('bhtd,md->bhtm', x, rf)
            scale = jnp.exp(-norms_sq * 0.5) / math.sqrt(m)
            return jnp.concatenate([jnp.cos(proj), jnp.sin(proj)], axis=-1) * scale
        B, T, D = x.shape
        H = N_HEADS
        Dh = D // H
        m = rf.shape[0]

        def heads(w):
            return (x @ w.T).reshape(B, T, H, Dh).transpose(0, 2, 1, 3)
        Q, K, V = (heads(wq), heads(wk), heads(wv))
        Qf = _phi(Q, rf, m)
        Kf = _phi(K, rf, m)
        KV = jnp.einsum('bhnd,bhnv->bhdv', Kf, V)
        QKV = jnp.einsum('bhnd,bhdv->bhnv', Qf, KV)
        K_sum = jnp.sum(Kf, axis=2)
        Z = jnp.maximum(jnp.einsum('bhnd,bhd->bhn', Qf, K_sum)[..., None], 1e-06)
        out = (QKV / Z).transpose(0, 2, 1, 3).reshape(B, T, D)
        return out @ wo.T

    def _L0_ffn_ref(x, w_gate, w_up, w_down):
        import jax, jax.numpy as jnp
        import numpy as np
        HIDDEN = 1024
        INNER = 512

        def _weight_quant(w):
            scale = 1.0 / jnp.clip(jnp.mean(jnp.abs(w)), 1e-05)
            wq = jnp.clip(jnp.round(w * scale), -1.0, 1.0) / scale
            return w + jax.lax.stop_gradient(wq - w)

        def _act_quant(x):
            scale = 127.0 / jnp.clip(jnp.max(jnp.abs(x), axis=-1, keepdims=True), 1e-05)
            xq = jnp.clip(jnp.round(x * scale), -128.0, 127.0) / scale
            return x + jax.lax.stop_gradient(xq - x)

        def _bitlinear(x, w):
            return jnp.einsum('bsi,oi->bso', _act_quant(x), _weight_quant(w))
        gate = jax.nn.silu(_bitlinear(x, w_gate))
        up = _bitlinear(x, w_up)
        return _bitlinear(gate * up, w_down)
    xn = _layernorm(x, axis=-1)
    x = x + _L0_gnn_ref(xn, edge_weight, L0_gnn_W, L0_gnn_b, src, dst) + _L0_mix_ref(xn[None], L0_mix_wq, L0_mix_wk, L0_mix_wv, L0_mix_wo, L0_mix_rf)[0]
    x = x + _L0_ffn_ref(_layernorm(x, axis=-1)[None], L0_ffn_w_gate, L0_ffn_w_up, L0_ffn_w_down)[0]
    return x

_drawn_inputs = setup_inputs


def setup_inputs(seed=0):
    import zlib

    import numpy as np

    out = dict(_drawn_inputs(seed))
    spreads = {'L0_gnn_b': (0.0, 0.1)}
    factors = {'edge_weight': 6.802, 'L0_gnn_W': 3.893}
    for name, (base, spread) in spreads.items():
        noise = np.random.default_rng([zlib.crc32(name.encode()), seed]).standard_normal(out[name].shape)
        drawn = base * np.exp(spread * noise) if base else spread * noise
        out[name] = jnp.asarray(drawn.astype(out[name].dtype))
    for name, factor in factors.items():
        out[name] = (out[name] * factor).astype(out[name].dtype)
    return out
```

```python
import concourse.bass as bass
from concourse import mybir
from contextlib import ExitStack
import numpy as np

F32 = mybir.dt.float32
F32R = mybir.dt.float32r
BF16 = mybir.dt.bfloat16
I32 = mybir.dt.int32
I16 = mybir.dt.int16
ACT = mybir.ActivationFunctionType
ALU = mybir.AluOpType
AX = mybir.AxisListType

N = 1250
D = 1024
E = 20000
P = 128
TR = 125
NT = N // TR
KD = D // P
NC = E // TR
CR = NC // 2
WIN = 25
NW = N // WIN
NWT = NW + 1
WPT = TR // WIN
PARTS = 3
OHW = (NT - 1) * TR + P
PREP_STEPS = 27
NP = NC // 2
LN_EPS = 1e-5


def node_stage(nc, x, src, dst, edge_weight, gnn_w, y_scr, xt_scr, at_scr, edge_scr):
    with ExitStack() as ctx:
        def sb(name, shape, dt):
            return ctx.enter_context(nc.sbuf_tensor(name, shape, dt))

        def pb(name, shape, dt=F32):
            return ctx.enter_context(nc.psum_tensor(name, shape, dt))

        def sem(name):
            return ctx.enter_context(nc.semaphore(name))

        ident = sb("n_ident", [P, P], F32)
        xin = [sb(f"n_xin{s}", [TR, D], F32) for s in range(2)]
        xn = [sb(f"n_xn{s}", [TR, D], F32) for s in range(2)]
        xt = [sb(f"n_xt{s}", [P, 2, KD, TR], F32R) for s in range(2)]
        w_raw = [sb(f"n_wraw{s}", [P, D], F32) for s in range(2)]
        w_hi = sb("n_whi", [P, KD, D], F32R)
        w_lo = sb("n_wlo", [P, KD, D], F32R)
        ysb = [sb(f"n_y{s}", [TR, D], F32) for s in range(2)]
        bn = [sb(f"n_bn{s}", [TR, 2, 6], F32) for s in range(2)]
        mv = [sb(f"n_mv{s}", [TR, 2], F32) for s in range(2)]
        std = [sb(f"n_std{s}", [TR, 1], F32) for s in range(2)]
        rstd = [sb(f"n_rstd{s}", [TR, 1], F32) for s in range(2)]
        nmr = [sb(f"n_nmr{s}", [TR, 1], F32) for s in range(2)]
        eps = sb("n_eps", [TR, 1], F32)
        src_r = sb("n_srcr", [CR, 2, TR], I32)
        dst_r = sb("n_dstr", [CR, 2, TR], I32)
        w_r = sb("n_wr", [CR, 2, TR], F32)
        src_f = sb("n_srcf", [CR, 2, TR], F32)
        dst_f = sb("n_dstf", [CR, 2, TR], F32)
        dmm = sb("n_dmm", [CR, 2, 2], F32)
        dmm_b = sb("n_dmmb", [CR, 2, 2, NWT], F32)
        edge_t = sb("n_edget", [TR, 3, NC], F32)
        wrest = sb("n_wrest", [TR, 2, NC], F32)
        wpart = sb("n_wpart", [TR, NC, PARTS], BF16)
        dloc = sb("n_dloc", [TR, 2, NC], F32)
        iota_s = sb("n_iotas", [TR, OHW + 3], I16)
        iota_d = sb("n_iotad", [TR, PARTS, WIN], I16)
        oh_s = sb("n_ohs", [TR, 2, OHW + 3], BF16)
        oh_d = sb("n_ohd", [TR, 2, PARTS * WIN], BF16)
        zero = sb("n_zero", [1, P], BF16)
        at = [sb(f"n_at{s}", [TR, NT, WIN], F32) for s in range(2)]
        wlo = sb("n_wlo_v", [NWT, 2], F32)
        iota_w = sb("n_iotaw", [NWT, 2], I32)
        cnum = sb("n_cnum", [NWT, 2, NP], F32)
        cnum_i = sb("n_cnumi", [NWT, 2, NP], I32)
        inwin = sb("n_inwin", [NWT, NC], F32)
        cand = sb("n_cand", [NWT, 2, NP], F32)
        inpair = sb("n_inpair", [NWT, NP], F32)
        rng = sb("n_rng", [NWT, 4], F32)
        tri = sb("n_tri", [NWT, NWT], F32)
        table = sb("n_table", [1, NWT * 4], I32)
        wbase_i = sb("n_wbasei", [TR, NWT], I32)
        wbase = sb("n_wbase", [TR, NWT], F32)

        ps_t = [pb(f"n_pst{s}", [P, 512]) for s in range(2)]
        ps_y = [pb(f"n_psy{s}", [TR, 512]) for s in range(2)]
        ps_a = [[pb(f"n_psa{s}{b}", [P, 512]) for b in range(2)] for s in range(2)]

        s_edge = sem("n_edge_loaded")
        s_x = [sem(f"n_x_loaded{s}") for s in range(2)]
        s_w = [sem(f"n_w_loaded{s}") for s in range(2)]
        s_ident = sem("n_const")
        s_split = sem("n_w_high")
        s_wlow = sem("n_w_low")
        s_prep = sem("n_prep")
        s_prep_pe = sem("n_prep_pe")
        s_stat = sem("n_stat")
        s_std = sem("n_std")
        s_xn = sem("n_xn")
        s_tp = sem("n_transposed")
        s_hi = sem("n_xt_high")
        s_lo = sem("n_xt_low")
        s_yp = sem("n_y_product")
        s_ye = sem("n_y_evacuated")
        s_ys = [sem(f"n_y_stored{s}") for s in range(2)]
        s_xs = [sem(f"n_xt_stored{s}") for s in range(2)]
        s_dl = sem("n_dloc_ready")
        s_ohr = sem("n_onehot_ready")
        s_ohu = sem("n_onehot_used")
        s_wr = sem("n_window_ready")
        s_we = sem("n_window_evacuated")
        s_as = [sem(f"n_window_stored{s}") for s in range(2)]

        PS = 5
        block = ctx.enter_context(nc.Block())

        @block.sync
        def _(sp):
            half = "(t r e) -> r t e"
            sp.dma_start(src_r[:, :, :], src.rearrange(half, t=2, r=CR)).then_inc(s_edge, 16)
            sp.dma_start(dst_r[:, :, :], dst.rearrange(half, t=2, r=CR)).then_inc(s_edge, 16)
            sp.dma_start(w_r[:, :, :], edge_weight.rearrange(half, t=2, r=CR)).then_inc(s_edge, 16)
            for s in range(2):
                sp.dma_start(xin[s][:, :], x[s * TR:(s + 1) * TR, :]).then_inc(s_x[s], 16)
            for k in range(KD):
                if k >= 2:
                    sp.wait_ge(s_wlow, k - 1)
                sp.dma_start(w_raw[k % 2][:, :], gnn_w[k * P:(k + 1) * P, :]).then_inc(s_w[k % 2], 16)
            for s in range(2):
                sp.sem_inc(s_as[s], 16)
                sp.sem_inc(s_ys[s], 16)
                sp.sem_inc(s_xs[s], 16)
            sp.wait_ge(s_prep, 9)
            sp.dma_start(edge_scr, edge_t[:, :, :]).then_inc(s_edge, 16)
            with sp.Fori(0, NT // 2) as i:
                for s in range(2):
                    sp.wait_ge(s_lo, (i * 2 + s + 1) * 2 + 2)
                    sp.dma_start(xt_scr[bass.ds(i * 2 + s, 1), :, :].rearrange("a p n -> p (a n)"),
                                 xt[s][:, :, :, :].rearrange("p h k n -> p (h k n)").bitcast(F32)).then_inc(s_xs[s], 16)
                    nxt = sp.snap((i * 2 + s + 2) % NT)
                    sp.wait_ge(s_xn, i * 2 + s + 1)
                    sp.dma_start(xin[s][:, :], x[bass.ds(nxt * TR, TR), :]).then_inc(s_x[s], 16)
                    for q in range(WPT):
                        w = (i * 2 + s) * WPT + q
                        sp.wait_ge(s_we, w + 3)
                        sp.dma_start(at_scr[bass.ds(w, 1), :, :].rearrange("a p n -> p (a n)"),
                                     at[(s * WPT + q) % 2][:, :, :].rearrange("p j d -> p (j d)")
                                     ).then_inc(s_as[(s * WPT + q) % 2], 16)
                    sp.wait_ge(s_ye, (i * 2 + s + 1) * 2 + 2)
                    sp.dma_start(y_scr[bass.ds(i * 2 + s, 1), :, :].rearrange("a p n -> p (a n)"),
                                 ysb[s][:, :]).then_inc(s_ys[s], 16)
            sp.wait_ge(s_x[0], (NT // 2 + 1) * 16)
            sp.wait_ge(s_x[1], (NT // 2 + 1) * 16)
            for s in range(2):
                sp.wait_ge(s_xs[s], (NT // 2 + 1) * 16)
                sp.wait_ge(s_as[s], (NW // 2 + 1) * 16)
                sp.wait_ge(s_ys[s], (NT // 2 + 1) * 16)
            sp.wait_ge(s_edge, 64)

        @block.gpsimd
        def _(pool):
            nc.gpsimd.memset(ident[:, :], 0.0).then_inc(s_ident, 1)
            nc.gpsimd.memset(tri[:, :], 0.0).then_inc(s_ident, 1)
            nc.gpsimd.memset(zero[:, :], 0.0).then_inc(s_ident, 1)
            nc.gpsimd.memset(eps[:, :], LN_EPS).then_inc(s_ident, 1)
            nc.gpsimd.iota(iota_s[:, :], pattern=[[1, OHW + 3]], base=0, channel_multiplier=0).then_inc(s_ident, 1)
            nc.gpsimd.iota(iota_d[:, :, :], pattern=[[0, PARTS], [1, WIN]], base=0,
                           channel_multiplier=0).then_inc(s_ident, 1)
            nc.gpsimd.iota(iota_w[:, :], pattern=[[WIN, 2]], base=0, channel_multiplier=WIN).then_inc(s_ident, 1)
            nc.gpsimd.iota(cnum_i[:, 0, :], pattern=[[1, NP]], base=1, channel_multiplier=0).then_inc(s_ident, 1)
            nc.gpsimd.iota(cnum_i[:, 1, :], pattern=[[-1, NP]], base=NP, channel_multiplier=0).then_inc(s_ident, 1)
            nc.gpsimd.iota(wbase_i[:, :], pattern=[[WIN, NWT]], base=0, channel_multiplier=0).then_inc(s_ident, 1)
            pool.wait_ge(s_ident, 10)
            nc.gpsimd.affine_select(out=ident[:, :], in_=ident[:, :], compare_op=ALU.not_equal, fill=1.0,
                                    base=0, pattern=[[-1, P]], channel_multiplier=1).then_inc(s_ident, 1)
            nc.gpsimd.affine_select(out=tri[:, :], in_=tri[:, :], compare_op=ALU.is_ge, fill=1.0,
                                    base=0, pattern=[[-1, NWT]], channel_multiplier=1).then_inc(s_ident, 1)

        @block.scalar
        def _(act):
            def normalise(s, count):
                act.wait_ge(s_stat, count * PS + 3)
                nc.scalar.activation(std[s][:, :], mv[s][:, 1:2], ACT.Sqrt, bias=eps[:, 0:1]).then_inc(s_std, 1)
                act.wait_ge(s_stat, count * PS + 5)
                nc.scalar.activation(xn[s][:, :], xin[s][:, :], ACT.Identity, bias=nmr[s][:, 0:1],
                                     scale=rstd[s][:, 0:1]).then_inc(s_xn, 1)

            act.wait_ge(s_ident, 12)
            normalise(0, 0)
            for k in range(KD):
                act.wait_ge(s_w[k % 2], (k // 2 + 1) * 16)
                nc.scalar.activation(w_hi[:, k, :], w_raw[k % 2][:, :], ACT.Copy).then_inc(s_split, 1)
            with act.Fori(0, NT // 2) as i:
                for s in range(2):
                    t = i * 2 + s
                    act.wait_ge(s_xs[s], (i + 1) * 16)
                    for b in range(2):
                        act.wait_ge(s_tp, t * 2 + b + 1)
                        nc.scalar.activation(
                            xt[s][:, 0, 4 * b:4 * b + 4, :],
                            ps_t[b][:, 0:4 * TR].rearrange("p (k n) -> p k n", k=4), ACT.Copy).then_inc(s_hi, 1)
                    normalise(1 - s, t + 1)
                    act.wait_ge(s_ys[s], (i + 1) * 16)
                    for b in range(2):
                        act.wait_ge(s_yp, t * 2 + b + 1)
                        nc.scalar.activation(ysb[s][:, b * 512:(b + 1) * 512], ps_y[b][:, :],
                                             ACT.Copy).then_inc(s_ye, 1)

        @block.vector
        def _(dve):
            prep = [0]

            def step(ins):
                prep[0] += 1
                ins.then_inc(s_prep, 1)
                dve.wait_ge(s_prep, prep[0])

            def statistics(s, count, loaded):
                dve.wait_ge(s_x[s], loaded)
                nc.vector.bn_stats(bn[s][:, 0, :], xin[s][:, 0:512]).then_inc(s_stat, 1)
                nc.vector.bn_stats(bn[s][:, 1, :], xin[s][:, 512:1024]).then_inc(s_stat, 1)
                dve.drain()
                nc.vector.bn_aggr(mv[s][:, :], bn[s][:, :, :].rearrange("p a b -> p (a b)")).then_inc(s_stat, 1)
                dve.wait_ge(s_std, count + 1)
                nc.vector.reciprocal(rstd[s][:, :], std[s][:, :]).then_inc(s_stat, 1)
                dve.wait_ge(s_stat, count * PS + 4)
                nc.vector.scalar_tensor_tensor(out=nmr[s][:, :], in0=mv[s][:, 0:1], scalar=-1.0,
                                               in1=rstd[s][:, :], op0=ALU.mult, op1=ALU.mult).then_inc(s_stat, 1)

            statistics(0, 0, 16)
            dve.wait_ge(s_edge, 48)
            step(nc.vector.tensor_copy(src_f[:, :, :], src_r[:, :, :]))
            step(nc.vector.tensor_copy(dst_f[:, :, :], dst_r[:, :, :]))
            step(nc.vector.tensor_reduce(dmm[:, :, 0:1], dst_f[:, :, :], axis=AX.X, op=ALU.min))
            step(nc.vector.tensor_reduce(dmm[:, :, 1:2], dst_f[:, :, :], axis=AX.X, op=ALU.max))
            step(nc.vector.tensor_copy(dmm_b[:, :, :, :],
                                       dmm[:, :, :].unsqueeze(3).broadcast_to([CR, 2, 2, NWT])))
            dve.wait_ge(s_ident, 12)
            step(nc.vector.tensor_copy(wlo[:, :], iota_w[:, :]))
            step(nc.vector.tensor_copy(cnum[:, :, :], cnum_i[:, :, :]))
            step(nc.vector.tensor_copy(wbase[:, :], wbase_i[:, :]))
            dve.wait_ge(s_prep_pe, 1)
            step(nc.vector.tensor_copy(edge_t[:, :, :], ps_t[0][0:TR, 0:3 * NC].rearrange(
                "p (a c) -> p a c", a=3)))
            step(nc.vector.tensor_copy(wpart[:, :, 0], edge_t[:, 2, :]))
            step(nc.vector.tensor_tensor(wrest[:, 0, :], edge_t[:, 2, :], wpart[:, :, 0], ALU.subtract))
            step(nc.vector.tensor_copy(wpart[:, :, 1], wrest[:, 0, :]))
            step(nc.vector.tensor_tensor(wrest[:, 1, :], wrest[:, 0, :], wpart[:, :, 1], ALU.subtract))
            step(nc.vector.tensor_copy(wpart[:, :, 2], wrest[:, 1, :]))
            dve.wait_ge(s_prep_pe, 2)
            lows = ps_t[1][0:NWT, 0:2 * NC].rearrange("v (m c) -> v m c", m=2)
            step(nc.vector.tensor_scalar(inwin[:, :], lows[:, 0, :], wlo[:, 1:2], None, ALU.is_lt))
            step(nc.vector.scalar_tensor_tensor(out=inwin[:, :], in0=lows[:, 1, :], scalar=wlo[:, 0:1],
                                                in1=inwin[:, :], op0=ALU.is_ge, op1=ALU.mult))
            step(nc.vector.tensor_reduce(inpair[:, :], inwin[:, :].rearrange("v (c a) -> v c a", a=2),
                                         axis=AX.X, op=ALU.max))
            step(nc.vector.tensor_tensor(cand[:, :, :], cnum[:, :, :],
                                         inpair[:, :].unsqueeze(1).broadcast_to([NWT, 2, NP]), ALU.mult))
            step(nc.vector.tensor_reduce(rng[:, 0:2], cand[:, :, :], axis=AX.X, op=ALU.max))
            step(nc.vector.tensor_scalar(rng[:, 2:3], rng[:, 1:2], -1.0, float(NP), ALU.mult, ALU.add))
            step(nc.vector.tensor_copy(rng[:, 1:2], rng[:, 0:1]))
            step(nc.vector.tensor_scalar(rng[:, 0:1], rng[:, 2:3], float(NP - 1), None, ALU.min))
            step(nc.vector.tensor_scalar(rng[:, 3:4], rng[:, 0:1], 1.0, None, ALU.add))
            step(nc.vector.tensor_tensor(rng[:, 1:2], rng[:, 1:2], rng[:, 3:4], ALU.max))
            step(nc.vector.tensor_tensor(rng[:, 3:4], rng[:, 1:2], rng[:, 0:1], ALU.subtract))
            dve.wait_ge(s_prep_pe, 3)
            step(nc.vector.scalar_tensor_tensor(out=rng[:, 2:3], in0=ps_y[0][0:NWT, 0:1], scalar=float(NP),
                                                in1=rng[:, 0:1], op0=ALU.add, op1=ALU.subtract))
            dve.wait_ge(s_prep_pe, 4)
            step(nc.vector.tensor_copy(table[0:1, :].rearrange("p (v q) -> p q v", q=4),
                                       ps_y[1][0:1, 0:4 * NWT].rearrange("p (q v) -> p q v", q=4)))
            assert prep[0] == PREP_STEPS
            for k in range(KD):
                dve.wait_ge(s_split, k + 1)
                nc.vector.tensor_tensor(w_lo[:, k, :], w_raw[k % 2][:, :], w_hi[:, k, :].bitcast(F32),
                                        ALU.subtract).then_inc(s_wlow, 1)

            nc.vector.sem_inc(s_ohr, 2 * NP)

            def build(par, w):
                first = dve.value_load(table[0:1, bass.ds(w * 4, 1)], min_val=0, max_val=NP - 1)
                end = dve.value_load(table[0:1, bass.ds(w * 4 + 1, 1)], min_val=1, max_val=NP)
                shift = dve.value_load(table[0:1, bass.ds(w * 4 + 2, 1)], min_val=1, max_val=NWT * NP)
                nc.vector.tensor_scalar(dloc[:, par, :], edge_t[:, 1, :], wbase[:, bass.ds(w, 1)], None,
                                        ALU.subtract).then_inc(s_dl, 1)
                with dve.Fori(first, end) as pair:
                    visit = dve.snap((shift + pair) * 2)
                    for h in range(2):
                        c = dve.snap(pair * 2 + h)
                        dve.wait_ge(s_ohu, visit + h + 1)
                        nc.vector.tensor_scalar(oh_s[:, h, :], iota_s[:, :], edge_t[:, 0, bass.ds(c, 1)],
                                                None, ALU.is_equal)
                        dve.wait_ge(s_dl, w + 1)
                        nc.vector.scalar_tensor_tensor(
                            out=oh_d[:, h, :].rearrange("p (m d) -> p m d", m=PARTS),
                            in0=iota_d[:, :, :], scalar=dloc[:, par, bass.ds(c, 1)],
                            in1=wpart[:, bass.ds(c, 1), :].rearrange("p a m -> p (a m)").unsqueeze(2)
                            .broadcast_to([TR, PARTS, WIN]),
                            op0=ALU.is_equal, op1=ALU.mult).then_inc(s_ohr, 1)

            def sum_parts(s, q, i):
                w = (i * 2 + s) * WPT + q
                par = (s * WPT + q) % 2
                dve.wait_ge(s_wr, w + 1)
                dve.wait_ge(s_as[par], (i * WPT + (s * WPT + q) // 2 + 1) * 16)
                for b in range(2):
                    ins = nc.vector.tensor_reduce(
                        at[par][:, 5 * b:5 * b + 5, :],
                        ps_a[par][b][0:TR, 0:5 * PARTS * WIN].rearrange("p (j m d) -> p j d m", j=5, m=PARTS),
                        axis=AX.X, op=ALU.add)
                ins.then_inc(s_we, 1)

            build(0, 0)
            with dve.Fori(0, NT // 2) as i:
                for s in range(2):
                    t = i * 2 + s
                    for b in range(2):
                        dve.wait_ge(s_hi, t * 2 + b + 1)
                        nc.vector.tensor_tensor(
                            xt[s][:, 1, 4 * b:4 * b + 4, :],
                            ps_t[b][:, 0:4 * TR].rearrange("p (k n) -> p k n", k=4),
                            xt[s][:, 0, 4 * b:4 * b + 4, :].bitcast(F32), ALU.subtract
                        ).then_inc(s_lo, 1)
                    statistics(1 - s, t + 1, (i + 1 + s) * 16)
                    for q in range(WPT):
                        build((s * WPT + q + 1) % 2, dve.snap(t * WPT + q + 1))
                        sum_parts(s, q, i)

        @block.tensor
        def _(pe):
            pe.wait_ge(s_ident, 12)
            pe.wait_ge(s_prep, 2)
            for a, rows in enumerate((src_f, dst_f, w_r)):
                for h in range(2):
                    ins = nc.tensor.transpose(ps_t[0][0:TR, a * NC + h * CR:a * NC + (h + 1) * CR],
                                              rows[:, h, :], ident[0:CR, 0:CR])
            ins.then_inc(s_prep_pe, 1)
            pe.wait_ge(s_prep, 5)
            for m in range(2):
                for h in range(2):
                    ins = nc.tensor.matmul(ps_t[1][0:NWT, m * NC + h * CR:m * NC + (h + 1) * CR],
                                           dmm_b[:, h, m, :], ident[0:CR, 0:CR], start=True, stop=True)
            ins.then_inc(s_prep_pe, 1)
            pe.wait_ge(s_prep, PREP_STEPS - 2)
            nc.tensor.matmul(ps_y[0][0:NWT, 0:1], tri[:, :], rng[:, 3:4], start=True, stop=True).then_inc(s_prep_pe, 1)
            pe.wait_ge(s_prep, PREP_STEPS - 1)
            for q in range(4):
                ins = nc.tensor.matmul(ps_y[1][0:1, q * NWT:(q + 1) * NWT], rng[:, q:q + 1], ident[0:NWT, 0:NWT],
                                       start=True, stop=True)
            ins.then_inc(s_prep_pe, 1)
            pe.wait_ge(s_prep, PREP_STEPS)
            pe.wait_ge(s_wlow, KD)
            pe.sem_inc(s_ohu, 2 * NP + 2)
            pe.sem_inc(s_we, 2)
            pe.sem_inc(s_ye, 2)
            pe.sem_inc(s_lo, 2)

            PIECES = 2 * 3 * KD

            def product(s, t, lo, hi):
                for n in range(lo, hi):
                    b, m, k = n // (3 * KD), n // KD % 3, n % KD
                    part, w = ((0, w_hi), (0, w_lo), (1, w_hi))[m]
                    if n % (3 * KD) == 0:
                        pe.wait_ge(s_ye, t * 2 + b + 1)
                    ins = nc.tensor.matmul(ps_y[b][:, :], xt[s][:, part, k, :], w[:, k, b * 512:(b + 1) * 512],
                                           start=(m == 0 and k == 0), stop=(m == 2 and k == KD - 1))
                    if n % (3 * KD) == 3 * KD - 1:
                        ins.then_inc(s_yp, 1)

            def window(t, s, q):
                w = pe.snap(t * WPT + q)
                par = (s * WPT + q) % 2
                first = pe.value_load(table[0:1, bass.ds(w * 4, 1)], min_val=0, max_val=NP - 1)
                end = pe.value_load(table[0:1, bass.ds(w * 4 + 1, 1)], min_val=1, max_val=NP)
                shift = pe.value_load(table[0:1, bass.ds(w * 4 + 2, 1)], min_val=1, max_val=NWT * NP)
                pe.wait_ge(s_we, w + 1)
                for b in range(2):
                    nc.tensor.matmul(ps_a[par][b][:, 511:512], zero[:, :], zero[:, 0:1], start=True, stop=False,
                                     skip_group_check=True)
                with pe.Fori(first, end) as pair:
                    visit = pe.snap((shift + pair) * 2)
                    for h in range(2):
                        pe.wait_ge(s_ohr, visit + h + 1)
                        for j in range(NT):
                            ins = nc.tensor.matmul(
                                ps_a[par][j // 5][:, (j % 5) * PARTS * WIN:(j % 5 + 1) * PARTS * WIN],
                                oh_s[:, h, j * TR:j * TR + P], oh_d[:, h, :],
                                start=False, stop=False, skip_group_check=True)
                        ins.then_inc(s_ohu, 1)
                for b in range(2):
                    ins = nc.tensor.matmul(ps_a[par][b][:, 511:512], zero[:, :], zero[:, 0:1], start=False,
                                           stop=True, skip_group_check=True)
                ins.then_inc(s_wr, 1)

            with pe.Fori(0, NT // 2) as i:
                for s in range(2):
                    t = i * 2 + s
                    pe.wait_ge(s_xn, t + 1)
                    for b in range(2):
                        pe.wait_ge(s_lo, t * 2 + b + 1)
                        for k in range(4):
                            ins = nc.tensor.transpose(ps_t[b][:, k * TR:(k + 1) * TR],
                                                      xn[s][:, (4 * b + k) * P:(4 * b + k + 1) * P],
                                                      ident[0:TR, 0:TR])
                        ins.then_inc(s_tp, 1)
                    window(t, s, 0)
                    pe.wait_ge(s_lo, t * 2 + 4)
                    for q in range(WPT):
                        product(s, t, q * PIECES // WPT, (q + 1) * PIECES // WPT)
                        if q < WPT - 1:
                            window(t, s, q + 1)


NH = 16
DH = D // NH
M = 256
JP = D // P
NF = 2 * M // P
DV = DH + 1
CH = [(0, 4), (4, 4), (8, 2)]
TWO_PI = 6.28318501
ROUND = 1.5 * 2.0 ** 23
Z_MIN = 1e-6


def attention_stage(nc, xt_scr, wq, wk, wv, rf, o_scr):
    with ExitStack() as ctx:
        def sb(name, shape, dt):
            return ctx.enter_context(nc.sbuf_tensor(name, shape, dt))

        def sem(name):
            return ctx.enter_context(nc.semaphore(name))

        xa = sb("a_x", [P, 2, KD, N], F32R)
        w_raw = sb("a_wraw", [P, 3, D], F32)
        wt = sb("a_wt", [P, 3, 2, KD, P], F32R)
        qt = sb("a_qt", [P, 2, N], F32R)
        kt = sb("a_kt", [P, 2, N], F32R)
        vt = sb("a_vt", [P, N], F32)
        sq = [sb(f"a_sq{m}", [P, N], F32) for m in range(2)]
        rf_in = sb("a_rfin", [P, 2, 2, DH], F32)
        bd32 = sb("a_bd32", [P, 2 * M], F32)
        bd = sb("a_bd", [P, 2, 2 * M], F32R)
        ub = [sb(f"a_u{s}", [P, 512], F32) for s in range(2)]
        rb = [sb(f"a_r{s}", [P, 512], F32) for s in range(2)]
        kf = [sb(f"a_kf{s}", [TR, 2, 2 * M], F32) for s in range(2)]
        qf = sb("a_qf", [P, 2, NF, 500], F32)
        vs = sb("a_vs", [TR, NT, 2, DV], F32)
        kv = sb("a_kv", [P, 2, NF, DV], F32)
        ob = sb("a_o", [TR, 4, P], F32)
        ot = sb("a_ot", [P, N], F32)
        es = sb("a_exp", [TR, 2, NT, 2], F32)
        zt = sb("a_z", [TR, 4, 4], F32)
        ident = sb("a_ident", [P, P], F32)
        hsel = sb("a_hsel", [P, 2], F32)
        c_round = sb("a_cround", [P, 1], F32)
        c_quarter = sb("a_cquarter", [P, 1], F32)
        c_ln = sb("a_cln", [P, 1], F32)

        gen = [ctx.enter_context(nc.psum_tensor(f"a_psg{s}", [P, 512], F32)) for s in range(3)]
        fea = [ctx.enter_context(nc.psum_tensor(f"a_psf{s}", [P, 512], F32)) for s in range(3)]
        acc = [ctx.enter_context(nc.psum_tensor(f"a_psa{s}", [P, 512], F32)) for s in range(2)]

        s_x = sem("a_x_loaded")
        s_rf = sem("a_rf_loaded")
        s_raw = sem("a_weights_loaded")
        s_cst = sem("a_const")
        s_bd = sem("a_bd")
        s_gen = sem("a_gen")
        s_fea = sem("a_fea")
        s_whi = sem("a_w_high")
        s_wlo = sem("a_w_low")
        s_hi = sem("a_qk_high")
        s_lo = sem("a_qk_low")
        s_vt = sem("a_v_copied")
        s_exp = sem("a_exps")
        s_vs = sem("a_v_scaled")
        s_v1 = sem("a_v_ones")
        s_u = sem("a_rounded")
        s_r = sem("a_remainder")
        s_abs = sem("a_abs")
        s_sc = sem("a_sincos")
        s_kv = sem("a_kv_tile")
        s_kve = sem("a_kv_evacuated")
        s_out = sem("a_out_product")
        s_z = sem("a_z_step")
        s_norm = sem("a_out_scaled")
        s_ot = sem("a_out_transposed")
        s_st = sem("a_stored")

        READ = ([(s_lo, 6, n) for n in range(6)] + [(s_vt, 3, n) for n in range(3)] +
                [(s_vs, 3, n) for n in range(3)])
        for c in range(3):
            READ += [(s_wlo, 6, 2 * c), (s_wlo, 6, 2 * c + 1), (s_ot, 3, c)]
        NG = len(READ)
        NU = NT + 12
        FREAD = [(s_exp, 2, n) for n in range(2)] + [(s_r, NU, n) for n in range(NU)]
        NE = len(FREAD)
        assert NG % 3 == 0 and NE % 3 == 0 and NU % 2 == 0

        def chunk(c):
            first, number = CH[c]
            return first * TR, number * TR

        block = ctx.enter_context(nc.Block())

        def units():
            return [(c, h, m) for c in range(3) for h in range(2) for m in range(2)]

        @block.sync
        def _(sp):
            sp.dma_start(rf_in[:, :, 0, :], rf.rearrange("(m p) d -> p m d", p=P)).then_inc(s_rf, 16)
            sp.dma_start(rf_in[:, :, 1, :], rf.rearrange("(m p) d -> p m d", p=P)).then_inc(s_rf, 16)
            for m, w in enumerate((wq, wk, wv)):
                sp.dma_start(w_raw[:, m, :], w[0:P, :]).then_inc(s_raw, 16)
            for t in range(NT):
                sp.dma_start(xa[:, :, :, t * TR:(t + 1) * TR].bitcast(F32),
                             xt_scr[t, :, :].rearrange("p (h k n) -> p h k n", h=2, k=KD)).then_inc(s_x, 16)
            sp.wait_ge(s_gen, 6)
            with sp.Fori(0, JP) as j:
                nxt = sp.snap((j + 1) % JP)
                for m, w in enumerate((wq, wk, wv)):
                    sp.dma_start(w_raw[:, m, :], w[bass.ds(nxt * P, P), :]).then_inc(s_raw, 16)
                sp.wait_ge(s_gen, j * NG + 6 + NG)
                sp.wait_ge(s_ot, j * 3 + 6)
                sp.dma_start(o_scr[bass.ds(j, 1), :, :].rearrange("a p n -> p (a n)"), ot[:, :]).then_inc(s_st, 16)
            sp.wait_ge(s_raw, 3 * 16 * (JP + 1))
            sp.wait_ge(s_st, 16 * (JP + 1))

        @block.gpsimd
        def _(pool):
            nc.gpsimd.memset(ident[:, :], 0.0).then_inc(s_cst, 1)
            nc.gpsimd.memset(hsel[:, :], 0.0).then_inc(s_cst, 1)
            nc.gpsimd.memset(bd32[:, :], 0.0).then_inc(s_cst, 1)
            nc.gpsimd.memset(c_round[:, :], ROUND).then_inc(s_cst, 1)
            nc.gpsimd.memset(c_quarter[:, :], float(np.float32(np.pi / 2))).then_inc(s_cst, 1)
            nc.gpsimd.memset(c_ln[:, :], -float(np.log(np.sqrt(M)))).then_inc(s_cst, 1)
            pool.wait_ge(s_cst, 6)
            nc.gpsimd.affine_select(out=ident[:, :], in_=ident[:, :], compare_op=ALU.not_equal, fill=1.0,
                                    base=0, pattern=[[-1, P]], channel_multiplier=1).then_inc(s_cst, 1)
            pool.wait_ge(s_cst, 7)
            nc.gpsimd.memset(hsel[0:DH, 0:1], 1.0).then_inc(s_cst, 1)
            pool.wait_ge(s_cst, 8)
            nc.gpsimd.memset(hsel[DH:P, 1:2], 1.0).then_inc(s_cst, 1)
            pool.sem_inc(s_lo, 6)
            pool.sem_inc(s_vt, 3)
            pool.sem_inc(s_vs, 3)
            pool.sem_inc(s_ot, 3)
            pool.sem_inc(s_exp, 2)
            pool.sem_inc(s_r, NU)
            pool.sem_inc(s_norm, 6)
            pool.sem_inc(s_sc, 2)
            pool.sem_inc(s_st, 16)

        @block.scalar
        def _(act):
            act.wait_ge(s_cst, 9)

            def weights(j, n):
                m, b = n // 2, n % 2
                g = (n % 3) if j is None else (NG - 9 + n // 2 * 3 + n % 2) % 3
                act.wait_ge(s_gen, n + 1 if j is None else j * NG + 6 + NG - 9 + n // 2 * 3 + n % 2 + 1)
                nc.scalar.activation(wt[:, m, 0, 4 * b:4 * b + 4, :],
                                     gen[g][:, :].rearrange("p (k n) -> p k n", k=4), ACT.Copy).then_inc(s_whi, 1)

            def transposed(j, c):
                o, size = chunk(c)
                if c == 0:
                    act.wait_ge(s_st, (j + 1) * 16)
                act.wait_ge(s_gen, j * NG + 6 + NG - 9 + 3 * c + 3)
                nc.scalar.activation(ot[:, o:o + size], gen[2][:, 0:size], ACT.Copy).then_inc(s_ot, 1)

            for n in range(6):
                weights(None, n)
            act.wait_ge(s_bd, 1)
            nc.scalar.activation(bd[:, 0, :], bd32[:, :], ACT.Copy).then_inc(s_bd, 1)
            with act.Fori(0, JP) as j:
                for n in range(9):
                    m, c = n // 3, n % 3
                    o, size = chunk(c)
                    act.wait_ge(s_gen, j * NG + 6 + n + 1)
                    if m < 2:
                        nc.scalar.activation(sq[m][:, o:o + size], gen[n % 3][:, 0:size], ACT.Square)
                        nc.scalar.activation((qt, kt)[m][:, 0, o:o + size], gen[n % 3][:, 0:size],
                                             ACT.Copy).then_inc(s_hi, 1)
                    else:
                        nc.scalar.activation(vt[:, o:o + size], gen[n % 3][:, 0:size], ACT.Copy).then_inc(s_vt, 1)
                for m in range(2):
                    act.wait_ge(s_fea, j * NE + 1 + m + 1)
                    nc.scalar.activation(es[:, 1 - m, :, :], fea[m][0:TR, 0:2 * NT].rearrange(
                        "p (t h) -> p t h", h=2), ACT.Exp, bias=c_ln[0:TR, 0:1], scale=-0.5).then_inc(s_exp, 1)

                def rounded(n, rows, size):
                    act.wait_ge(s_sc, j * NU + n + 1)
                    act.wait_ge(s_fea, j * NE + 1 + 2 + n + 1)
                    nc.scalar.activation(ub[n % 2][0:rows, 0:size], fea[(2 + n) % 3][0:rows, 0:size],
                                         ACT.Identity, bias=c_round[0:rows, 0:1]).then_inc(s_u, 1)

                def sincos(n, rows, size, sin_out, cos_out):
                    act.wait_ge(s_abs, j * NU + n + 1)
                    nc.scalar.activation(sin_out, rb[n % 2][0:rows, 0:size], ACT.Sin, scale=-TWO_PI)
                    nc.scalar.activation(cos_out, ub[n % 2][0:rows, 0:size], ACT.Sin,
                                         bias=c_quarter[0:rows, 0:1], scale=-TWO_PI).then_inc(s_sc, 1)

                for t in range(NT + 1):
                    if t < NT:
                        rounded(t, TR, 512)
                    if t > 0:
                        if t - 1 >= 2:
                            act.wait_ge(s_kv, j * NT + t - 2)
                        sincos(t - 1, TR, 512, kf[(t - 1) % 2][:, 1, :], kf[(t - 1) % 2][:, 0, :])
                us = units()
                for n in range(len(us) + 1):
                    if n < len(us):
                        rounded(NT + n, P, chunk(us[n][0])[1])
                    if n > 0:
                        c, h, m = us[n - 1]
                        size = chunk(c)[1]
                        if c > 0:
                            act.wait_ge(s_out, j * 6 + 2 * (c - 1) + h + 1)
                        sincos(NT + n - 1, P, size, qf[:, h, 2 + m, 0:size], qf[:, h, m, 0:size])
                    if n % 4 == 3:
                        if n > 3:
                            transposed(j, n // 4 - 1)
                        weights(j, n // 4 * 2)
                        weights(j, n // 4 * 2 + 1)
                transposed(j, 2)

        @block.vector
        def _(dve):
            def weights(j, n):
                m, b = n // 2, n % 2
                g = (n % 3) if j is None else (NG - 9 + n // 2 * 3 + n % 2) % 3
                dve.wait_ge(s_whi, n + 1 if j is None else j * 6 + 6 + n + 1)
                nc.vector.tensor_tensor(wt[:, m, 1, 4 * b:4 * b + 4, :],
                                        gen[g][:, :].rearrange("p (k n) -> p k n", k=4),
                                        wt[:, m, 0, 4 * b:4 * b + 4, :].bitcast(F32), ALU.subtract
                                        ).then_inc(s_wlo, 1)

            for n in range(6):
                weights(None, n)
            dve.wait_ge(s_cst, 9)
            dve.wait_ge(s_fea, 1)
            for h in range(2):
                for m in range(2):
                    ins = nc.vector.tensor_scalar(
                        bd32[DH * h:DH * h + DH, M * h + P * m:M * h + P * m + P],
                        fea[0][DH * h:DH * h + DH, P * m:P * m + P], float(1 / (2 * np.pi)), None, ALU.mult)
            ins.then_inc(s_bd, 1)
            dve.wait_ge(s_bd, 2)
            nc.vector.tensor_tensor(bd[:, 1, :], bd32[:, :], bd[:, 0, :].bitcast(F32), ALU.subtract).then_inc(s_bd, 1)
            with dve.Fori(0, JP) as j:
                for n in range(6):
                    m, c = n // 3, n % 3
                    o, size = chunk(c)
                    x = (qt, kt)[m]
                    dve.wait_ge(s_hi, j * 6 + n + 1)
                    nc.vector.tensor_tensor(x[:, 1, o:o + size], gen[n % 3][:, 0:size],
                                            x[:, 0, o:o + size].bitcast(F32), ALU.subtract).then_inc(s_lo, 1)
                dve.wait_ge(s_exp, j * 2 + 3)
                nc.vector.tensor_copy(vs[:, :, :, DH], es[:, 1, :, :]).then_inc(s_v1, 1)
                for c, (t0, nt) in enumerate(CH):
                    dve.wait_ge(s_gen, j * NG + 6 + 9 + c + 1)
                    nc.vector.tensor_tensor(
                        vs[:, t0:t0 + nt, :, 0:DH],
                        gen[c][0:TR, 0:nt * P].rearrange("p (t h d) -> p t h d", t=nt, h=2),
                        es[:, 1, t0:t0 + nt, :].unsqueeze(3).broadcast_to([TR, nt, 2, DH]),
                        ALU.mult).then_inc(s_vs, 1)

                def remainder(n, rows, size):
                    u, r = ub[n % 2][0:rows, 0:size], rb[n % 2][0:rows, 0:size]
                    dve.wait_ge(s_u, j * NU + n + 1)
                    nc.vector.scalar_tensor_tensor(out=r, in0=u, scalar=ROUND, in1=fea[(2 + n) % 3][0:rows, 0:size],
                                                   op0=ALU.subtract, op1=ALU.subtract).then_inc(s_r, 1)
                    dve.wait_ge(s_r, j * NU + NU + n + 1)
                    nc.vector.tensor_scalar(u.bitcast(I32), r.bitcast(I32), 0x7fffffff, None,
                                            ALU.bitwise_and).then_inc(s_abs, 1)

                def scaled(c, h):
                    t0, nt = CH[c]
                    prod = acc[h][0:TR, 0:nt * DV].rearrange("p (t v) -> p t v", v=DV)
                    scale = es[:, 0, t0:t0 + nt, h]
                    first = (2 * c + h) * 4
                    dve.wait_ge(s_out, j * 6 + 2 * c + h + 1)
                    nc.vector.tensor_tensor(zt[:, 0, 0:nt], prod[:, :, DH], scale, ALU.mult).then_inc(s_z, 1)
                    dve.wait_ge(s_z, j * 24 + first + 1)
                    nc.vector.tensor_scalar(zt[:, 1, 0:nt], zt[:, 0, 0:nt], Z_MIN, None, ALU.max).then_inc(s_z, 1)
                    dve.wait_ge(s_z, j * 24 + first + 2)
                    nc.vector.reciprocal(zt[:, 2, 0:nt], zt[:, 1, 0:nt]).then_inc(s_z, 1)
                    dve.wait_ge(s_z, j * 24 + first + 3)
                    nc.vector.tensor_tensor(zt[:, 3, 0:nt], zt[:, 2, 0:nt], scale, ALU.mult).then_inc(s_z, 1)
                    dve.wait_ge(s_z, j * 24 + first + 4)
                    nc.vector.tensor_tensor(ob[:, 0:nt, DH * h:DH * h + DH], prod[:, :, 0:DH],
                                            zt[:, 3, 0:nt].unsqueeze(2).broadcast_to([TR, nt, DH]),
                                            ALU.mult).then_inc(s_norm, 1)

                for t in range(NT):
                    dve.wait_ge(s_sc, j * NU + t + 1)
                    remainder(t, TR, 512)
                dve.wait_ge(s_kv, j * NT + NT)
                for h in range(2):
                    ins = nc.vector.tensor_copy(kv[:, h, :, :].rearrange("p f v -> p (f v)"), acc[h][:, 0:NF * DV])
                ins.then_inc(s_kve, 1)
                for n, (c, h, m) in enumerate(units()):
                    dve.wait_ge(s_sc, j * NU + NT + n + 1)
                    remainder(NT + n, P, chunk(c)[1])
                    if c > 0 and m == 1:
                        scaled(c - 1, h)
                    if n % 4 == 3:
                        weights(j, n // 4 * 2)
                        weights(j, n // 4 * 2 + 1)
                scaled(2, 0)
                scaled(2, 1)

        @block.tensor
        def _(pe):
            def weights(j, n):
                m, b = n // 2, n % 2
                if j is None:
                    if n >= 3:
                        pe.wait_ge(s_wlo, n - 2)
                    g = n % 3
                else:
                    g = NG - 9 + n // 2 * 3 + n % 2
                    free(j, g)
                    pe.wait_ge(s_raw, j * 48 + 96)
                    g %= 3
                for k in range(4):
                    ins = nc.tensor.transpose(gen[g][:, k * P:(k + 1) * P],
                                              w_raw[:, m, (4 * b + k) * P:(4 * b + k + 1) * P], ident[:, :])
                ins.then_inc(s_gen, 1)

            def free(j, g):
                sem_, per, n = READ[(g - 3) % NG]
                pe.wait_ge(sem_, j * per + n + 1 + (per if g >= 3 else 0))

            def free_fea(j, f):
                sem_, per, n = FREAD[(f - 3) % NE]
                pe.wait_ge(sem_, j * per + n + 1 + (per if f >= 3 else 0))

            PASSES = ((0, 0), (0, 1), (1, 0))

            pe.wait_ge(s_cst, 9)
            pe.wait_ge(s_raw, 48)
            for n in range(6):
                weights(None, n)
            pe.wait_ge(s_rf, 32)
            for m in range(2):
                ins = nc.tensor.transpose(fea[0][:, m * P:(m + 1) * P], rf_in[:, m, :, :].rearrange("p a d -> p (a d)"),
                                          ident[:, :])
            ins.then_inc(s_fea, 1)
            pe.wait_ge(s_bd, 3)
            pe.wait_ge(s_x, 16 * NT)
            with pe.Fori(0, JP) as j:
                pe.wait_ge(s_wlo, j * 6 + 6)
                for n in range(9):
                    m, c = n // 3, n % 3
                    o, size = chunk(c)
                    free(j, n)
                    for a, (pw, px) in enumerate(PASSES):
                        for k in range(KD):
                            ins = nc.tensor.matmul(gen[n % 3][:, 0:size], wt[:, m, pw, k, :], xa[:, px, k, o:o + size],
                                                   start=(a == 0 and k == 0), stop=(a == 2 and k == KD - 1))
                    ins.then_inc(s_gen, 1)
                for c, (t0, nt) in enumerate(CH):
                    free(j, 9 + c)
                    for i in range(nt):
                        ins = nc.tensor.transpose(gen[c][0:TR, i * P:(i + 1) * P],
                                                  vt[:, (t0 + i) * TR:(t0 + i + 1) * TR], ident[:, :])
                    ins.then_inc(s_gen, 1)
                pe.wait_ge(s_hi, j * 6 + 6)
                for f, m in enumerate((1, 0)):
                    free_fea(j, f)
                    for t in range(NT):
                        ins = nc.tensor.matmul(fea[f][0:TR, 2 * t:2 * t + 2], sq[m][:, t * TR:(t + 1) * TR], hsel[:, :],
                                               start=True, stop=True)
                    ins.then_inc(s_fea, 1)
                for t in range(NT + 2):
                    if t < NT:
                        free_fea(j, 2 + t)
                        if t == 0:
                            pe.wait_ge(s_lo, j * 6 + 12)
                        for a, (pk, pr) in enumerate(PASSES):
                            ins = nc.tensor.matmul(fea[(2 + t) % 3][0:TR, :], kt[:, pk, t * TR:(t + 1) * TR],
                                                   bd[:, pr, :], start=(a == 0), stop=(a == 2))
                        ins.then_inc(s_fea, 1)
                    if t >= 2:
                        s = t - 2
                        if s == 0:
                            pe.wait_ge(s_v1, j + 1)
                            pe.wait_ge(s_vs, j * 3 + 6)
                            pe.wait_ge(s_norm, j * 6 + 6)
                        pe.wait_ge(s_sc, j * NU + s + 3)
                        for h in range(2):
                            for f in range(NF):
                                ins = nc.tensor.matmul(
                                    acc[h][:, f * DV:(f + 1) * DV],
                                    kf[s % 2][:, f // 2, h * M + f % 2 * P:h * M + f % 2 * P + P], vs[:, s, h, :],
                                    start=(s == 0 and f == 0), stop=(s == NT - 1 and f == NF - 1),
                                    skip_group_check=True)
                        ins.then_inc(s_kv, 1)

                def angles(c, h):
                    o, size = chunk(c)
                    for m in range(2):
                        n = 4 * c + 2 * h + m
                        free_fea(j, 2 + NT + n)
                        for a, (pr, pq) in enumerate(PASSES):
                            ins = nc.tensor.matmul(fea[(2 + NT + n) % 3][:, 0:size],
                                                   bd[:, pr, h * M + m * P:h * M + m * P + P], qt[:, pq, o:o + size],
                                                   start=(a == 0), stop=(a == 2))
                        ins.then_inc(s_fea, 1)

                def output(c, h):
                    nt = CH[c][1]
                    if c == 0:
                        pe.wait_ge(s_kve, j + 1)
                    else:
                        pe.wait_ge(s_norm, j * 6 + 6 + 2 * (c - 1) + h + 1)
                    pe.wait_ge(s_sc, j * NU + NT + 4 * c + 2 * h + 4)
                    for i in range(nt):
                        for f in range(NF):
                            ins = nc.tensor.matmul(acc[h][0:TR, i * DV:(i + 1) * DV], qf[:, h, f, i * TR:(i + 1) * TR],
                                                   kv[:, h, f, :], start=(f == 0), stop=(f == NF - 1))
                    ins.then_inc(s_out, 1)

                def transpose_output(c):
                    free(j, NG - 9 + 3 * c + 2)
                    pe.wait_ge(s_norm, j * 6 + 6 + 2 * c + 2)
                    for i in range(CH[c][1]):
                        ins = nc.tensor.transpose(gen[2][:, i * TR:(i + 1) * TR], ob[:, i, :], ident[0:TR, 0:TR])
                    ins.then_inc(s_gen, 1)

                for c in range(3):
                    for h in range(2):
                        if c > 0:
                            output(c - 1, h)
                        angles(c, h)
                    if c > 0:
                        transpose_output(c - 1)
                    weights(j, 2 * c)
                    weights(j, 2 * c + 1)
                output(2, 0)
                output(2, 1)
                transpose_output(2)


FI = 512
KI = FI // P


def output_stage(nc, o_scr, wo, x, edge_scr, x1_scr, norm_scr):
    with ExitStack() as ctx:
        def sb(name, shape, dt):
            return ctx.enter_context(nc.sbuf_tensor(name, shape, dt))

        def sem(name):
            return ctx.enter_context(nc.semaphore(name))

        ident = sb("o_ident", [P, P], F32)
        w_raw = [sb(f"o_wraw{s}", [P, D], F32) for s in range(2)]
        wt = sb("o_wt", [P, 2, KD, D], F32R)
        of = [sb(f"o_of{s}", [P, KD, TR], F32) for s in range(2)]
        oh = [sb(f"o_oh{s}", [P, 2, KD, TR], F32R) for s in range(2)]
        xin = [sb(f"o_x{s}", [TR, D], F32) for s in range(2)]
        xout = [sb(f"o_xo{s}", [TR, D], F32) for s in range(2)]
        edge_t = sb("o_edge", [TR, 3, NC], F32)
        tile_f = sb("o_tile", [TR, 2, NC], F32)
        row_f = sb("o_row", [TR, 2, NC], F32)
        wrest = sb("o_wrest", [TR, 2, NC], F32)
        wpart = sb("o_wpart", [TR, NC, 4], BF16)
        iota_t = sb("o_iotat", [TR, NC, NT], I16)
        iota_p = sb("o_iotap", [TR, TR + 1], I16)
        oh_t = sb("o_oht", [TR, NC, NT], BF16)
        rhs = sb("o_rhs", [TR, 2, NC, 4, NT], BF16)
        oh_p = sb("o_ohp", [TR, 2, 2, P], BF16)
        sums = sb("o_sums", [TR, 2, 4 * NT], F32)
        nrm = sb("o_nrm", [TR, 2, 6, NT], F32)
        nout = sb("o_nout", [TR, NT, 2], F32)

        ps_t = [ctx.enter_context(nc.psum_tensor(f"o_pst{s}", [P, 512], F32)) for s in range(2)]
        ps_o = [ctx.enter_context(nc.psum_tensor(f"o_pso{s}", [TR, 512], F32)) for s in range(4)]
        ps_h = [ctx.enter_context(nc.psum_tensor(f"o_psh{s}", [TR, 512], F32)) for s in range(2)]

        s_w = [sem(f"o_w_loaded{s}") for s in range(2)]
        s_o = [sem(f"o_o_loaded{s}") for s in range(2)]
        s_x = [sem(f"o_x_loaded{s}") for s in range(2)]
        s_e = sem("o_edge_loaded")
        s_cst = sem("o_const")
        s_tp = sem("o_transposed")
        s_whi = sem("o_w_high")
        s_wlo = sem("o_w_low")
        s_ohi = sem("o_o_high")
        s_olo = sem("o_o_low")
        s_pr = sem("o_product")
        s_add = sem("o_added")
        s_st = [sem(f"o_stored{s}") for s in range(2)]
        s_hp = sem("o_hist_step")
        s_hr = sem("o_hist_onehot")
        s_hu = sem("o_hist_used")
        s_sq = sem("o_hist_sqrt")
        s_ns = sem("o_norm_stored")
        CPT = NC // NT
        block = ctx.enter_context(nc.Block())

        @block.sync
        def _(sp):
            for k in range(KD):
                if k >= 2:
                    sp.wait_ge(s_tp, 2 * (k - 1))
                sp.dma_start(w_raw[k % 2][:, :], wo[k * P:(k + 1) * P, :]).then_inc(s_w[k % 2], 16)
                if k == 1:
                    sp.dma_start(edge_t[:, :, :], edge_scr).then_inc(s_e, 16)
                    for s in range(2):
                        sp.dma_start(of[s][:, :, :], o_scr[:, :, s * TR:(s + 1) * TR].rearrange("j p n -> p j n")
                                     ).then_inc(s_o[s], 16)
                        sp.dma_start(xin[s][:, :], x[s * TR:(s + 1) * TR, :]).then_inc(s_x[s], 16)
            for s in range(2):
                sp.sem_inc(s_st[s], 16)
            with sp.Fori(0, NT // 2) as i:
                for s in range(2):
                    nxt = sp.snap((i * 2 + s + 2) % NT)
                    sp.wait_ge(s_olo, i * 2 + s + 1)
                    sp.dma_start(of[s][:, :, :], o_scr[:, :, bass.ds(nxt * TR, TR)].rearrange("j p n -> p j n")
                                 ).then_inc(s_o[s], 16)
                    sp.wait_ge(s_add, (i * 2 + s) * 2 + 6)
                    sp.dma_start(xin[s][:, :], x[bass.ds(nxt * TR, TR), :]).then_inc(s_x[s], 16)
                    sp.dma_start(x1_scr[bass.ds(i * 2 + s, 1), :, :].rearrange("a p n -> p (a n)"),
                                 xout[s][:, :]).then_inc(s_st[s], 16)
            sp.wait_ge(s_hp, HIST_STEPS)
            sp.dma_start(norm_scr, nout[:, :, :]).then_inc(s_ns, 16)
            sp.wait_ge(s_ns, 16)
            for s in range(2):
                sp.wait_ge(s_st[s], 16 * (NT // 2 + 1))
                sp.wait_ge(s_o[s], 16 * (NT // 2 + 1))
                sp.wait_ge(s_x[s], 16 * (NT // 2 + 1))

        @block.gpsimd
        def _(pool):
            nc.gpsimd.memset(ident[:, :], 0.0).then_inc(s_cst, 1)
            nc.gpsimd.iota(iota_t[:, :, :], pattern=[[0, NC], [1, NT]], base=0, channel_multiplier=0).then_inc(s_cst, 1)
            nc.gpsimd.iota(iota_p[:, :], pattern=[[1, TR + 1]], base=0, channel_multiplier=0).then_inc(s_cst, 1)
            nc.gpsimd.memset(wpart[:, :, 0], 1.0).then_inc(s_cst, 1)
            pool.wait_ge(s_cst, 4)
            nc.gpsimd.affine_select(out=ident[:, :], in_=ident[:, :], compare_op=ALU.not_equal, fill=1.0,
                                    base=0, pattern=[[-1, P]], channel_multiplier=1).then_inc(s_cst, 1)

        @block.scalar
        def _(act):
            for n in range(2 * KD):
                m, b = n // 2, n % 2
                act.wait_ge(s_tp, n + 1)
                nc.scalar.activation(wt[:, 0, 4 * b:4 * b + 4, m * P:(m + 1) * P],
                                     ps_t[b][:, :].rearrange("p (k n) -> p k n", k=4), ACT.Copy).then_inc(s_whi, 1)
            with act.Fori(0, NT // 2) as i:
                for s in range(2):
                    t = i * 2 + s
                    act.wait_ge(s_o[s], i * 16 + 16)
                    act.wait_ge(s_pr, t * 2 + 2)
                    nc.scalar.activation(oh[s][:, 0, :, :], of[s][:, :, :], ACT.Copy).then_inc(s_ohi, 1)
            act.wait_ge(s_hp, HIST_SQRT)
            nc.scalar.activation(nrm[:, :, 4, :], nrm[:, :, 3, :], ACT.Sqrt).then_inc(s_sq, 1)

        @block.vector
        def _(dve):
            steps = [0]

            def step(ins):
                steps[0] += 1
                ins.then_inc(s_hp, 1)
                dve.wait_ge(s_hp, steps[0])

            for n in range(2 * KD):
                m, b = n // 2, n % 2
                dve.wait_ge(s_whi, n + 1)
                nc.vector.tensor_tensor(wt[:, 1, 4 * b:4 * b + 4, m * P:(m + 1) * P],
                                        ps_t[b][:, :].rearrange("p (k n) -> p k n", k=4),
                                        wt[:, 0, 4 * b:4 * b + 4, m * P:(m + 1) * P].bitcast(F32),
                                        ALU.subtract).then_inc(s_wlo, 1)
            dve.wait_ge(s_e, 16)
            dve.wait_ge(s_cst, 5)
            step(nc.vector.tensor_scalar(tile_f[:, :, :], edge_t[:, 0:2, :], 1.0 / TR, -0.5 + 0.5 / TR, ALU.mult, ALU.add))
            step(nc.vector.tensor_scalar(tile_f[:, :, :], tile_f[:, :, :], ROUND, ROUND, ALU.add, ALU.subtract))
            step(nc.vector.scalar_tensor_tensor(out=row_f[:, :, :], in0=tile_f[:, :, :], scalar=-float(TR),
                                                in1=edge_t[:, 0:2, :], op0=ALU.mult, op1=ALU.add))
            step(nc.vector.tensor_copy(wpart[:, :, 1], edge_t[:, 2, :]))
            step(nc.vector.tensor_tensor(wrest[:, 0, :], edge_t[:, 2, :], wpart[:, :, 1], ALU.subtract))
            step(nc.vector.tensor_copy(wpart[:, :, 2], wrest[:, 0, :]))
            step(nc.vector.tensor_tensor(wrest[:, 1, :], wrest[:, 0, :], wpart[:, :, 2], ALU.subtract))
            step(nc.vector.tensor_copy(wpart[:, :, 3], wrest[:, 1, :]))
            for e in range(2):
                step(nc.vector.tensor_tensor(oh_t[:, :, :], iota_t[:, :, :],
                                             tile_f[:, e, :].unsqueeze(2).broadcast_to([TR, NC, NT]), ALU.is_equal))
                for m in range(4):
                    step(nc.vector.tensor_tensor(rhs[:, e, :, m, :], oh_t[:, :, :],
                                                 wpart[:, :, m].unsqueeze(2).broadcast_to([TR, NC, NT]), ALU.mult))
            with dve.Fori(0, NT // 2) as i:
                for s in range(2):
                    t = i * 2 + s
                    dve.wait_ge(s_ohi, t + 1)
                    nc.vector.tensor_tensor(oh[s][:, 1, :, :], of[s][:, :, :], oh[s][:, 0, :, :].bitcast(F32),
                                            ALU.subtract).then_inc(s_olo, 1)
                    with dve.Fori(0, CPT // 2) as g:
                        for h in range(2):
                            n = dve.snap(t * CPT + g * 2 + h)
                            dve.wait_ge(s_hu, n + 1)
                            for e in range(2):
                                ins = nc.vector.tensor_scalar(oh_p[:, h, e, 0:TR + 1], iota_p[:, :],
                                                              row_f[:, e, bass.ds(n, 1)], None, ALU.is_equal)
                            ins.then_inc(s_hr, 1)
                    dve.wait_ge(s_x[s], i * 16 + 16)
                    dve.wait_ge(s_st[s], i * 16 + 16)
                    for b in range(2):
                        dve.wait_ge(s_pr, t * 2 + b + 5)
                        nc.vector.tensor_tensor(xout[s][:, b * 512:(b + 1) * 512], ps_o[2 * s + b][:, :],
                                                xin[s][:, b * 512:(b + 1) * 512], ALU.add).then_inc(s_add, 1)
            dve.wait_ge(s_hu, NC + 2)
            for e in range(2):
                step(nc.vector.tensor_copy(sums[:, e, :], ps_h[e][:, 0:4 * NT]))
            sv = sums[:, :, :].rearrange("p e (m t) -> p e m t", m=4)
            step(nc.vector.tensor_scalar(nrm[:, :, 0, :], sv[:, :, 0, :], 1.0, None, ALU.max))
            step(nc.vector.tensor_tensor(nrm[:, :, 1, :], sv[:, :, 1, :], sv[:, :, 2, :], ALU.add))
            step(nc.vector.tensor_tensor(nrm[:, :, 1, :], nrm[:, :, 1, :], sv[:, :, 3, :], ALU.add))
            step(nc.vector.scalar_tensor_tensor(out=nrm[:, :, 2, :], in0=sv[:, :, 0, :], scalar=0.0,
                                                in1=nrm[:, :, 1, :], op0=ALU.is_equal, op1=ALU.add))
            step(nc.vector.tensor_tensor(nrm[:, :, 3, :], nrm[:, :, 2, :], nrm[:, :, 0, :], ALU.mult))
            assert steps[0] == HIST_SQRT
            dve.wait_ge(s_sq, 1)
            step(nc.vector.reciprocal(nrm[:, :, 5, :], nrm[:, :, 4, :]))
            step(nc.vector.tensor_tensor(nrm[:, :, 4, :], nrm[:, :, 5, :], nrm[:, :, 5, :], ALU.mult))
            step(nc.vector.tensor_tensor(nrm[:, :, 4, :], nrm[:, :, 4, :], nrm[:, :, 3, :], ALU.mult))
            step(nc.vector.tensor_scalar(nrm[:, :, 4, :], nrm[:, :, 4, :], -0.5, 1.5, ALU.mult, ALU.add))
            step(nc.vector.tensor_tensor(nout[:, :, :], nrm[:, :, 4, :].rearrange("p e t -> p t e"),
                                         nrm[:, :, 5, :].rearrange("p e t -> p t e"), ALU.mult))
            assert steps[0] == HIST_STEPS

        @block.tensor
        def _(pe):
            pe.sem_inc(s_hu, 2)
            pe.sem_inc(s_pr, 4)
            pe.sem_inc(s_add, 4)
            pe.wait_ge(s_cst, 5)
            for n in range(2 * KD):
                m, b = n // 2, n % 2
                if b == 0:
                    pe.wait_ge(s_w[m % 2], (m // 2 + 1) * 16)
                if n >= 2:
                    pe.wait_ge(s_wlo, n - 1)
                for k in range(4):
                    ins = nc.tensor.transpose(ps_t[b][:, k * P:(k + 1) * P],
                                              w_raw[m % 2][:, (4 * b + k) * P:(4 * b + k + 1) * P], ident[:, :])
                ins.then_inc(s_tp, 1)
            pe.wait_ge(s_wlo, 2 * KD)
            pe.wait_ge(s_hr, 1)
            for e in range(2):
                nc.tensor.matmul(ps_h[e][:, 511:512], oh_p[:, 0, 0, 0:TR], oh_p[:, 0, 0, 0:1], start=True, stop=False,
                                 skip_group_check=True)
            with pe.Fori(0, NT // 2) as i:
                for s in range(2):
                    t = i * 2 + s
                    pe.wait_ge(s_olo, t + 1)
                    for b in range(2):
                        pe.wait_ge(s_add, t * 2 + b + 1)
                        for a, (po, pw) in enumerate(((0, 0), (0, 1), (1, 0))):
                            for k in range(KD):
                                ins = nc.tensor.matmul(ps_o[2 * s + b][:, :], oh[s][:, po, k, :],
                                                       wt[:, pw, k, b * 512:(b + 1) * 512],
                                                       start=(a == 0 and k == 0), stop=(a == 2 and k == KD - 1))
                        ins.then_inc(s_pr, 1)
                    with pe.Fori(0, CPT // 2) as g:
                        for h in range(2):
                            n = pe.snap(t * CPT + g * 2 + h)
                            pe.wait_ge(s_hr, n + 1)
                            for e in range(2):
                                ins = nc.tensor.matmul(ps_h[e][:, 0:4 * NT], oh_p[:, h, e, 0:TR],
                                                       rhs[:, e, bass.ds(n, 1), :, :].rearrange("p a m t -> p (a m t)"),
                                                       start=False, stop=False, skip_group_check=True)
                            ins.then_inc(s_hu, 1)


HIST_SQRT = 8 + 10 + 2 + 5
HIST_STEPS = HIST_SQRT + 5


HO = FI // P
LN_STEPS = 17
H_STEPS = 6
Q_MAX = 127.0
Q_MIN = -128.0
Q_EPS = 1e-5


def feed_forward_stage(nc, y_scr, at_scr, norm_scr, x1_scr, gnn_b, w_gate, w_up, w_down, out):
    with ExitStack() as outer:
        wgt = outer.enter_context(nc.sbuf_tensor("f_wgt", [P, KD, FI], BF16))
        wut = outer.enter_context(nc.sbuf_tensor("f_wut", [P, KD, FI], BF16))
        wdt = outer.enter_context(nc.sbuf_tensor("f_wdt", [P, KI, D], BF16))
        ident = outer.enter_context(nc.sbuf_tensor("f_ident", [P, P], BF16))
        wsc = outer.enter_context(nc.sbuf_tensor("f_wsc", [P, 3], F32))
        ternary_weights(nc, w_gate, w_up, w_down, wgt, wut, wdt, ident, wsc)
        feed_forward_tiles(nc, y_scr, at_scr, norm_scr, x1_scr, gnn_b, wgt, wut, wdt, ident, wsc, out)


def ternary_weights(nc, w_gate, w_up, w_down, wgt, wut, wdt, ident, wsc):
    with ExitStack() as ctx:
        def sb(name, shape, dt):
            return ctx.enter_context(nc.sbuf_tensor(name, shape, dt))

        def sem(name):
            return ctx.enter_context(nc.semaphore(name))

        WN = FI * D // P
        raw = [sb(f"t_raw{m}", [P, WN], F32) for m in range(3)]
        tern = [sb(f"t_tern{m}", [P, WN], BF16) for m in range(3)]
        part = sb("t_part", [P, 3], F32)
        scale = sb("t_scale", [P, 3], F32)
        ones = sb("t_ones", [P, P], F32)
        ps_s = [ctx.enter_context(nc.psum_tensor(f"t_pss{m}", [P, 512], F32)) for m in range(3)]
        ps_t = [ctx.enter_context(nc.psum_tensor(f"t_pst{s}", [P, 1024], BF16)) for s in range(2)]
        s_w = [sem(f"t_loaded{m}") for m in range(3)]
        s_c = sem("t_const")
        s_v = sem("t_vector")
        s_sum = sem("t_summed")
        s_tp = sem("t_transposed")
        s_ev = sem("t_evacuated")
        VS = 7
        block = ctx.enter_context(nc.Block())

        @block.sync
        def _(sp):
            for m, w in enumerate((w_gate, w_up, w_down)):
                sp.dma_start(raw[m][:, :], w.rearrange("(a p) n -> p a n", p=P)).then_inc(s_w[m], 16)

        @block.gpsimd
        def _(pool):
            nc.gpsimd.memset(ident[:, :], 0.0).then_inc(s_c, 1)
            nc.gpsimd.memset(ones[:, :], 1.0).then_inc(s_c, 1)
            pool.wait_ge(s_c, 2)
            nc.gpsimd.affine_select(out=ident[:, :], in_=ident[:, :], compare_op=ALU.not_equal, fill=1.0,
                                    base=0, pattern=[[-1, P]], channel_multiplier=1).then_inc(s_c, 1)

        @block.vector
        def _(dve):
            steps = [0]

            def step(ins):
                steps[0] += 1
                ins.then_inc(s_v, 1)
                dve.wait_ge(s_v, steps[0])

            for m in range(3):
                dve.wait_ge(s_w[m], 16)
                step(nc.vector.tensor_reduce(part[:, m:m + 1], raw[m][:, :], axis=AX.X, op=ALU.add,
                                             apply_absolute_value=True))
                dve.wait_ge(s_sum, m + 1)
                step(nc.vector.tensor_scalar(wsc[:, m:m + 1], ps_s[m][:, 0:1], 1.0 / (FI * D), Q_EPS, ALU.mult, ALU.max))
                step(nc.vector.reciprocal(scale[:, m:m + 1], wsc[:, m:m + 1]))
                step(nc.vector.tensor_scalar(raw[m][:, :], raw[m][:, :], scale[:, m:m + 1], 1.0, ALU.mult, ALU.min))
                step(nc.vector.tensor_scalar(raw[m][:, :], raw[m][:, :], -1.0, ROUND, ALU.max, ALU.add))
                h = WN // 2
                step(nc.vector.tensor_scalar(tern[m][:, 0:h], raw[m][:, 0:h], ROUND, None, ALU.subtract))
                step(nc.vector.tensor_scalar(tern[m][:, h:WN], raw[m][:, h:WN], ROUND, None, ALU.subtract))

        @block.tensor
        def _(pe):
            pe.wait_ge(s_c, 3)
            n = 0
            for m in range(3):
                pe.wait_ge(s_v, VS * m + 1)
                nc.tensor.matmul(ps_s[m][:, 0:1], ones[:, :], part[:, m:m + 1], start=True, stop=True).then_inc(s_sum, 1)
                pe.wait_ge(s_v, VS * m + VS)
                rows, cols = (HO, KD) if m < 2 else (KD, KI)
                for c in range(4):
                    if n >= 2:
                        pe.wait_ge(s_ev, n - 1)
                    for b in range(8):
                        blk = 8 * c + b
                        k, a = blk // rows, blk % rows
                        ins = nc.tensor.transpose(ps_t[n % 2][:, b * P:(b + 1) * P],
                                                  tern[m][:, a * cols * P + k * P:a * cols * P + (k + 1) * P], ident[:, :])
                    ins.then_inc(s_tp, 1)
                    n += 1

        @block.scalar
        def _(act):
            for n in range(12):
                m, c = n // 4, n % 4
                wt = (wgt, wut, wdt)[m]
                act.wait_ge(s_tp, n + 1)
                nc.scalar.activation(wt[:, :, :].rearrange("p k n -> p (k n)")[:, c * 1024:(c + 1) * 1024],
                                     ps_t[n % 2][:, :], ACT.Copy).then_inc(s_ev, 1)


def feed_forward_tiles(nc, y_scr, at_scr, norm_scr, x1_scr, gnn_b, wgt, wut, wdt, ident, wsc, out):
    with ExitStack() as ctx:
        def sb(name, shape, dt):
            return ctx.enter_context(nc.sbuf_tensor(name, shape, dt))

        def sem(name):
            return ctx.enter_context(nc.semaphore(name))

        norm = sb("f_norm", [TR, NT, 2], F32)
        bias = sb("f_bias", [TR, D], F32)
        y_raw = [sb(f"f_yraw{s}", [TR, D], F32) for s in range(2)]
        yh = sb("f_yh", [TR, NT, D], F32R)
        yl = sb("f_yl", [TR, NT, D], F32R)
        a_raw = [sb(f"f_araw{s}", [TR, WPT, NT, WIN], F32) for s in range(2)]
        ah = [sb(f"f_ah{s}", [TR, NT, TR], F32R) for s in range(2)]
        al = [sb(f"f_al{s}", [TR, NT, TR], F32R) for s in range(2)]
        xin = [sb(f"f_xin{s}", [TR, D], F32) for s in range(2)]
        x1 = [sb(f"f_x1{s}", [TR, D], F32) for s in range(2)]
        z = sb("f_z", [TR, D], F32)
        xn = sb("f_xn", [TR, D], F32)
        q = sb("f_q", [TR, D], BF16)
        qt = sb("f_qt", [P, KD, P], BF16)
        gate = sb("f_gate", [TR, FI], F32)
        h = sb("f_h", [TR, FI], F32)
        hr = sb("f_hr", [TR, FI], F32)
        hq = sb("f_hq", [TR, FI], BF16)
        hqt = sb("f_hqt", [P, KI, P], BF16)
        o = [sb(f"f_out{s}", [TR, D], F32) for s in range(2)]
        eps = sb("f_eps", [TR, 1], F32)
        rnd = sb("f_round", [TR, 2], F32)
        bn = sb("f_bn", [TR, 2, 6], F32)
        mv = sb("f_mv", [TR, 2], F32)
        std = sb("f_std", [TR, 1], F32)
        lnw = sb("f_lnw", [TR, 4], F32)
        amax = [sb(f"f_amax{s}", [TR, 2], F32) for s in range(2)]
        dq = [sb(f"f_dq{s}", [TR, 2], F32) for s in range(2)]
        hmax = sb("f_hmax", [TR, 2], F32)
        dqh = sb("f_dqh", [TR, 1], F32)

        ps_a = [ctx.enter_context(nc.psum_tensor(f"f_psa{b}", [TR, 512], F32)) for b in range(2)]
        ps_q = ctx.enter_context(nc.psum_tensor("f_psq", [P, 1024], BF16))
        ps_h = ctx.enter_context(nc.psum_tensor("f_psh", [P, 1024], BF16))
        ps_g = ctx.enter_context(nc.psum_tensor("f_psg", [TR, 512], F32))
        ps_u = ctx.enter_context(nc.psum_tensor("f_psu", [TR, 512], F32))
        ps_d = [ctx.enter_context(nc.psum_tensor(f"f_psd{b}", [TR, 512], F32)) for b in range(2)]

        s_nb = sem("f_norm_bias_loaded")
        s_y = [sem(f"f_y_loaded{s}") for s in range(2)]
        s_a = [sem(f"f_a_loaded{s}") for s in range(2)]
        s_x = [sem(f"f_x_loaded{s}") for s in range(2)]
        s_st = [sem(f"f_stored{s}") for s in range(2)]
        s_c = sem("f_const")
        s_yh = sem("f_y_high")
        s_yl = sem("f_y_low")
        s_ah = sem("f_a_high")
        s_al = sem("f_a_low")
        s_agg = sem("f_edges_summed")
        s_ln = sem("f_ln")
        s_lna = sem("f_ln_scalar")
        s_qtp = sem("f_q_transposed")
        s_qt = sem("f_qt_ready")
        s_gu = sem("f_gate_up")
        s_hv = sem("f_h")
        s_ha = sem("f_h_scalar")
        s_htp = sem("f_h_transposed")
        s_ht = sem("f_ht_ready")
        s_dn = sem("f_down")
        s_o = sem("f_out_ready")
        block = ctx.enter_context(nc.Block())

        def tiles(eng, step):
            for n in range(2):
                step(n % 2, True, n > 0, False, n - 2)
            with eng.Fori(0, (NT - 2) // 2) as i:
                for s in range(2):
                    step(s, True, True, True, i * 2 + s)
            for n in range(NT, NT + 2):
                step(n % 2, False, n == NT, True, n - 2)

        @block.sync
        def _(sp):
            sp.dma_start(norm[:, :, :], norm_scr).then_inc(s_nb, 16)
            sp.dma_start(bias[:, :], gnn_b.rearrange("(a n) -> a n", a=1).broadcast_to([TR, D])).then_inc(s_nb, 16)

            def load_a(s, t):
                sp.dma_start(a_raw[s][:, :, :, :].rearrange("p w j d -> p w (j d)"),
                             at_scr[bass.ds(t * WPT, WPT), :, :].rearrange("w p n -> p w n")).then_inc(s_a[s], 16)

            def load_x(s, t):
                sp.dma_start(xin[s][:, :], x1_scr[bass.ds(t, 1), :, :].rearrange("a p n -> p (a n)")).then_inc(s_x[s], 16)

            for j in range(NT):
                if j >= 2:
                    sp.wait_ge(s_yl, j - 1)
                sp.dma_start(y_raw[j % 2][:, :], y_scr[j]).then_inc(s_y[j % 2], 16)
                if j < 2:
                    load_a(j, j)
                    load_x(j, j)
            for s in range(2):
                sp.sem_inc(s_st[s], 16)
            with sp.Fori(0, NT // 2) as i:
                for s in range(2):
                    t = i * 2 + s
                    nxt = sp.snap((t + 2) % NT)
                    sp.wait_ge(s_al, t + 1)
                    load_a(s, nxt)
                    sp.wait_ge(s_ln, t * LN_STEPS + 3)
                    load_x(s, nxt)
                    sp.wait_ge(s_o, t * 2 + 2)
                    sp.dma_start(out[bass.ds(t * TR, TR), :], o[s][:, :]).then_inc(s_st[s], 16)
            for s in range(2):
                sp.wait_ge(s_a[s], 16 * (NT // 2 + 1))
                sp.wait_ge(s_x[s], 16 * (NT // 2 + 1))
                sp.wait_ge(s_st[s], 16 * (NT // 2 + 1))

        @block.gpsimd
        def _(pool):
            nc.gpsimd.memset(eps[:, :], LN_EPS).then_inc(s_c, 1)
            nc.gpsimd.memset(rnd[:, 0:1], ROUND).then_inc(s_c, 1)
            nc.gpsimd.memset(rnd[:, 1:2], -ROUND).then_inc(s_c, 1)

        @block.scalar
        def _(act):
            def a_high(s, b, peeled):
                act.wait_ge(s_a[s], b * 8 + 32 - 8 * s)
                if not peeled:
                    act.wait_ge(s_agg, b * 2 + 2)
                nc.scalar.activation(ah[s][:, :, :].rearrange("p j (w d) -> p w j d", w=WPT),
                                     a_raw[s][:, :, :, :], ACT.Copy).then_inc(s_ah, 1)

            act.wait_ge(s_c, 3)
            act.wait_ge(s_nb, 32)
            a_high(0, -2, True)
            for j in range(NT):
                act.wait_ge(s_y[j % 2], 16 * (j // 2 + 1))
                nc.scalar.activation(yh[:, j, :], y_raw[j % 2][:, :], ACT.Copy, scale=norm[:, j, 0:1]).then_inc(s_yh, 1)

            def step(s, edges, gate_up, down, b):
                if down:
                    act.wait_ge(s_htp, b + 1)
                    nc.scalar.activation(hqt[:, :, 0:TR], ps_h[:, 0:KI * P].rearrange("p (k n) -> p k n", k=KI)[:, :, 0:TR],
                                         ACT.Copy).then_inc(s_ht, 1)
                if edges:
                    a_high(1 - s, b + 1, isinstance(b, int) and b < -1)
                if gate_up:
                    act.wait_ge(s_qtp, b + 2)
                    nc.scalar.activation(qt[:, :, 0:TR], ps_q[:, :].rearrange("p (k n) -> p k n", k=KD)[:, :, 0:TR],
                                         ACT.Copy).then_inc(s_qt, 1)
                if edges:
                    act.wait_ge(s_ln, b * LN_STEPS + 2 * LN_STEPS + 6)
                    nc.scalar.activation(std[:, :], mv[:, 1:2], ACT.Sqrt, bias=eps[:, 0:1]).then_inc(s_lna, 1)
                    act.wait_ge(s_ln, b * LN_STEPS + 2 * LN_STEPS + 12)
                    nc.scalar.activation(xn[:, :], x1[s][:, :], ACT.Identity, bias=lnw[:, 3:4],
                                         scale=lnw[:, 0:1]).then_inc(s_lna, 1)
                if gate_up:
                    act.wait_ge(s_gu, b + 2)
                    nc.scalar.activation(gate[:, :], ps_g[:, :], ACT.Silu, scale=dq[1 - s][:, 0:1]).then_inc(s_ha, 1)
                    act.wait_ge(s_hv, b * H_STEPS + H_STEPS + 4)
                    nc.scalar.activation(hr[:, :], h[:, :], ACT.Identity, bias=rnd[:, 0:1],
                                         scale=hmax[:, 1:2]).then_inc(s_ha, 1)
                if edges:
                    act.wait_ge(s_ln, b * LN_STEPS + 2 * LN_STEPS + 15)
                    nc.scalar.activation(z[:, :], xn[:, :], ACT.Identity, bias=rnd[:, 0:1],
                                         scale=amax[s][:, 1:2]).then_inc(s_lna, 1)
                if gate_up:
                    act.wait_ge(s_hv, b * H_STEPS + H_STEPS + 6)
                    nc.scalar.activation(hq[:, :], hr[:, :], ACT.Identity, bias=rnd[:, 1:2]).then_inc(s_ha, 1)
                if edges:
                    act.wait_ge(s_ln, b * LN_STEPS + 2 * LN_STEPS + 17)
                    nc.scalar.activation(q[:, :], z[:, :], ACT.Identity, bias=rnd[:, 1:2]).then_inc(s_lna, 1)

            tiles(act, step)

        @block.vector
        def _(dve):
            def a_low(s, b):
                dve.wait_ge(s_ah, b + 3)
                view = "p j (w d) -> p w j d"
                nc.vector.tensor_tensor(al[s][:, :, :].rearrange(view, w=WPT), a_raw[s][:, :, :, :],
                                        ah[s][:, :, :].rearrange(view, w=WPT).bitcast(F32), ALU.subtract).then_inc(s_al, 1)

            dve.wait_ge(s_nb, 32)
            a_low(0, -2)
            for j in range(NT):
                dve.wait_ge(s_yh, j + 1)
                nc.vector.scalar_tensor_tensor(out=yl[:, j, :], in0=y_raw[j % 2][:, :], scalar=norm[:, j, 0:1],
                                               in1=yh[:, j, :].bitcast(F32), op0=ALU.mult, op1=ALU.subtract
                                               ).then_inc(s_yl, 1)

            def step(s, edges, gate_up, down, b):
                k = [0]
                kh = [0]

                def ln(ins):
                    k[0] += 1
                    ins.then_inc(s_ln, 1)
                    if k[0] not in (4, 5):
                        dve.wait_ge(s_ln, b * LN_STEPS + 2 * LN_STEPS + k[0])

                def hs(ins):
                    kh[0] += 1
                    ins.then_inc(s_hv, 1)
                    dve.wait_ge(s_hv, b * H_STEPS + H_STEPS + kh[0])

                if down:
                    dve.wait_ge(s_st[s], b * 8 + 16 - 8 * s)
                    for m in range(2):
                        dve.wait_ge(s_dn, b * 2 + 1 + m)
                        nc.vector.scalar_tensor_tensor(out=o[s][:, m * 512:(m + 1) * 512], in0=ps_d[m][:, :],
                                                       scalar=dqh[:, 0:1], in1=x1[s][:, m * 512:(m + 1) * 512],
                                                       op0=ALU.mult, op1=ALU.add).then_inc(s_o, 1)
                    if edges or gate_up:
                        dve.wait_ge(s_o, b * 2 + 2)
                if edges:
                    a_low(1 - s, b + 1)
                    if not isinstance(b, int) or b >= -1:
                        dve.wait_ge(s_lna, b * 4 + 8)
                    for m in range(2):
                        dve.wait_ge(s_agg, b * 2 + 5 + m)
                        ln(nc.vector.scalar_tensor_tensor(
                            out=z[:, m * 512:(m + 1) * 512], in0=ps_a[m][:, :],
                            scalar=norm[:, b + 2, 1:2] if isinstance(b, int) else norm[:, bass.ds(b + 2, 1), 1],
                            in1=bias[:, m * 512:(m + 1) * 512], op0=ALU.mult, op1=ALU.add))
                    dve.wait_ge(s_x[s], b * 8 + 32 - 8 * s)
                    ln(nc.vector.scalar_tensor_tensor(out=x1[s][:, :], in0=z[:, :], scalar=0.0, in1=xin[s][:, :],
                                                      op0=ALU.max, op1=ALU.add))
                    for m in range(2):
                        ln(nc.vector.bn_stats(bn[:, m, :], x1[s][:, m * 512:(m + 1) * 512]))
                    dve.drain()
                    ln(nc.vector.bn_aggr(mv[:, :], bn[:, :, :].rearrange("p a b -> p (a b)")))
                    dve.wait_ge(s_lna, b * 4 + 9)
                    ln(nc.vector.reciprocal(lnw[:, 0:1], std[:, :]))
                    ln(nc.vector.tensor_tensor(lnw[:, 1:2], lnw[:, 0:1], lnw[:, 0:1], ALU.mult))
                    ln(nc.vector.scalar_tensor_tensor(out=lnw[:, 1:2], in0=mv[:, 1:2], scalar=LN_EPS,
                                                      in1=lnw[:, 1:2], op0=ALU.add, op1=ALU.mult))
                    ln(nc.vector.tensor_scalar(lnw[:, 1:2], lnw[:, 1:2], -0.5, 1.5, ALU.mult, ALU.add))
                    ln(nc.vector.tensor_tensor(lnw[:, 0:1], lnw[:, 0:1], lnw[:, 1:2], ALU.mult))
                    ln(nc.vector.scalar_tensor_tensor(out=lnw[:, 3:4], in0=mv[:, 0:1], scalar=-1.0,
                                                      in1=lnw[:, 0:1], op0=ALU.mult, op1=ALU.mult))
                    dve.wait_ge(s_lna, b * 4 + 10)
                    ln(nc.vector.tensor_reduce(amax[s][:, 0:1], xn[:, :], axis=AX.X, op=ALU.max,
                                               apply_absolute_value=True))
                    ln(nc.vector.tensor_scalar(amax[s][:, 0:1], amax[s][:, 0:1], Q_EPS, 1.0 / Q_MAX, ALU.max, ALU.mult))
                    ln(nc.vector.reciprocal(amax[s][:, 1:2], amax[s][:, 0:1]))
                    ln(nc.vector.tensor_scalar(dq[s][:, :], wsc[0:TR, 0:2], amax[s][:, 0:1], None, ALU.mult))
                if gate_up:
                    dve.wait_ge(s_ha, b * 3 + 4)
                    hs(nc.vector.scalar_tensor_tensor(out=h[:, :], in0=ps_u[:, :], scalar=dq[1 - s][:, 1:2],
                                                      in1=gate[:, :], op0=ALU.mult, op1=ALU.mult))
                    hs(nc.vector.tensor_reduce(hmax[:, 0:1], h[:, :], axis=AX.X, op=ALU.max,
                                               apply_absolute_value=True))
                    hs(nc.vector.tensor_scalar(hmax[:, 0:1], hmax[:, 0:1], Q_EPS, 1.0 / Q_MAX, ALU.max, ALU.mult))
                    hs(nc.vector.reciprocal(hmax[:, 1:2], hmax[:, 0:1]))
                    hs(nc.vector.tensor_scalar(dqh[:, 0:1], hmax[:, 0:1], wsc[0:TR, 2:3], None, ALU.mult))
                    dve.wait_ge(s_ha, b * 3 + 5)
                    hs(nc.vector.tensor_scalar(hr[:, :], hr[:, :], ROUND + Q_MIN, ROUND + Q_MAX, ALU.max, ALU.min))
                if edges:
                    dve.wait_ge(s_lna, b * 4 + 11)
                    ln(nc.vector.tensor_scalar(z[:, :], z[:, :], ROUND + Q_MIN, ROUND + Q_MAX, ALU.max, ALU.min))
                    assert k[0] == LN_STEPS
                if gate_up:
                    assert kh[0] == H_STEPS

            tiles(dve, step)

        @block.tensor
        def _(pe):
            def edge_sums(s, b, m, peeled):
                if m == 0:
                    pe.wait_ge(s_al, b + 3)
                if not peeled:
                    pe.wait_ge(s_ln, b * LN_STEPS + LN_STEPS + 1 + m)
                for a, (pa, py) in enumerate(((ah, yh), (ah, yl), (al, yh))):
                    for j in range(NT):
                        ins = nc.tensor.matmul(ps_a[m][:, :], pa[s][:, j, :], py[:, j, m * 512:(m + 1) * 512],
                                               start=(a == 0 and j == 0), stop=(a == 2 and j == NT - 1))
                ins.then_inc(s_agg, 1)

            def step(s, edges, gate_up, down, b):
                peeled = isinstance(b, int) and b < -1
                if edges:
                    edge_sums(s, b, 0, peeled)
                if down:
                    pe.wait_ge(s_ha, b * 3 + 3)
                    for k in range(KI):
                        ins = nc.tensor.transpose(ps_h[:, k * P:k * P + TR], hq[:, k * P:(k + 1) * P],
                                                  ident[0:TR, 0:TR])
                    ins.then_inc(s_htp, 1)
                    pe.wait_ge(s_ht, b + 1)
                    if not isinstance(b, int) or b >= 1:
                        pe.wait_ge(s_o, b * 2)
                    for m in range(2):
                        for k in range(KI):
                            ins = nc.tensor.matmul(ps_d[m][:, :], hqt[:, k, 0:TR], wdt[:, k, m * 512:(m + 1) * 512],
                                                   start=(k == 0), stop=(k == KI - 1))
                        ins.then_inc(s_dn, 1)
                if edges:
                    edge_sums(s, b, 1, peeled)
                if gate_up:
                    pe.wait_ge(s_lna, b * 4 + 8)
                    for k in range(KD):
                        ins = nc.tensor.transpose(ps_q[:, k * P:k * P + TR], q[:, k * P:(k + 1) * P],
                                                  ident[0:TR, 0:TR])
                    ins.then_inc(s_qtp, 1)
                    pe.wait_ge(s_qt, b + 2)
                    if not isinstance(b, int) or b >= 0:
                        pe.wait_ge(s_hv, b * H_STEPS + 1)
                    for w, ps in ((wgt, ps_g), (wut, ps_u)):
                        for k in range(KD):
                            ins = nc.tensor.matmul(ps[:, :], qt[:, k, 0:TR], w[:, k, :], start=(k == 0), stop=(k == KD - 1))
                    ins.then_inc(s_gu, 1)

            pe.wait_ge(s_yl, NT)
            tiles(pe, step)


_INS = ("x", "src", "dst", "edge_weight", "L0_gnn_W", "L0_gnn_b", "L0_mix_wq", "L0_mix_wk", "L0_mix_wv", "L0_mix_wo",
        "L0_mix_rf", "L0_ffn_w_gate", "L0_ffn_w_up", "L0_ffn_w_down")


def graph_layer(nc, x, src, dst, edge_weight, gnn_w, gnn_b, wq, wk, wv, wo, rf, w_gate, w_up, w_down, out):
    def scratch(name, shape):
        return nc.dram_tensor(name, shape, F32, kind="Internal").ap()

    y_scr = scratch("y_scr", (NT, TR, D))
    xt_scr = scratch("xt_scr", (NT, P, 2 * KD * TR))
    at_scr = scratch("at_scr", (NW, TR, NT * WIN))
    edge_scr = scratch("edge_scr", (TR, 3, NC))
    o_scr = scratch("o_scr", (KD, P, N))
    x1_scr = scratch("x1_scr", (NT, TR, D))
    norm_scr = scratch("norm_scr", (TR, NT, 2))
    node_stage(nc, x, src, dst, edge_weight, gnn_w, y_scr, xt_scr, at_scr, edge_scr)
    attention_stage(nc, xt_scr, wq, wk, wv, rf, o_scr)
    output_stage(nc, o_scr, wo, x, edge_scr, x1_scr, norm_scr)
    feed_forward_stage(nc, y_scr, at_scr, norm_scr, x1_scr, gnn_b, w_gate, w_up, w_down, out)


def kernel(**inputs):
    import numpy as _np
    import concourse.bacc as _bacc
    from concourse import mybir as _mybir
    from concourse.bass_utils import run_bass_kernel_spmd as _run

    nc = _bacc.Bacc("TRN2", target_bir_lowering=False, num_devices=1)
    arrays, args = {}, []
    for name in _INS:
        a = _np.ascontiguousarray(inputs[name])
        arrays[f"in_{name}_dram"] = a
        args.append(nc.dram_tensor(f"in_{name}_dram", a.shape, _mybir.dt.from_np(a.dtype), kind="ExternalInput").ap())
    args.append(nc.dram_tensor("out_0_dram", (N, D), F32, kind="ExternalOutput").ap())
    graph_layer(nc, *args)
    r = _run(nc, [arrays], core_ids=[0])
    return r.results[0]["out_0_dram"]
```

```python
import concourse.bass as bass
from concourse import mybir
from contextlib import ExitStack
import numpy as np

F32 = mybir.dt.float32
F32R = mybir.dt.float32r
BF16 = mybir.dt.bfloat16
I32 = mybir.dt.int32
I16 = mybir.dt.int16
ACT = mybir.ActivationFunctionType
ALU = mybir.AluOpType
AX = mybir.AxisListType

N = 1250
D = 1024
E = 20000
P = 128
TR = 125
NT = N // TR
KD = D // P
NC = E // TR
CR = NC // 2
WIN = 25
NW = N // WIN
NWT = NW + 1
WPT = TR // WIN
PARTS = 3
OHW = (NT - 1) * TR + P
PREP_STEPS = 27
NP = NC // 2
LN_EPS = 1e-5


def node_stage(nc, x, src, dst, edge_weight, gnn_w, y_scr, xt_scr, at_scr, edge_scr):
    with ExitStack() as ctx:
        def sb(name, shape, dt):
            return ctx.enter_context(nc.sbuf_tensor(name, shape, dt))

        def pb(name, shape, dt=F32):
            return ctx.enter_context(nc.psum_tensor(name, shape, dt))

        def sem(name):
            return ctx.enter_context(nc.semaphore(name))

        ident = sb("n_ident", [P, P], F32)
        xin = [sb(f"n_xin{s}", [TR, D], F32) for s in range(2)]
        xn = [sb(f"n_xn{s}", [TR, D], F32) for s in range(2)]
        xt = [sb(f"n_xt{s}", [P, 2, KD, TR], F32R) for s in range(2)]
        w_raw = [sb(f"n_wraw{s}", [P, D], F32) for s in range(2)]
        w_hi = sb("n_whi", [P, KD, D], F32R)
        w_lo = sb("n_wlo", [P, KD, D], F32R)
        ysb = [sb(f"n_y{s}", [TR, D], F32) for s in range(2)]
        bn = [sb(f"n_bn{s}", [TR, 2, 6], F32) for s in range(2)]
        mv = [sb(f"n_mv{s}", [TR, 2], F32) for s in range(2)]
        std = [sb(f"n_std{s}", [TR, 1], F32) for s in range(2)]
        rstd = [sb(f"n_rstd{s}", [TR, 1], F32) for s in range(2)]
        nmr = [sb(f"n_nmr{s}", [TR, 1], F32) for s in range(2)]
        eps = sb("n_eps", [TR, 1], F32)
        src_r = sb("n_srcr", [CR, 2, TR], I32)
        dst_r = sb("n_dstr", [CR, 2, TR], I32)
        w_r = sb("n_wr", [CR, 2, TR], F32)
        src_f = sb("n_srcf", [CR, 2, TR], F32)
        dst_f = sb("n_dstf", [CR, 2, TR], F32)
        dmm = sb("n_dmm", [CR, 2, 2], F32)
        dmm_b = sb("n_dmmb", [CR, 2, 2, NWT], F32)
        edge_t = sb("n_edget", [TR, 3, NC], F32)
        wrest = sb("n_wrest", [TR, 2, NC], F32)
        wpart = sb("n_wpart", [TR, NC, PARTS], BF16)
        dloc = sb("n_dloc", [TR, 2, NC], F32)
        iota_s = sb("n_iotas", [TR, OHW + 3], I16)
        iota_d = sb("n_iotad", [TR, PARTS, WIN], I16)
        oh_s = sb("n_ohs", [TR, 2, OHW + 3], BF16)
        oh_d = sb("n_ohd", [TR, 2, PARTS * WIN], BF16)
        zero = sb("n_zero", [1, P], BF16)
        at = [sb(f"n_at{s}", [TR, NT, WIN], F32) for s in range(2)]
        wlo = sb("n_wlo_v", [NWT, 2], F32)
        iota_w = sb("n_iotaw", [NWT, 2], I32)
        cnum = sb("n_cnum", [NWT, 2, NP], F32)
        cnum_i = sb("n_cnumi", [NWT, 2, NP], I32)
        inwin = sb("n_inwin", [NWT, NC], F32)
        cand = sb("n_cand", [NWT, 2, NP], F32)
        inpair = sb("n_inpair", [NWT, NP], F32)
        rng = sb("n_rng", [NWT, 4], F32)
        tri = sb("n_tri", [NWT, NWT], F32)
        table = sb("n_table", [1, NWT * 4], I32)
        wbase_i = sb("n_wbasei", [TR, NWT], I32)
        wbase = sb("n_wbase", [TR, NWT], F32)

        ps_t = [pb(f"n_pst{s}", [P, 512]) for s in range(2)]
        ps_y = [pb(f"n_psy{s}", [TR, 512]) for s in range(2)]
        ps_a = [[pb(f"n_psa{s}{b}", [P, 512]) for b in range(2)] for s in range(2)]

        s_edge = sem("n_edge_loaded")
        s_x = [sem(f"n_x_loaded{s}") for s in range(2)]
        s_w = [sem(f"n_w_loaded{s}") for s in range(2)]
        s_ident = sem("n_const")
        s_split = sem("n_w_high")
        s_wlow = sem("n_w_low")
        s_prep = sem("n_prep")
        s_prep_pe = sem("n_prep_pe")
        s_stat = sem("n_stat")
        s_std = sem("n_std")
        s_xn = sem("n_xn")
        s_tp = sem("n_transposed")
        s_hi = sem("n_xt_high")
        s_lo = sem("n_xt_low")
        s_yp = sem("n_y_product")
        s_ye = sem("n_y_evacuated")
        s_ys = [sem(f"n_y_stored{s}") for s in range(2)]
        s_xs = [sem(f"n_xt_stored{s}") for s in range(2)]
        s_dl = sem("n_dloc_ready")
        s_ohr = sem("n_onehot_ready")
        s_ohu = sem("n_onehot_used")
        s_wr = sem("n_window_ready")
        s_we = sem("n_window_evacuated")
        s_as = [sem(f"n_window_stored{s}") for s in range(2)]

        PS = 5
        block = ctx.enter_context(nc.Block())

        @block.sync
        def _(sp):
            half = "(t r e) -> r t e"
            sp.dma_start(src_r[:, :, :], src.rearrange(half, t=2, r=CR)).then_inc(s_edge, 16)
            sp.dma_start(dst_r[:, :, :], dst.rearrange(half, t=2, r=CR)).then_inc(s_edge, 16)
            sp.dma_start(w_r[:, :, :], edge_weight.rearrange(half, t=2, r=CR)).then_inc(s_edge, 16)
            for s in range(2):
                sp.dma_start(xin[s][:, :], x[s * TR:(s + 1) * TR, :]).then_inc(s_x[s], 16)
            for k in range(KD):
                if k >= 2:
                    sp.wait_ge(s_wlow, k - 1)
                sp.dma_start(w_raw[k % 2][:, :], gnn_w[k * P:(k + 1) * P, :]).then_inc(s_w[k % 2], 16)
            for s in range(2):
                sp.sem_inc(s_as[s], 16)
                sp.sem_inc(s_ys[s], 16)
                sp.sem_inc(s_xs[s], 16)
            sp.wait_ge(s_prep, 9)
            sp.dma_start(edge_scr, edge_t[:, :, :]).then_inc(s_edge, 16)
            with sp.Fori(0, NT // 2) as i:
                for s in range(2):
                    sp.wait_ge(s_lo, (i * 2 + s + 1) * 2 + 2)
                    sp.dma_start(xt_scr[bass.ds(i * 2 + s, 1), :, :].rearrange("a p n -> p (a n)"),
                                 xt[s][:, :, :, :].rearrange("p h k n -> p (h k n)").bitcast(F32)).then_inc(s_xs[s], 16)
                    nxt = sp.snap((i * 2 + s + 2) % NT)
                    sp.wait_ge(s_xn, i * 2 + s + 1)
                    sp.dma_start(xin[s][:, :], x[bass.ds(nxt * TR, TR), :]).then_inc(s_x[s], 16)
                    for q in range(WPT):
                        w = (i * 2 + s) * WPT + q
                        sp.wait_ge(s_we, w + 3)
                        sp.dma_start(at_scr[bass.ds(w, 1), :, :].rearrange("a p n -> p (a n)"),
                                     at[(s * WPT + q) % 2][:, :, :].rearrange("p j d -> p (j d)")
                                     ).then_inc(s_as[(s * WPT + q) % 2], 16)
                    sp.wait_ge(s_ye, (i * 2 + s + 1) * 2 + 2)
                    sp.dma_start(y_scr[bass.ds(i * 2 + s, 1), :, :].rearrange("a p n -> p (a n)"),
                                 ysb[s][:, :]).then_inc(s_ys[s], 16)
            sp.wait_ge(s_x[0], (NT // 2 + 1) * 16)
            sp.wait_ge(s_x[1], (NT // 2 + 1) * 16)
            for s in range(2):
                sp.wait_ge(s_xs[s], (NT // 2 + 1) * 16)
                sp.wait_ge(s_as[s], (NW // 2 + 1) * 16)
                sp.wait_ge(s_ys[s], (NT // 2 + 1) * 16)
            sp.wait_ge(s_edge, 64)

        @block.gpsimd
        def _(pool):
            nc.gpsimd.memset(ident[:, :], 0.0).then_inc(s_ident, 1)
            nc.gpsimd.memset(tri[:, :], 0.0).then_inc(s_ident, 1)
            nc.gpsimd.memset(zero[:, :], 0.0).then_inc(s_ident, 1)
            nc.gpsimd.memset(eps[:, :], LN_EPS).then_inc(s_ident, 1)
            nc.gpsimd.iota(iota_s[:, :], pattern=[[1, OHW + 3]], base=0, channel_multiplier=0).then_inc(s_ident, 1)
            nc.gpsimd.iota(iota_d[:, :, :], pattern=[[0, PARTS], [1, WIN]], base=0,
                           channel_multiplier=0).then_inc(s_ident, 1)
            nc.gpsimd.iota(iota_w[:, :], pattern=[[WIN, 2]], base=0, channel_multiplier=WIN).then_inc(s_ident, 1)
            nc.gpsimd.iota(cnum_i[:, 0, :], pattern=[[1, NP]], base=1, channel_multiplier=0).then_inc(s_ident, 1)
            nc.gpsimd.iota(cnum_i[:, 1, :], pattern=[[-1, NP]], base=NP, channel_multiplier=0).then_inc(s_ident, 1)
            nc.gpsimd.iota(wbase_i[:, :], pattern=[[WIN, NWT]], base=0, channel_multiplier=0).then_inc(s_ident, 1)
            pool.wait_ge(s_ident, 10)
            nc.gpsimd.affine_select(out=ident[:, :], in_=ident[:, :], compare_op=ALU.not_equal, fill=1.0,
                                    base=0, pattern=[[-1, P]], channel_multiplier=1).then_inc(s_ident, 1)
            nc.gpsimd.affine_select(out=tri[:, :], in_=tri[:, :], compare_op=ALU.is_ge, fill=1.0,
                                    base=0, pattern=[[-1, NWT]], channel_multiplier=1).then_inc(s_ident, 1)

        @block.scalar
        def _(act):
            def normalise(s, count):
                act.wait_ge(s_stat, count * PS + 3)
                nc.scalar.activation(std[s][:, :], mv[s][:, 1:2], ACT.Sqrt, bias=eps[:, 0:1]).then_inc(s_std, 1)
                act.wait_ge(s_stat, count * PS + 5)
                nc.scalar.activation(xn[s][:, :], xin[s][:, :], ACT.Identity, bias=nmr[s][:, 0:1],
                                     scale=rstd[s][:, 0:1]).then_inc(s_xn, 1)

            act.wait_ge(s_ident, 12)
            normalise(0, 0)
            for k in range(KD):
                act.wait_ge(s_w[k % 2], (k // 2 + 1) * 16)
                nc.scalar.activation(w_hi[:, k, :], w_raw[k % 2][:, :], ACT.Copy).then_inc(s_split, 1)
            with act.Fori(0, NT // 2) as i:
                for s in range(2):
                    t = i * 2 + s
                    act.wait_ge(s_xs[s], (i + 1) * 16)
                    for b in range(2):
                        act.wait_ge(s_tp, t * 2 + b + 1)
                        nc.scalar.activation(
                            xt[s][:, 0, 4 * b:4 * b + 4, :],
                            ps_t[b][:, 0:4 * TR].rearrange("p (k n) -> p k n", k=4), ACT.Copy).then_inc(s_hi, 1)
                    normalise(1 - s, t + 1)
                    act.wait_ge(s_ys[s], (i + 1) * 16)
                    for b in range(2):
                        act.wait_ge(s_yp, t * 2 + b + 1)
                        nc.scalar.activation(ysb[s][:, b * 512:(b + 1) * 512], ps_y[b][:, :],
                                             ACT.Copy).then_inc(s_ye, 1)

        @block.vector
        def _(dve):
            prep = [0]

            def step(ins):
                prep[0] += 1
                ins.then_inc(s_prep, 1)
                dve.wait_ge(s_prep, prep[0])

            def statistics(s, count, loaded):
                dve.wait_ge(s_x[s], loaded)
                nc.vector.bn_stats(bn[s][:, 0, :], xin[s][:, 0:512]).then_inc(s_stat, 1)
                nc.vector.bn_stats(bn[s][:, 1, :], xin[s][:, 512:1024]).then_inc(s_stat, 1)
                dve.drain()
                nc.vector.bn_aggr(mv[s][:, :], bn[s][:, :, :].rearrange("p a b -> p (a b)")).then_inc(s_stat, 1)
                dve.wait_ge(s_std, count + 1)
                nc.vector.reciprocal(rstd[s][:, :], std[s][:, :]).then_inc(s_stat, 1)
                dve.wait_ge(s_stat, count * PS + 4)
                nc.vector.scalar_tensor_tensor(out=nmr[s][:, :], in0=mv[s][:, 0:1], scalar=-1.0,
                                               in1=rstd[s][:, :], op0=ALU.mult, op1=ALU.mult).then_inc(s_stat, 1)

            statistics(0, 0, 16)
            dve.wait_ge(s_edge, 48)
            step(nc.vector.tensor_copy(src_f[:, :, :], src_r[:, :, :]))
            step(nc.vector.tensor_copy(dst_f[:, :, :], dst_r[:, :, :]))
            step(nc.vector.tensor_reduce(dmm[:, :, 0:1], dst_f[:, :, :], axis=AX.X, op=ALU.min))
            step(nc.vector.tensor_reduce(dmm[:, :, 1:2], dst_f[:, :, :], axis=AX.X, op=ALU.max))
            step(nc.vector.tensor_copy(dmm_b[:, :, :, :],
                                       dmm[:, :, :].unsqueeze(3).broadcast_to([CR, 2, 2, NWT])))
            dve.wait_ge(s_ident, 12)
            step(nc.vector.tensor_copy(wlo[:, :], iota_w[:, :]))
            step(nc.vector.tensor_copy(cnum[:, :, :], cnum_i[:, :, :]))
            step(nc.vector.tensor_copy(wbase[:, :], wbase_i[:, :]))
            dve.wait_ge(s_prep_pe, 1)
            step(nc.vector.tensor_copy(edge_t[:, :, :], ps_t[0][0:TR, 0:3 * NC].rearrange(
                "p (a c) -> p a c", a=3)))
            step(nc.vector.tensor_copy(wpart[:, :, 0], edge_t[:, 2, :]))
            step(nc.vector.tensor_tensor(wrest[:, 0, :], edge_t[:, 2, :], wpart[:, :, 0], ALU.subtract))
            step(nc.vector.tensor_copy(wpart[:, :, 1], wrest[:, 0, :]))
            step(nc.vector.tensor_tensor(wrest[:, 1, :], wrest[:, 0, :], wpart[:, :, 1], ALU.subtract))
            step(nc.vector.tensor_copy(wpart[:, :, 2], wrest[:, 1, :]))
            dve.wait_ge(s_prep_pe, 2)
            lows = ps_t[1][0:NWT, 0:2 * NC].rearrange("v (m c) -> v m c", m=2)
            step(nc.vector.tensor_scalar(inwin[:, :], lows[:, 0, :], wlo[:, 1:2], None, ALU.is_lt))
            step(nc.vector.scalar_tensor_tensor(out=inwin[:, :], in0=lows[:, 1, :], scalar=wlo[:, 0:1],
                                                in1=inwin[:, :], op0=ALU.is_ge, op1=ALU.mult))
            step(nc.vector.tensor_reduce(inpair[:, :], inwin[:, :].rearrange("v (c a) -> v c a", a=2),
                                         axis=AX.X, op=ALU.max))
            step(nc.vector.tensor_tensor(cand[:, :, :], cnum[:, :, :],
                                         inpair[:, :].unsqueeze(1).broadcast_to([NWT, 2, NP]), ALU.mult))
            step(nc.vector.tensor_reduce(rng[:, 0:2], cand[:, :, :], axis=AX.X, op=ALU.max))
            step(nc.vector.tensor_scalar(rng[:, 2:3], rng[:, 1:2], -1.0, float(NP), ALU.mult, ALU.add))
            step(nc.vector.tensor_copy(rng[:, 1:2], rng[:, 0:1]))
            step(nc.vector.tensor_scalar(rng[:, 0:1], rng[:, 2:3], float(NP - 1), None, ALU.min))
            step(nc.vector.tensor_scalar(rng[:, 3:4], rng[:, 0:1], 1.0, None, ALU.add))
            step(nc.vector.tensor_tensor(rng[:, 1:2], rng[:, 1:2], rng[:, 3:4], ALU.max))
            step(nc.vector.tensor_tensor(rng[:, 3:4], rng[:, 1:2], rng[:, 0:1], ALU.subtract))
            dve.wait_ge(s_prep_pe, 3)
            step(nc.vector.scalar_tensor_tensor(out=rng[:, 2:3], in0=ps_y[0][0:NWT, 0:1], scalar=float(NP),
                                                in1=rng[:, 0:1], op0=ALU.add, op1=ALU.subtract))
            dve.wait_ge(s_prep_pe, 4)
            step(nc.vector.tensor_copy(table[0:1, :].rearrange("p (v q) -> p q v", q=4),
                                       ps_y[1][0:1, 0:4 * NWT].rearrange("p (q v) -> p q v", q=4)))
            assert prep[0] == PREP_STEPS
            for k in range(KD):
                dve.wait_ge(s_split, k + 1)
                nc.vector.tensor_tensor(w_lo[:, k, :], w_raw[k % 2][:, :], w_hi[:, k, :].bitcast(F32),
                                        ALU.subtract).then_inc(s_wlow, 1)

            nc.vector.sem_inc(s_ohr, 2 * NP)

            def build(par, w):
                first = dve.value_load(table[0:1, bass.ds(w * 4, 1)], min_val=0, max_val=NP - 1)
                end = dve.value_load(table[0:1, bass.ds(w * 4 + 1, 1)], min_val=1, max_val=NP)
                shift = dve.value_load(table[0:1, bass.ds(w * 4 + 2, 1)], min_val=1, max_val=NWT * NP)
                nc.vector.tensor_scalar(dloc[:, par, :], edge_t[:, 1, :], wbase[:, bass.ds(w, 1)], None,
                                        ALU.subtract).then_inc(s_dl, 1)
                with dve.Fori(first, end) as pair:
                    visit = dve.snap((shift + pair) * 2)
                    for h in range(2):
                        c = dve.snap(pair * 2 + h)
                        dve.wait_ge(s_ohu, visit + h + 1)
                        nc.vector.tensor_scalar(oh_s[:, h, :], iota_s[:, :], edge_t[:, 0, bass.ds(c, 1)],
                                                None, ALU.is_equal)
                        dve.wait_ge(s_dl, w + 1)
                        nc.vector.scalar_tensor_tensor(
                            out=oh_d[:, h, :].rearrange("p (m d) -> p m d", m=PARTS),
                            in0=iota_d[:, :, :], scalar=dloc[:, par, bass.ds(c, 1)],
                            in1=wpart[:, bass.ds(c, 1), :].rearrange("p a m -> p (a m)").unsqueeze(2)
                            .broadcast_to([TR, PARTS, WIN]),
                            op0=ALU.is_equal, op1=ALU.mult).then_inc(s_ohr, 1)

            def sum_parts(s, q, i):
                w = (i * 2 + s) * WPT + q
                par = (s * WPT + q) % 2
                dve.wait_ge(s_wr, w + 1)
                dve.wait_ge(s_as[par], (i * WPT + (s * WPT + q) // 2 + 1) * 16)
                for b in range(2):
                    ins = nc.vector.tensor_reduce(
                        at[par][:, 5 * b:5 * b + 5, :],
                        ps_a[par][b][0:TR, 0:5 * PARTS * WIN].rearrange("p (j m d) -> p j d m", j=5, m=PARTS),
                        axis=AX.X, op=ALU.add)
                ins.then_inc(s_we, 1)

            build(0, 0)
            with dve.Fori(0, NT // 2) as i:
                for s in range(2):
                    t = i * 2 + s
                    for b in range(2):
                        dve.wait_ge(s_hi, t * 2 + b + 1)
                        nc.vector.tensor_tensor(
                            xt[s][:, 1, 4 * b:4 * b + 4, :],
                            ps_t[b][:, 0:4 * TR].rearrange("p (k n) -> p k n", k=4),
                            xt[s][:, 0, 4 * b:4 * b + 4, :].bitcast(F32), ALU.subtract
                        ).then_inc(s_lo, 1)
                    statistics(1 - s, t + 1, (i + 1 + s) * 16)
                    for q in range(WPT):
                        build((s * WPT + q + 1) % 2, dve.snap(t * WPT + q + 1))
                        sum_parts(s, q, i)

        @block.tensor
        def _(pe):
            pe.wait_ge(s_ident, 12)
            pe.wait_ge(s_prep, 2)
            for a, rows in enumerate((src_f, dst_f, w_r)):
                for h in range(2):
                    ins = nc.tensor.transpose(ps_t[0][0:TR, a * NC + h * CR:a * NC + (h + 1) * CR],
                                              rows[:, h, :], ident[0:CR, 0:CR])
            ins.then_inc(s_prep_pe, 1)
            pe.wait_ge(s_prep, 5)
            for m in range(2):
                for h in range(2):
                    ins = nc.tensor.matmul(ps_t[1][0:NWT, m * NC + h * CR:m * NC + (h + 1) * CR],
                                           dmm_b[:, h, m, :], ident[0:CR, 0:CR], start=True, stop=True)
            ins.then_inc(s_prep_pe, 1)
            pe.wait_ge(s_prep, PREP_STEPS - 2)
            nc.tensor.matmul(ps_y[0][0:NWT, 0:1], tri[:, :], rng[:, 3:4], start=True, stop=True).then_inc(s_prep_pe, 1)
            pe.wait_ge(s_prep, PREP_STEPS - 1)
            for q in range(4):
                ins = nc.tensor.matmul(ps_y[1][0:1, q * NWT:(q + 1) * NWT], rng[:, q:q + 1], ident[0:NWT, 0:NWT],
                                       start=True, stop=True)
            ins.then_inc(s_prep_pe, 1)
            pe.wait_ge(s_prep, PREP_STEPS)
            pe.wait_ge(s_wlow, KD)
            pe.sem_inc(s_ohu, 2 * NP + 2)
            pe.sem_inc(s_we, 2)
            pe.sem_inc(s_ye, 2)
            pe.sem_inc(s_lo, 2)

            PIECES = 2 * 3 * KD

            def product(s, t, lo, hi):
                for n in range(lo, hi):
                    b, m, k = n // (3 * KD), n // KD % 3, n % KD
                    part, w = ((0, w_hi), (0, w_lo), (1, w_hi))[m]
                    if n % (3 * KD) == 0:
                        pe.wait_ge(s_ye, t * 2 + b + 1)
                    ins = nc.tensor.matmul(ps_y[b][:, :], xt[s][:, part, k, :], w[:, k, b * 512:(b + 1) * 512],
                                           start=(m == 0 and k == 0), stop=(m == 2 and k == KD - 1))
                    if n % (3 * KD) == 3 * KD - 1:
                        ins.then_inc(s_yp, 1)

            def window(t, s, q):
                w = pe.snap(t * WPT + q)
                par = (s * WPT + q) % 2
                first = pe.value_load(table[0:1, bass.ds(w * 4, 1)], min_val=0, max_val=NP - 1)
                end = pe.value_load(table[0:1, bass.ds(w * 4 + 1, 1)], min_val=1, max_val=NP)
                shift = pe.value_load(table[0:1, bass.ds(w * 4 + 2, 1)], min_val=1, max_val=NWT * NP)
                pe.wait_ge(s_we, w + 1)
                for b in range(2):
                    nc.tensor.matmul(ps_a[par][b][:, 511:512], zero[:, :], zero[:, 0:1], start=True, stop=False,
                                     skip_group_check=True)
                with pe.Fori(first, end) as pair:
                    visit = pe.snap((shift + pair) * 2)
                    for h in range(2):
                        pe.wait_ge(s_ohr, visit + h + 1)
                        for j in range(NT):
                            ins = nc.tensor.matmul(
                                ps_a[par][j // 5][:, (j % 5) * PARTS * WIN:(j % 5 + 1) * PARTS * WIN],
                                oh_s[:, h, j * TR:j * TR + P], oh_d[:, h, :],
                                start=False, stop=False, skip_group_check=True)
                        ins.then_inc(s_ohu, 1)
                for b in range(2):
                    ins = nc.tensor.matmul(ps_a[par][b][:, 511:512], zero[:, :], zero[:, 0:1], start=False,
                                           stop=True, skip_group_check=True)
                ins.then_inc(s_wr, 1)

            with pe.Fori(0, NT // 2) as i:
                for s in range(2):
                    t = i * 2 + s
                    pe.wait_ge(s_xn, t + 1)
                    for b in range(2):
                        pe.wait_ge(s_lo, t * 2 + b + 1)
                        for k in range(4):
                            ins = nc.tensor.transpose(ps_t[b][:, k * TR:(k + 1) * TR],
                                                      xn[s][:, (4 * b + k) * P:(4 * b + k + 1) * P],
                                                      ident[0:TR, 0:TR])
                        ins.then_inc(s_tp, 1)
                    window(t, s, 0)
                    pe.wait_ge(s_lo, t * 2 + 4)
                    for q in range(WPT):
                        product(s, t, q * PIECES // WPT, (q + 1) * PIECES // WPT)
                        if q < WPT - 1:
                            window(t, s, q + 1)


NH = 16
DH = D // NH
M = 256
JP = D // P
NF = 2 * M // P
DV = DH + 1
CH = [(0, 4), (4, 4), (8, 2)]
TWO_PI = 6.28318501
ROUND = 1.5 * 2.0 ** 23
Z_MIN = 1e-6


def attention_stage(nc, xt_scr, wq, wk, wv, rf, o_scr):
    with ExitStack() as ctx:
        def sb(name, shape, dt):
            return ctx.enter_context(nc.sbuf_tensor(name, shape, dt))

        def sem(name):
            return ctx.enter_context(nc.semaphore(name))

        xa = sb("a_x", [P, 2, KD, N], F32R)
        w_raw = sb("a_wraw", [P, 3, D], F32)
        wt = sb("a_wt", [P, 3, 2, KD, P], F32R)
        qt = sb("a_qt", [P, 2, N], F32R)
        kt = sb("a_kt", [P, 2, N], F32R)
        vt = sb("a_vt", [P, N], F32)
        sq = [sb(f"a_sq{m}", [P, N], F32) for m in range(2)]
        rf_in = sb("a_rfin", [P, 2, 2, DH], F32)
        bd32 = sb("a_bd32", [P, 2 * M], F32)
        bd = sb("a_bd", [P, 2, 2 * M], F32R)
        ub = [sb(f"a_u{s}", [P, 512], F32) for s in range(2)]
        rb = [sb(f"a_r{s}", [P, 512], F32) for s in range(2)]
        kf = [sb(f"a_kf{s}", [TR, 2, 2 * M], F32) for s in range(2)]
        qf = sb("a_qf", [P, 2, NF, 500], F32)
        vs = sb("a_vs", [TR, NT, 2, DV], F32)
        kv = sb("a_kv", [P, 2, NF, DV], F32)
        ob = sb("a_o", [TR, 4, P], F32)
        ot = sb("a_ot", [P, N], F32)
        es = sb("a_exp", [TR, 2, NT, 2], F32)
        zt = sb("a_z", [TR, 4, 4], F32)
        ident = sb("a_ident", [P, P], F32)
        hsel = sb("a_hsel", [P, 2], F32)
        c_round = sb("a_cround", [P, 1], F32)
        c_quarter = sb("a_cquarter", [P, 1], F32)
        c_ln = sb("a_cln", [P, 1], F32)

        gen = [ctx.enter_context(nc.psum_tensor(f"a_psg{s}", [P, 512], F32)) for s in range(3)]
        fea = [ctx.enter_context(nc.psum_tensor(f"a_psf{s}", [P, 512], F32)) for s in range(3)]
        acc = [ctx.enter_context(nc.psum_tensor(f"a_psa{s}", [P, 512], F32)) for s in range(2)]

        s_x = [sem(f"a_x_loaded{c}") for c in range(3)]
        s_rf = sem("a_rf_loaded")
        s_raw = [sem(f"a_weights_loaded{m}") for m in range(3)]
        s_cst = sem("a_const")
        s_bd = sem("a_bd")
        s_gen = sem("a_gen")
        s_fea = sem("a_fea")
        s_whi = sem("a_w_high")
        s_wlo = sem("a_w_low")
        s_hi = [sem("a_q_high"), sem("a_k_high")]
        s_lo = [sem("a_q_low"), sem("a_k_low")]
        s_sq = [sem("a_q_squared"), sem("a_k_squared")]
        s_vt = sem("a_v_copied")
        s_exp = [sem("a_q_exp"), sem("a_k_exp")]
        s_vs = sem("a_v_scaled")
        s_v1 = sem("a_v_ones")
        s_u = sem("a_rounded")
        s_r = sem("a_remainder")
        s_abs = sem("a_abs")
        s_sc = sem("a_sincos")
        s_kv = sem("a_kv_tile")
        s_kve = sem("a_kv_evacuated")
        s_out = sem("a_out_product")
        s_z = sem("a_z_step")
        s_norm = sem("a_out_scaled")
        s_ot = sem("a_out_transposed")
        s_st = sem("a_stored")

        MM = 3 * KD
        K_PLAN = [[("p", 0, 0, 0, 12)], [("p", 0, 0, 12, MM)],
                  [("p", 0, 1, 0, 8)], [("p", 0, 1, 8, 16)], [("p", 0, 1, 16, MM)],
                  [("p", 0, 2, 0, 12)], [("p", 0, 2, 12, MM)],
                  [("w", 1, 0)], [("w", 1, 1), ("n", 0)], [("w", 2, 0)], [("w", 2, 1)], []]
        Q_PLAN = [[("p", 1, 0, 0, MM)], [("p", 1, 1, 0, 12)],
                  [("p", 1, 1, 12, MM)], [("p", 1, 2, 0, MM), ("o", 0)],
                  [("p", 2, 0, 0, MM)], [("n", 1), ("p", 2, 1, 0, MM), ("o", 1)],
                  [("p", 2, 2, 0, MM)],
                  [("v", 0), ("v", 1), ("w", 0, 0), ("w", 0, 1), ("v", 2), ("o", 2)]]
        START = [("w", 1, 0), ("w", 1, 1), ("w", 2, 0), ("w", 2, 1), ("w", 0, 0), ("w", 0, 1),
                 ("p", 1, 0, 0, MM), ("p", 1, 1, 0, MM), ("p", 1, 2, 0, MM), ("n", 1),
                 ("p", 2, 0, 0, MM), ("p", 2, 1, 0, MM), ("p", 2, 2, 0, MM), ("v", 0), ("v", 1), ("v", 2)]

        def readers(pieces):
            found = []
            for piece in pieces:
                if piece[0] == "w":
                    found.append((s_wlo, 6, (4, 0, 2)[piece[1]] + piece[2]))
                elif piece[0] == "p" and piece[4] == MM:
                    found.append((s_vt, 3, piece[2]) if piece[1] == 2 else (s_lo[piece[1]], 3, piece[2]))
                elif piece[0] == "v":
                    found.append((s_vs, 3, piece[1]))
                elif piece[0] == "o":
                    found.append((s_ot, 3, piece[1]))
            return found

        READ = readers(piece for step in K_PLAN + Q_PLAN for piece in step)
        NG = len(READ)
        START_READ = readers(START)
        NS = len(START_READ)
        FREAD = []
        for t in range(NT):
            FREAD.append((s_r, NT + 12, t))
            FREAD += [(s_exp[x[1]], 1, 0) for x in K_PLAN[t] if x[0] == "n"]
        for i in range(6):
            FREAD += [(s_r, NT + 12, NT + 2 * i), (s_r, NT + 12, NT + 2 * i + 1)]
            FREAD += [(s_exp[x[1]], 1, 0) for x in Q_PLAN[i] if x[0] == "n"]
        NU = NT + 12
        NE = len(FREAD)
        FS = 3
        assert NG % 3 == 0 and NS % 3 == 0 and NE % 3 == 0 and NU % 2 == 0
        UNIT = [f for f in range(NE) if FREAD[f][0] is s_r]
        NORM = {m: [f for f in range(NE) if FREAD[f][0] is s_exp[m]][0] for m in range(2)}

        def use(piece):
            key = {"w": lambda: (s_wlo, (4, 0, 2)[piece[1]] + piece[2]),
                   "p": lambda: (s_vt, piece[2]) if piece[1] == 2 else (s_lo[piece[1]], piece[2]),
                   "v": lambda: (s_vs, piece[1]), "o": lambda: (s_ot, piece[1])}[piece[0]]()
            where = [[g for g, r in enumerate(table) if r[0] is key[0] and r[2] == key[1]]
                     for table in (READ, START_READ)]
            return where[0][0], (where[1][0] if where[1] else None)

        def chunk(c):
            first, number = CH[c]
            return first * TR, number * TR

        def filled(eng, j, piece):
            g, g0 = use(piece)
            eng.wait_ge(s_gen, g0 + 1 if j is None else j * NG + NS + g + 1)
            return gen[(g0 if j is None else g) % 3]

        block = ctx.enter_context(nc.Block())

        def units():
            return [(c, h, m) for c in range(3) for h in range(2) for m in range(2)]

        @block.sync
        def _(sp):
            for m in (1, 2, 0):
                sp.dma_start(w_raw[:, m, :], (wq, wk, wv)[m][0:P, :]).then_inc(s_raw[m], 16)
            sp.dma_start(rf_in[:, :, 0, :], rf.rearrange("(m p) d -> p m d", p=P)).then_inc(s_rf, 16)
            sp.dma_start(rf_in[:, :, 1, :], rf.rearrange("(m p) d -> p m d", p=P)).then_inc(s_rf, 16)
            for c, (t0, nt) in enumerate(CH):
                for t in range(t0, t0 + nt):
                    sp.dma_start(xa[:, :, :, t * TR:(t + 1) * TR].bitcast(F32),
                                 xt_scr[t, :, :].rearrange("p (h k n) -> p h k n", h=2, k=KD)).then_inc(s_x[c], 16)
            sp.wait_ge(s_gen, 6)
            for m in (1, 2, 0):
                sp.dma_start(w_raw[:, m, :], (wq, wk, wv)[m][P:2 * P, :]).then_inc(s_raw[m], 16)
            with sp.Fori(0, JP) as j:
                nxt = sp.snap((j + 2) % JP)
                for m in (1, 2, 0):
                    sp.wait_ge(s_gen, j * NG + NS + use(("w", m, 1))[0] + 1)
                    sp.dma_start(w_raw[:, m, :], (wq, wk, wv)[m][bass.ds(nxt * P, P), :]).then_inc(s_raw[m], 16)
                sp.wait_ge(s_ot, j * 3 + 6)
                sp.dma_start(o_scr[bass.ds(j, 1), :, :].rearrange("a p n -> p (a n)"), ot[:, :]).then_inc(s_st, 16)
            for m in range(3):
                sp.wait_ge(s_raw[m], 16 * (JP + 2))
            sp.wait_ge(s_st, 16 * (JP + 1))

        @block.gpsimd
        def _(pool):
            nc.gpsimd.memset(ident[:, :], 0.0).then_inc(s_cst, 1)
            nc.gpsimd.memset(hsel[:, :], 0.0).then_inc(s_cst, 1)
            nc.gpsimd.memset(bd32[:, :], 0.0).then_inc(s_cst, 1)
            nc.gpsimd.memset(c_round[:, :], ROUND).then_inc(s_cst, 1)
            nc.gpsimd.memset(c_quarter[:, :], float(np.float32(np.pi / 2))).then_inc(s_cst, 1)
            nc.gpsimd.memset(c_ln[:, :], -float(np.log(np.sqrt(M)))).then_inc(s_cst, 1)
            pool.wait_ge(s_cst, 6)
            nc.gpsimd.affine_select(out=ident[:, :], in_=ident[:, :], compare_op=ALU.not_equal, fill=1.0,
                                    base=0, pattern=[[-1, P]], channel_multiplier=1).then_inc(s_cst, 1)
            pool.wait_ge(s_cst, 7)
            nc.gpsimd.memset(hsel[0:DH, 0:1], 1.0).then_inc(s_cst, 1)
            pool.wait_ge(s_cst, 8)
            nc.gpsimd.memset(hsel[DH:P, 1:2], 1.0).then_inc(s_cst, 1)
            pool.sem_inc(s_lo[0], 3)
            pool.sem_inc(s_ot, 3)
            pool.sem_inc(s_exp[0], 1)
            pool.sem_inc(s_r, NU)
            pool.sem_inc(s_norm, 6)
            pool.sem_inc(s_sc, 2)
            pool.sem_inc(s_st, 16)

        @block.scalar
        def _(act):
            act.wait_ge(s_cst, 9)

            def read(j, piece):
                kind = piece[0]
                if kind == "n":
                    m = piece[1]
                    act.wait_ge(s_fea, 2 if j is None else j * NE + FS + NORM[m] + 1)
                    nc.scalar.activation(es[:, m, :, :], fea[1 if j is None else NORM[m] % 3][0:TR, 0:2 * NT].rearrange(
                        "p (t h) -> p t h", h=2), ACT.Exp, bias=c_ln[0:TR, 0:1], scale=-0.5).then_inc(s_exp[m], 1)
                elif kind == "w":
                    m, b = piece[1:]
                    bank = filled(act, j, piece)
                    nc.scalar.activation(wt[:, m, 0, 4 * b:4 * b + 4, :],
                                         bank[:, :].rearrange("p (k n) -> p k n", k=4), ACT.Copy).then_inc(s_whi, 1)
                elif kind == "p" and piece[4] == MM:
                    m, c = piece[1:3]
                    o, size = chunk(c)
                    bank = filled(act, j, piece)
                    if m < 2:
                        nc.scalar.activation((qt, kt)[m][:, 0, o:o + size], bank[:, 0:size], ACT.Copy
                                             ).then_inc(s_hi[m], 1)
                        nc.scalar.activation(sq[m][:, o:o + size], bank[:, 0:size], ACT.Square).then_inc(s_sq[m], 1)
                    else:
                        nc.scalar.activation(vt[:, o:o + size], bank[:, 0:size], ACT.Copy).then_inc(s_vt, 1)
                elif kind == "o":
                    c = piece[1]
                    o, size = chunk(c)
                    if c == 0:
                        act.wait_ge(s_st, (j + 1) * 16)
                    bank = filled(act, j, piece)
                    nc.scalar.activation(ot[:, o:o + size], bank[:, 0:size], ACT.Copy).then_inc(s_ot, 1)

            for n in range(6):
                read(None, START[n])
            act.wait_ge(s_bd, 1)
            nc.scalar.activation(bd[:, 0, :], bd32[:, :], ACT.Copy).then_inc(s_bd, 1)
            for piece in START[6:]:
                read(None, piece)

            with act.Fori(0, JP) as j:
                def rounded(n, rows, size):
                    act.wait_ge(s_sc, j * NU + n + 1)
                    act.wait_ge(s_fea, j * NE + FS + UNIT[n] + 1)
                    nc.scalar.activation(ub[n % 2][0:rows, 0:size], fea[UNIT[n] % 3][0:rows, 0:size],
                                         ACT.Identity, bias=c_round[0:rows, 0:1]).then_inc(s_u, 1)

                def sincos(n, rows, size, sin_out, cos_out):
                    act.wait_ge(s_abs, j * NU + n + 1)
                    nc.scalar.activation(sin_out, rb[n % 2][0:rows, 0:size], ACT.Sin, scale=-TWO_PI)
                    nc.scalar.activation(cos_out, ub[n % 2][0:rows, 0:size], ACT.Sin,
                                         bias=c_quarter[0:rows, 0:1], scale=-TWO_PI).then_inc(s_sc, 1)

                for t in range(NT + 2):
                    if t < NT:
                        rounded(t, TR, 512)
                    if 0 < t <= NT:
                        if t - 1 >= 2:
                            act.wait_ge(s_kv, j * NT + t - 2)
                        sincos(t - 1, TR, 512, kf[(t - 1) % 2][:, 1, :], kf[(t - 1) % 2][:, 0, :])
                    for piece in K_PLAN[t]:
                        read(j, piece)

                def q_sincos(n):
                    c, h, m = units()[n]
                    size = chunk(c)[1]
                    if c > 0:
                        act.wait_ge(s_out, j * 6 + 2 * (c - 1) + h + 1)
                    sincos(NT + n, P, size, qf[:, h, 2 + m, 0:size], qf[:, h, m, 0:size])

                for i in range(8):
                    for n in (2 * i, 2 * i + 1):
                        if n < 12:
                            rounded(NT + n, P, chunk(units()[n][0])[1])
                        if 0 < n < 13:
                            q_sincos(n - 1)
                    for piece in Q_PLAN[i]:
                        read(j, piece)

        @block.vector
        def _(dve):
            def read(j, piece):
                kind = piece[0]
                if kind == "w":
                    m, b = piece[1:]
                    n = (4, 0, 2)[m] + b
                    g, g0 = use(piece)
                    dve.wait_ge(s_whi, n + 1 if j is None else j * 6 + 6 + n + 1)
                    nc.vector.tensor_tensor(wt[:, m, 1, 4 * b:4 * b + 4, :],
                                            gen[(g0 if j is None else g) % 3][:, :].rearrange("p (k n) -> p k n", k=4),
                                            wt[:, m, 0, 4 * b:4 * b + 4, :].bitcast(F32), ALU.subtract
                                            ).then_inc(s_wlo, 1)
                elif kind == "p" and piece[4] == MM and piece[1] < 2:
                    m, c = piece[1:3]
                    o, size = chunk(c)
                    x = (qt, kt)[m]
                    g, g0 = use(piece)
                    dve.wait_ge(s_hi[m], c + 1 if j is None else j * 3 + (0, 3)[m] + c + 1)
                    dve.wait_ge(s_sq[m], c + 1 if j is None else j * 3 + (0, 3)[m] + c + 1)
                    nc.vector.tensor_tensor(x[:, 1, o:o + size], gen[(g0 if j is None else g) % 3][:, 0:size],
                                            x[:, 0, o:o + size].bitcast(F32), ALU.subtract).then_inc(s_lo[m], 1)
                elif kind == "v":
                    c = piece[1]
                    t0, nt = CH[c]
                    bank = filled(dve, j, piece)
                    dve.wait_ge(s_exp[1], 1 if j is None else j + 2)
                    if c == 0:
                        nc.vector.tensor_copy(vs[:, :, :, DH], es[:, 1, :, :]).then_inc(s_v1, 1)
                    nc.vector.tensor_tensor(
                        vs[:, t0:t0 + nt, :, 0:DH],
                        bank[0:TR, 0:nt * P].rearrange("p (t h d) -> p t h d", t=nt, h=2),
                        es[:, 1, t0:t0 + nt, :].unsqueeze(3).broadcast_to([TR, nt, 2, DH]),
                        ALU.mult).then_inc(s_vs, 1)

            for piece in START[:6]:
                read(None, piece)
            dve.wait_ge(s_cst, 9)
            dve.wait_ge(s_fea, 1)
            for h in range(2):
                for m in range(2):
                    ins = nc.vector.tensor_scalar(
                        bd32[DH * h:DH * h + DH, M * h + P * m:M * h + P * m + P],
                        fea[0][DH * h:DH * h + DH, P * m:P * m + P], float(1 / (2 * np.pi)), None, ALU.mult)
            ins.then_inc(s_bd, 1)
            dve.wait_ge(s_bd, 2)
            nc.vector.tensor_tensor(bd[:, 1, :], bd32[:, :], bd[:, 0, :].bitcast(F32), ALU.subtract).then_inc(s_bd, 1)
            for piece in START[6:]:
                read(None, piece)

            with dve.Fori(0, JP) as j:
                def remainder(n, rows, size):
                    u, r = ub[n % 2][0:rows, 0:size], rb[n % 2][0:rows, 0:size]
                    dve.wait_ge(s_sc, j * NU + n + 1)
                    dve.wait_ge(s_u, j * NU + n + 1)
                    nc.vector.scalar_tensor_tensor(out=r, in0=u, scalar=ROUND, in1=fea[UNIT[n] % 3][0:rows, 0:size],
                                                   op0=ALU.subtract, op1=ALU.subtract).then_inc(s_r, 1)
                    dve.wait_ge(s_r, j * NU + NU + n + 1)
                    nc.vector.tensor_scalar(u.bitcast(I32), r.bitcast(I32), 0x7fffffff, None,
                                            ALU.bitwise_and).then_inc(s_abs, 1)

                def scaled(c, h):
                    t0, nt = CH[c]
                    prod = acc[h][0:TR, 0:nt * DV].rearrange("p (t v) -> p t v", v=DV)
                    scale = es[:, 0, t0:t0 + nt, h]
                    first = (2 * c + h) * 4
                    dve.wait_ge(s_out, j * 6 + 2 * c + h + 1)
                    nc.vector.tensor_tensor(zt[:, 0, 0:nt], prod[:, :, DH], scale, ALU.mult).then_inc(s_z, 1)
                    dve.wait_ge(s_z, j * 24 + first + 1)
                    nc.vector.tensor_scalar(zt[:, 1, 0:nt], zt[:, 0, 0:nt], Z_MIN, None, ALU.max).then_inc(s_z, 1)
                    dve.wait_ge(s_z, j * 24 + first + 2)
                    nc.vector.reciprocal(zt[:, 2, 0:nt], zt[:, 1, 0:nt]).then_inc(s_z, 1)
                    dve.wait_ge(s_z, j * 24 + first + 3)
                    nc.vector.tensor_tensor(zt[:, 3, 0:nt], zt[:, 2, 0:nt], scale, ALU.mult).then_inc(s_z, 1)
                    dve.wait_ge(s_z, j * 24 + first + 4)
                    nc.vector.tensor_tensor(ob[:, 0:nt, DH * h:DH * h + DH], prod[:, :, 0:DH],
                                            zt[:, 3, 0:nt].unsqueeze(2).broadcast_to([TR, nt, DH]),
                                            ALU.mult).then_inc(s_norm, 1)

                for t in range(NT + 2):
                    if t < NT:
                        remainder(t, TR, 512)
                    for piece in K_PLAN[t]:
                        read(j, piece)
                dve.wait_ge(s_kv, j * NT + NT)
                for h in range(2):
                    ins = nc.vector.tensor_copy(kv[:, h, :, :].rearrange("p f v -> p (f v)"), acc[h][:, 0:NF * DV])
                ins.then_inc(s_kve, 1)
                for i in range(8):
                    if i < 6:
                        remainder(NT + 2 * i, P, chunk(i // 2)[1])
                    if i >= 2:
                        scaled(i // 2 - 1, i % 2)
                    if i < 6:
                        remainder(NT + 2 * i + 1, P, chunk(i // 2)[1])
                    for piece in Q_PLAN[i]:
                        read(j, piece)

        @block.tensor
        def _(pe):
            def free(j, g):
                if j is None:
                    if g >= 3:
                        sem_, _, n = START_READ[g - 3]
                        pe.wait_ge(sem_, n + 1)
                elif g < 3:
                    sem_, per, n = READ[(g - 3) % NG]
                    pe.wait_ge(sem_, j * per + n + 1)
                    pe.wait_ge(s_vs, j * 3 + 3)
                else:
                    sem_, per, n = READ[g - 3]
                    pe.wait_ge(sem_, j * per + per + n + 1)

            def free_fea(j, f):
                sem_, per, n = FREAD[(f - 3) % NE]
                pe.wait_ge(sem_, j * per + n + 1 + (per if f >= 3 else 0))

            PASSES = ((0, 0), (0, 1), (1, 0))

            def do(j, piece):
                kind = piece[0]
                if kind == "n":
                    m = piece[1]
                    if j is None:
                        bank = fea[1]
                        pe.wait_ge(s_sq[m], 3)
                    else:
                        free_fea(j, NORM[m])
                        bank = fea[NORM[m] % 3]
                        pe.wait_ge(s_sq[m], j * 3 + 3 + (0, 3)[m])
                    for t in range(NT):
                        ins = nc.tensor.matmul(bank[0:TR, 2 * t:2 * t + 2], sq[m][:, t * TR:(t + 1) * TR], hsel[:, :],
                                               start=True, stop=True)
                    ins.then_inc(s_fea, 1)
                    return
                g, g0 = use(piece)
                bank = gen[(g0 if j is None else g) % 3]
                if kind != "p" or piece[3] == 0:
                    free(j, g0 if j is None else g)
                if kind == "w":
                    m, b = piece[1:]
                    if b == 0:
                        pe.wait_ge(s_raw[m], 16 if j is None else j * 16 + 32)
                    for k in range(4):
                        ins = nc.tensor.transpose(bank[:, k * P:(k + 1) * P],
                                                  w_raw[:, m, (4 * b + k) * P:(4 * b + k + 1) * P], ident[:, :])
                    ins.then_inc(s_gen, 1)
                elif kind == "p":
                    m, c, first, end = piece[1:]
                    o, size = chunk(c)
                    if c == 0 and first == 0:
                        last = (6, 2, 4)[m]
                        pe.wait_ge(s_wlo, last if j is None else j * 6 + last + (0, 6, 6)[m])
                    if j is None and m == 1:
                        pe.wait_ge(s_x[c], 16 * CH[c][1])
                    for n in range(first, end):
                        a, k = n // KD, n % KD
                        pw, px = PASSES[a]
                        ins = nc.tensor.matmul(bank[:, 0:size], wt[:, m, pw, k, :], xa[:, px, k, o:o + size],
                                               start=(n == 0), stop=(n == MM - 1))
                    if end == MM:
                        ins.then_inc(s_gen, 1)
                elif kind == "v":
                    c = piece[1]
                    t0, nt = CH[c]
                    pe.wait_ge(s_vt, c + 1 if j is None else j * 3 + 3 + c + 1)
                    for i in range(nt):
                        ins = nc.tensor.transpose(bank[0:TR, i * P:(i + 1) * P],
                                                  vt[:, (t0 + i) * TR:(t0 + i + 1) * TR], ident[:, :])
                    ins.then_inc(s_gen, 1)
                else:
                    c = piece[1]
                    pe.wait_ge(s_norm, j * 6 + 6 + 2 * c + 2)
                    for i in range(CH[c][1]):
                        ins = nc.tensor.transpose(bank[:, i * TR:(i + 1) * TR], ob[:, i, :], ident[0:TR, 0:TR])
                    ins.then_inc(s_gen, 1)

            pe.wait_ge(s_cst, 9)
            for piece in START[:6]:
                do(None, piece)
            pe.wait_ge(s_rf, 32)
            for m in range(2):
                ins = nc.tensor.transpose(fea[0][:, m * P:(m + 1) * P], rf_in[:, m, :, :].rearrange("p a d -> p (a d)"),
                                          ident[:, :])
            ins.then_inc(s_fea, 1)
            for piece in START[6:]:
                do(None, piece)
            pe.sem_inc(s_fea, 1)
            pe.wait_ge(s_bd, 3)
            pe.wait_ge(s_exp[1], 1)
            with pe.Fori(0, JP) as j:
                pe.wait_ge(s_lo[1], j * 3 + 3)
                for t in range(NT + 2):
                    if t < NT:
                        free_fea(j, UNIT[t])
                        for a, (pk, pr) in enumerate(PASSES):
                            ins = nc.tensor.matmul(fea[UNIT[t] % 3][0:TR, :], kt[:, pk, t * TR:(t + 1) * TR],
                                                   bd[:, pr, :], start=(a == 0), stop=(a == 2))
                        ins.then_inc(s_fea, 1)
                    if t >= 2:
                        s = t - 2
                        if s == 0:
                            pe.wait_ge(s_v1, j + 1)
                            pe.wait_ge(s_vs, j * 3 + 3)
                            pe.wait_ge(s_norm, j * 6 + 6)
                        pe.wait_ge(s_sc, j * NU + s + 3)
                        for h in range(2):
                            for f in range(NF):
                                ins = nc.tensor.matmul(
                                    acc[h][:, f * DV:(f + 1) * DV],
                                    kf[s % 2][:, f // 2, h * M + f % 2 * P:h * M + f % 2 * P + P], vs[:, s, h, :],
                                    start=(s == 0 and f == 0), stop=(s == NT - 1 and f == NF - 1),
                                    skip_group_check=True)
                        ins.then_inc(s_kv, 1)
                    for piece in K_PLAN[t]:
                        do(j, piece)

                def angles(c, h):
                    o, size = chunk(c)
                    for m in range(2):
                        n = NT + 4 * c + 2 * h + m
                        free_fea(j, UNIT[n])
                        for a, (pr, pq) in enumerate(PASSES):
                            ins = nc.tensor.matmul(fea[UNIT[n] % 3][:, 0:size],
                                                   bd[:, pr, h * M + m * P:h * M + m * P + P], qt[:, pq, o:o + size],
                                                   start=(a == 0), stop=(a == 2))
                        ins.then_inc(s_fea, 1)

                def output(c, h):
                    nt = CH[c][1]
                    if c == 0:
                        pe.wait_ge(s_kve, j + 1)
                    else:
                        pe.wait_ge(s_norm, j * 6 + 6 + 2 * (c - 1) + h + 1)
                    pe.wait_ge(s_sc, j * NU + NT + 4 * c + 2 * h + 4)
                    for i in range(nt):
                        for f in range(NF):
                            ins = nc.tensor.matmul(acc[h][0:TR, i * DV:(i + 1) * DV], qf[:, h, f, i * TR:(i + 1) * TR],
                                                   kv[:, h, f, :], start=(f == 0), stop=(f == NF - 1))
                    ins.then_inc(s_out, 1)

                pe.wait_ge(s_lo[0], j * 3 + 6)
                for i in range(8):
                    if i >= 2:
                        output(i // 2 - 1, i % 2)
                    if i < 6:
                        angles(i // 2, i % 2)
                    for piece in Q_PLAN[i]:
                        do(j, piece)


FI = 512
KI = FI // P


def output_stage(nc, o_scr, wo, x, edge_scr, x1_scr, norm_scr):
    CPT = NC // NT
    with ExitStack() as ctx:
        def sb(name, shape, dt):
            return ctx.enter_context(nc.sbuf_tensor(name, shape, dt))

        def sem(name):
            return ctx.enter_context(nc.semaphore(name))

        ident = sb("o_ident", [P, P], F32)
        w_raw = [sb(f"o_wraw{s}", [P, D], F32) for s in range(2)]
        wt = sb("o_wt", [P, 2, KD, D], F32R)
        of = [sb(f"o_of{s}", [P, KD, TR], F32) for s in range(2)]
        oh = [sb(f"o_oh{s}", [P, 2, KD, TR], F32R) for s in range(2)]
        xin = [sb(f"o_x{s}", [TR, D], F32) for s in range(2)]
        xout = [sb(f"o_xo{s}", [TR, D], F32) for s in range(2)]
        edge_t = sb("o_edge", [TR, 3, NC], F32)
        tile_f = sb("o_tile", [TR, 2, NC], F32)
        row_f = sb("o_row", [TR, 2, NC], F32)
        wrest = sb("o_wrest", [TR, 2, NC], F32)
        wpart = sb("o_wpart", [TR, NC, 4], BF16)
        iota_t = sb("o_iotat", [TR, CPT, NT], F32)
        iota_p = sb("o_iotap", [TR, CPT, TR], F32)
        oh_t = [sb(f"o_oht{s}", [TR, 2, CPT, NT], BF16) for s in range(2)]
        rhs = [sb(f"o_rhs{s}", [TR, 2, CPT, 4, NT], BF16) for s in range(2)]
        oh_p = [sb(f"o_ohp{s}", [TR, 2, CPT, TR + 1], BF16) for s in range(2)]
        sums = sb("o_sums", [TR, 2, 4 * NT], F32)
        nrm = sb("o_nrm", [TR, 2, 6, NT], F32)
        nout = sb("o_nout", [TR, NT, 2], F32)

        ps_t = [ctx.enter_context(nc.psum_tensor(f"o_pst{s}", [P, 512], F32)) for s in range(2)]
        ps_o = [ctx.enter_context(nc.psum_tensor(f"o_pso{s}", [TR, 512], F32)) for s in range(4)]
        ps_h = [ctx.enter_context(nc.psum_tensor(f"o_psh{s}", [TR, 512], F32)) for s in range(2)]

        s_w = [sem(f"o_w_loaded{s}") for s in range(2)]
        s_o = [sem(f"o_o_loaded{s}") for s in range(2)]
        s_x = [sem(f"o_x_loaded{s}") for s in range(2)]
        s_e = sem("o_edge_loaded")
        s_cst = sem("o_const")
        s_tp = sem("o_transposed")
        s_whi = sem("o_w_high")
        s_wlo = sem("o_w_low")
        s_ohi = sem("o_o_high")
        s_olo = sem("o_o_low")
        s_pr = sem("o_product")
        s_add = sem("o_added")
        s_st = [sem(f"o_stored{s}") for s in range(2)]
        s_hp = sem("o_hist_step")
        s_ht = sem("o_hist_tile_onehot")
        s_hr = sem("o_hist_onehot")
        s_hu = sem("o_hist_used")
        s_sq = sem("o_hist_sqrt")
        s_ns = sem("o_norm_stored")
        block = ctx.enter_context(nc.Block())

        @block.sync
        def _(sp):
            for k in range(KD):
                if k >= 2:
                    sp.wait_ge(s_tp, 2 * (k - 1))
                sp.dma_start(w_raw[k % 2][:, :], wo[k * P:(k + 1) * P, :]).then_inc(s_w[k % 2], 16)
                if k == 1:
                    sp.dma_start(edge_t[:, :, :], edge_scr).then_inc(s_e, 16)
                    for s in range(2):
                        sp.dma_start(of[s][:, :, :], o_scr[:, :, s * TR:(s + 1) * TR].rearrange("j p n -> p j n")
                                     ).then_inc(s_o[s], 16)
                        sp.dma_start(xin[s][:, :], x[s * TR:(s + 1) * TR, :]).then_inc(s_x[s], 16)
            for s in range(2):
                sp.sem_inc(s_st[s], 16)
            with sp.Fori(0, NT // 2) as i:
                for s in range(2):
                    nxt = sp.snap((i * 2 + s + 2) % NT)
                    sp.wait_ge(s_olo, i * 2 + s + 1)
                    sp.dma_start(of[s][:, :, :], o_scr[:, :, bass.ds(nxt * TR, TR)].rearrange("j p n -> p j n")
                                 ).then_inc(s_o[s], 16)
                    sp.wait_ge(s_add, (i * 2 + s) * 2 + 6)
                    sp.dma_start(xin[s][:, :], x[bass.ds(nxt * TR, TR), :]).then_inc(s_x[s], 16)
                    sp.dma_start(x1_scr[bass.ds(i * 2 + s, 1), :, :].rearrange("a p n -> p (a n)"),
                                 xout[s][:, :]).then_inc(s_st[s], 16)
            sp.wait_ge(s_hp, HIST_STEPS)
            sp.dma_start(norm_scr, nout[:, :, :]).then_inc(s_ns, 16)
            sp.wait_ge(s_ns, 16)
            for s in range(2):
                sp.wait_ge(s_st[s], 16 * (NT // 2 + 1))
                sp.wait_ge(s_o[s], 16 * (NT // 2 + 1))
                sp.wait_ge(s_x[s], 16 * (NT // 2 + 1))

        @block.gpsimd
        def _(pool):
            nc.gpsimd.memset(ident[:, :], 0.0).then_inc(s_cst, 1)
            nc.gpsimd.iota(iota_t[:, :, :].bitcast(I32), pattern=[[0, CPT], [1, NT]], base=0,
                           channel_multiplier=0).then_inc(s_cst, 1)
            nc.gpsimd.iota(iota_p[:, :, :].bitcast(I32), pattern=[[0, CPT], [1, TR]], base=0,
                           channel_multiplier=0).then_inc(s_cst, 1)
            nc.gpsimd.memset(wpart[:, :, 0], 1.0).then_inc(s_cst, 1)
            pool.wait_ge(s_cst, 4)
            nc.gpsimd.affine_select(out=ident[:, :], in_=ident[:, :], compare_op=ALU.not_equal, fill=1.0,
                                    base=0, pattern=[[-1, P]], channel_multiplier=1).then_inc(s_cst, 1)
            nc.gpsimd.tensor_copy(iota_t[:, :, :], iota_t[:, :, :].bitcast(I32)).then_inc(s_cst, 1)
            nc.gpsimd.tensor_copy(iota_p[:, :, :], iota_p[:, :, :].bitcast(I32)).then_inc(s_cst, 1)

        @block.scalar
        def _(act):
            for n in range(2 * KD):
                m, b = n // 2, n % 2
                act.wait_ge(s_tp, n + 1)
                nc.scalar.activation(wt[:, 0, 4 * b:4 * b + 4, m * P:(m + 1) * P],
                                     ps_t[b][:, :].rearrange("p (k n) -> p k n", k=4), ACT.Copy).then_inc(s_whi, 1)

            def high(s, i, t):
                act.wait_ge(s_o[s], i * 16 + 16)
                act.wait_ge(s_pr, t * 2 + 2)
                nc.scalar.activation(oh[s][:, 0, :, :], of[s][:, :, :], ACT.Copy).then_inc(s_ohi, 1)

            high(0, 0, 0)
            with act.Fori(0, NT // 2) as i:
                for s in range(2):
                    high(1 - s, i + s, i * 2 + s + 1)
            act.wait_ge(s_hp, HIST_SQRT)
            nc.scalar.activation(nrm[:, :, 4, :], nrm[:, :, 3, :], ACT.Sqrt).then_inc(s_sq, 1)

        @block.vector
        def _(dve):
            steps = [0]

            def step(ins):
                steps[0] += 1
                ins.then_inc(s_hp, 1)
                dve.wait_ge(s_hp, steps[0])

            for n in range(2 * KD):
                m, b = n // 2, n % 2
                dve.wait_ge(s_whi, n + 1)
                nc.vector.tensor_tensor(wt[:, 1, 4 * b:4 * b + 4, m * P:(m + 1) * P],
                                        ps_t[b][:, :].rearrange("p (k n) -> p k n", k=4),
                                        wt[:, 0, 4 * b:4 * b + 4, m * P:(m + 1) * P].bitcast(F32),
                                        ALU.subtract).then_inc(s_wlo, 1)
            dve.wait_ge(s_e, 16)
            dve.wait_ge(s_cst, 7)
            step(nc.vector.tensor_scalar(tile_f[:, :, :], edge_t[:, 0:2, :], 1.0 / TR, -0.5 + 0.5 / TR, ALU.mult, ALU.add))
            step(nc.vector.tensor_scalar(tile_f[:, :, :], tile_f[:, :, :], ROUND, ROUND, ALU.add, ALU.subtract))
            step(nc.vector.scalar_tensor_tensor(out=row_f[:, :, :], in0=tile_f[:, :, :], scalar=-float(TR),
                                                in1=edge_t[:, 0:2, :], op0=ALU.mult, op1=ALU.add))
            step(nc.vector.tensor_copy(wpart[:, :, 1], edge_t[:, 2, :]))
            step(nc.vector.tensor_tensor(wrest[:, 0, :], edge_t[:, 2, :], wpart[:, :, 1], ALU.subtract))
            step(nc.vector.tensor_copy(wpart[:, :, 2], wrest[:, 0, :]))
            step(nc.vector.tensor_tensor(wrest[:, 1, :], wrest[:, 0, :], wpart[:, :, 2], ALU.subtract))
            step(nc.vector.tensor_copy(wpart[:, :, 3], wrest[:, 1, :]))

            def low(s, t):
                dve.wait_ge(s_ohi, t + 1)
                nc.vector.tensor_tensor(oh[s][:, 1, :, :], of[s][:, :, :], oh[s][:, 0, :, :].bitcast(F32),
                                        ALU.subtract).then_inc(s_olo, 1)

            low(0, 0)
            with dve.Fori(0, NT // 2) as i:
                for s in range(2):
                    t = i * 2 + s
                    low(1 - s, t + 1)
                    dve.wait_ge(s_hu, t + 1)
                    edges = bass.ds(t * CPT, CPT)
                    for e in range(2):
                        nc.vector.tensor_tensor(oh_p[s][:, e, :, 0:TR], iota_p[:, :, :],
                                                row_f[:, e, edges].unsqueeze(2).broadcast_to([TR, CPT, TR]), ALU.is_equal)
                        nc.vector.tensor_tensor(oh_t[s][:, e, :, :], iota_t[:, :, :],
                                                tile_f[:, e, edges].unsqueeze(2).broadcast_to([TR, CPT, NT]),
                                                ALU.is_equal).then_inc(s_ht, 1)
                    for e in range(2):
                        dve.wait_ge(s_ht, t * 2 + e + 1)
                        ins = nc.vector.tensor_tensor(rhs[s][:, e, :, :, :],
                                                      oh_t[s][:, e, :, :].unsqueeze(2).broadcast_to([TR, CPT, 4, NT]),
                                                      wpart[:, edges, :].unsqueeze(3).broadcast_to([TR, CPT, 4, NT]),
                                                      ALU.mult)
                    ins.then_inc(s_hr, 1)
                    dve.wait_ge(s_x[s], i * 16 + 16)
                    dve.wait_ge(s_st[s], i * 16 + 16)
                    for b in range(2):
                        dve.wait_ge(s_pr, t * 2 + b + 5)
                        nc.vector.tensor_tensor(xout[s][:, b * 512:(b + 1) * 512], ps_o[2 * s + b][:, :],
                                                xin[s][:, b * 512:(b + 1) * 512], ALU.add).then_inc(s_add, 1)
            dve.wait_ge(s_hu, NT + 2)
            for e in range(2):
                step(nc.vector.tensor_copy(sums[:, e, :], ps_h[e][:, 0:4 * NT]))
            sv = sums[:, :, :].rearrange("p e (m t) -> p e m t", m=4)
            step(nc.vector.tensor_scalar(nrm[:, :, 0, :], sv[:, :, 0, :], 1.0, None, ALU.max))
            step(nc.vector.tensor_tensor(nrm[:, :, 1, :], sv[:, :, 1, :], sv[:, :, 2, :], ALU.add))
            step(nc.vector.tensor_tensor(nrm[:, :, 1, :], nrm[:, :, 1, :], sv[:, :, 3, :], ALU.add))
            step(nc.vector.scalar_tensor_tensor(out=nrm[:, :, 2, :], in0=sv[:, :, 0, :], scalar=0.0,
                                                in1=nrm[:, :, 1, :], op0=ALU.is_equal, op1=ALU.add))
            step(nc.vector.tensor_tensor(nrm[:, :, 3, :], nrm[:, :, 2, :], nrm[:, :, 0, :], ALU.mult))
            assert steps[0] == HIST_SQRT
            dve.wait_ge(s_sq, 1)
            step(nc.vector.reciprocal(nrm[:, :, 5, :], nrm[:, :, 4, :]))
            step(nc.vector.tensor_tensor(nrm[:, :, 4, :], nrm[:, :, 5, :], nrm[:, :, 5, :], ALU.mult))
            step(nc.vector.tensor_tensor(nrm[:, :, 4, :], nrm[:, :, 4, :], nrm[:, :, 3, :], ALU.mult))
            step(nc.vector.tensor_scalar(nrm[:, :, 4, :], nrm[:, :, 4, :], -0.5, 1.5, ALU.mult, ALU.add))
            step(nc.vector.tensor_tensor(nout[:, :, :], nrm[:, :, 4, :].rearrange("p e t -> p t e"),
                                         nrm[:, :, 5, :].rearrange("p e t -> p t e"), ALU.mult))
            assert steps[0] == HIST_STEPS

        @block.tensor
        def _(pe):
            pe.sem_inc(s_hu, 2)
            pe.sem_inc(s_pr, 4)
            pe.sem_inc(s_add, 4)
            pe.wait_ge(s_cst, 5)
            for n in range(2 * KD):
                m, b = n // 2, n % 2
                if b == 0:
                    pe.wait_ge(s_w[m % 2], (m // 2 + 1) * 16)
                if n >= 2:
                    pe.wait_ge(s_wlo, n - 1)
                for k in range(4):
                    ins = nc.tensor.transpose(ps_t[b][:, k * P:(k + 1) * P],
                                              w_raw[m % 2][:, (4 * b + k) * P:(4 * b + k + 1) * P], ident[:, :])
                ins.then_inc(s_tp, 1)
            pe.wait_ge(s_wlo, 2 * KD)
            pe.wait_ge(s_hr, 1)
            for e in range(2):
                nc.tensor.matmul(ps_h[e][:, 511:512], oh_p[0][:, 0, 0, 0:TR], oh_p[0][:, 0, 0, 0:1], start=True, stop=False,
                                 skip_group_check=True)
            with pe.Fori(0, NT // 2) as i:
                for s in range(2):
                    t = i * 2 + s
                    pe.wait_ge(s_olo, t + 1)
                    for b in range(2):
                        pe.wait_ge(s_add, t * 2 + b + 1)
                        for a, (po, pw) in enumerate(((0, 0), (0, 1), (1, 0))):
                            for k in range(KD):
                                ins = nc.tensor.matmul(ps_o[2 * s + b][:, :], oh[s][:, po, k, :],
                                                       wt[:, pw, k, b * 512:(b + 1) * 512],
                                                       start=(a == 0 and k == 0), stop=(a == 2 and k == KD - 1))
                        ins.then_inc(s_pr, 1)
                    pe.wait_ge(s_hr, t + 1)
                    for q in range(CPT):
                        for e in range(2):
                            ins = nc.tensor.matmul(ps_h[e][:, 0:4 * NT], oh_p[s][:, e, q, 0:TR],
                                                   rhs[s][:, e, q, :, :].rearrange("p m t -> p (m t)"),
                                                   start=False, stop=False, skip_group_check=True)
                    ins.then_inc(s_hu, 1)


HIST_SQRT = 8 + 2 + 5
HIST_STEPS = HIST_SQRT + 5


HO = FI // P
LN_STEPS = 17
H_STEPS = 6
Q_MAX = 127.0
Q_MIN = -128.0
Q_EPS = 1e-5


def feed_forward_stage(nc, y_scr, at_scr, norm_scr, x1_scr, gnn_b, w_gate, w_up, w_down, out):
    with ExitStack() as outer:
        wgt = outer.enter_context(nc.sbuf_tensor("f_wgt", [P, KD, FI], BF16))
        wut = outer.enter_context(nc.sbuf_tensor("f_wut", [P, KD, FI], BF16))
        wdt = outer.enter_context(nc.sbuf_tensor("f_wdt", [P, KI, D], BF16))
        ident = outer.enter_context(nc.sbuf_tensor("f_ident", [P, P], BF16))
        wsc = outer.enter_context(nc.sbuf_tensor("f_wsc", [P, 3], F32))
        norm = outer.enter_context(nc.sbuf_tensor("f_norm", [TR, NT, 2], F32))
        yh = outer.enter_context(nc.sbuf_tensor("f_yh", [TR, NT, D], F32R))
        yl = outer.enter_context(nc.sbuf_tensor("f_yl", [TR, NT, D], F32R))
        feed_forward_operands(nc, y_scr, norm_scr, w_gate, w_up, w_down, wgt, wut, wdt, ident, wsc, norm, yh, yl)
        feed_forward_tiles(nc, at_scr, x1_scr, gnn_b, wgt, wut, wdt, ident, wsc, norm, yh, yl, out)


def feed_forward_operands(nc, y_scr, norm_scr, w_gate, w_up, w_down, wgt, wut, wdt, ident, wsc, norm, yh, yl):
    with ExitStack() as ctx:
        def sb(name, shape, dt):
            return ctx.enter_context(nc.sbuf_tensor(name, shape, dt))

        def sem(name):
            return ctx.enter_context(nc.semaphore(name))

        WN = FI * D // P
        raw = [sb(f"t_raw{m}", [P, WN], F32) for m in range(3)]
        tern = [sb(f"t_tern{m}", [P, WN], BF16) for m in range(3)]
        part = sb("t_part", [P, 3], F32)
        scale = sb("t_scale", [P, 3], F32)
        ones = sb("t_ones", [P, P], F32)
        ps_s = [ctx.enter_context(nc.psum_tensor(f"t_pss{m}", [P, 512], F32)) for m in range(3)]
        ps_t = [ctx.enter_context(nc.psum_tensor(f"t_pst{s}", [P, 1024], BF16)) for s in range(2)]
        s_w = [sem(f"t_loaded{m}") for m in range(3)]
        s_c = sem("t_const")
        s_n = sem("t_norm_loaded")
        s_y = [sem(f"t_y_loaded{i}") for i in range(NT // 2)]
        s_yh = sem("t_y_high")
        s_yl = sem("t_y_low")
        s_v = sem("t_vector")
        s_sum = sem("t_summed")
        s_tp = sem("t_transposed")
        s_ev = sem("t_evacuated")
        VS = 7
        PAIRS = ((0,), (1, 2), (3, 4))
        block = ctx.enter_context(nc.Block())

        @block.sync
        def _(sp):
            sp.dma_start(norm[:, :, :], norm_scr).then_inc(s_n, 16)
            for m, w in enumerate((w_gate, w_up, w_down)):
                sp.dma_start(raw[m][:, :], w.rearrange("(a p) n -> p a n", p=P)).then_inc(s_w[m], 16)
                for i in PAIRS[m]:
                    sp.dma_start(yl[:, 2 * i:2 * i + 2, :].bitcast(F32),
                                 y_scr[2 * i:2 * i + 2].rearrange("a p n -> p a n")).then_inc(s_y[i], 16)
            sp.wait_ge(s_yl, NT)

        @block.gpsimd
        def _(pool):
            nc.gpsimd.memset(ident[:, :], 0.0).then_inc(s_c, 1)
            nc.gpsimd.memset(ones[:, :], 1.0).then_inc(s_c, 1)
            pool.wait_ge(s_c, 2)
            nc.gpsimd.affine_select(out=ident[:, :], in_=ident[:, :], compare_op=ALU.not_equal, fill=1.0,
                                    base=0, pattern=[[-1, P]], channel_multiplier=1).then_inc(s_c, 1)

        @block.vector
        def _(dve):
            steps = [0]

            def step(ins):
                steps[0] += 1
                ins.then_inc(s_v, 1)
                dve.wait_ge(s_v, steps[0])

            for m in range(3):
                dve.wait_ge(s_w[m], 16)
                step(nc.vector.tensor_reduce(part[:, m:m + 1], raw[m][:, :], axis=AX.X, op=ALU.add,
                                             apply_absolute_value=True))
                dve.wait_ge(s_sum, m + 1)
                step(nc.vector.tensor_scalar(wsc[:, m:m + 1], ps_s[m][:, 0:1], 1.0 / (FI * D), Q_EPS, ALU.mult, ALU.max))
                step(nc.vector.reciprocal(scale[:, m:m + 1], wsc[:, m:m + 1]))
                step(nc.vector.tensor_scalar(raw[m][:, :], raw[m][:, :], scale[:, m:m + 1], 1.0, ALU.mult, ALU.min))
                step(nc.vector.tensor_scalar(raw[m][:, :], raw[m][:, :], -1.0, ROUND, ALU.max, ALU.add))
                h = WN // 2
                step(nc.vector.tensor_scalar(tern[m][:, 0:h], raw[m][:, 0:h], ROUND, None, ALU.subtract))
                step(nc.vector.tensor_scalar(tern[m][:, h:WN], raw[m][:, h:WN], ROUND, None, ALU.subtract))
                for j in [2 * i + e for i in PAIRS[m] for e in range(2)]:
                    dve.wait_ge(s_yh, j + 1)
                    nc.vector.scalar_tensor_tensor(out=yl[:, j, :], in0=yl[:, j, :].bitcast(F32),
                                                   scalar=norm[:, j, 0:1], in1=yh[:, j, :].bitcast(F32),
                                                   op0=ALU.mult, op1=ALU.subtract).then_inc(s_yl, 1)

        @block.tensor
        def _(pe):
            pe.wait_ge(s_c, 3)
            n = 0
            for m in range(3):
                pe.wait_ge(s_v, VS * m + 1)
                nc.tensor.matmul(ps_s[m][:, 0:1], ones[:, :], part[:, m:m + 1], start=True, stop=True).then_inc(s_sum, 1)
                pe.wait_ge(s_v, VS * m + VS)
                rows, cols = (HO, KD) if m < 2 else (KD, KI)
                for c in range(4):
                    if n >= 2:
                        pe.wait_ge(s_ev, n - 1)
                    for b in range(8):
                        blk = 8 * c + b
                        k, a = blk // rows, blk % rows
                        ins = nc.tensor.transpose(ps_t[n % 2][:, b * P:(b + 1) * P],
                                                  tern[m][:, a * cols * P + k * P:a * cols * P + (k + 1) * P], ident[:, :])
                    ins.then_inc(s_tp, 1)
                    n += 1

        @block.scalar
        def _(act):
            act.wait_ge(s_n, 16)
            for n in range(12):
                m, c = n // 4, n % 4
                if c == 0:
                    for j in [2 * i + e for i in PAIRS[m] for e in range(2)]:
                        act.wait_ge(s_y[j // 2], 16)
                        nc.scalar.activation(yh[:, j, :], yl[:, j, :].bitcast(F32), ACT.Copy,
                                             scale=norm[:, j, 0:1]).then_inc(s_yh, 1)
                wt = (wgt, wut, wdt)[m]
                act.wait_ge(s_tp, n + 1)
                nc.scalar.activation(wt[:, :, :].rearrange("p k n -> p (k n)")[:, c * 1024:(c + 1) * 1024],
                                     ps_t[n % 2][:, :], ACT.Copy).then_inc(s_ev, 1)


def feed_forward_tiles(nc, at_scr, x1_scr, gnn_b, wgt, wut, wdt, ident, wsc, norm, yh, yl, out):
    with ExitStack() as ctx:
        def sb(name, shape, dt):
            return ctx.enter_context(nc.sbuf_tensor(name, shape, dt))

        def sem(name):
            return ctx.enter_context(nc.semaphore(name))

        bias = sb("f_bias", [TR, D], F32)
        a_raw = [sb(f"f_araw{s}", [TR, WPT, NT, WIN], F32) for s in range(2)]
        ah = [sb(f"f_ah{s}", [TR, NT, TR], F32R) for s in range(2)]
        al = [sb(f"f_al{s}", [TR, NT, TR], F32R) for s in range(2)]
        xin = [sb(f"f_xin{s}", [TR, D], F32) for s in range(2)]
        x1 = [sb(f"f_x1{s}", [TR, D], F32) for s in range(2)]
        z = sb("f_z", [TR, D], F32)
        xn = sb("f_xn", [TR, D], F32)
        q = sb("f_q", [TR, D], BF16)
        qt = sb("f_qt", [P, KD, P], BF16)
        gate = sb("f_gate", [TR, FI], F32)
        h = sb("f_h", [TR, FI], F32)
        hr = sb("f_hr", [TR, FI], F32)
        hq = sb("f_hq", [TR, FI], BF16)
        hqt = sb("f_hqt", [P, KI, P], BF16)
        o = [sb(f"f_out{s}", [TR, D], F32) for s in range(2)]
        eps = sb("f_eps", [TR, 1], F32)
        rnd = sb("f_round", [TR, 2], F32)
        bn = sb("f_bn", [TR, 2, 6], F32)
        mv = sb("f_mv", [TR, 2], F32)
        std = sb("f_std", [TR, 1], F32)
        lnw = sb("f_lnw", [TR, 4], F32)
        amax = [sb(f"f_amax{s}", [TR, 2], F32) for s in range(2)]
        dq = [sb(f"f_dq{s}", [TR, 2], F32) for s in range(2)]
        hmax = sb("f_hmax", [TR, 2], F32)
        dqh = sb("f_dqh", [TR, 1], F32)

        ps_a = [ctx.enter_context(nc.psum_tensor(f"f_psa{b}", [TR, 512], F32)) for b in range(2)]
        ps_q = ctx.enter_context(nc.psum_tensor("f_psq", [P, 1024], BF16))
        ps_h = ctx.enter_context(nc.psum_tensor("f_psh", [P, 1024], BF16))
        ps_g = ctx.enter_context(nc.psum_tensor("f_psg", [TR, 512], F32))
        ps_u = ctx.enter_context(nc.psum_tensor("f_psu", [TR, 512], F32))
        ps_d = [ctx.enter_context(nc.psum_tensor(f"f_psd{b}", [TR, 512], F32)) for b in range(2)]

        s_nb = sem("f_bias_loaded")
        s_a = [sem(f"f_a_loaded{s}") for s in range(2)]
        s_x = [sem(f"f_x_loaded{s}") for s in range(2)]
        s_st = [sem(f"f_stored{s}") for s in range(2)]
        s_c = sem("f_const")
        s_ah = sem("f_a_high")
        s_al = sem("f_a_low")
        s_agg = sem("f_edges_summed")
        s_ln = sem("f_ln")
        s_lna = sem("f_ln_scalar")
        s_qtp = sem("f_q_transposed")
        s_qt = sem("f_qt_ready")
        s_gu = sem("f_gate_up")
        s_hv = sem("f_h")
        s_ha = sem("f_h_scalar")
        s_htp = sem("f_h_transposed")
        s_ht = sem("f_ht_ready")
        s_dn = sem("f_down")
        s_o = sem("f_out_ready")
        block = ctx.enter_context(nc.Block())

        def tiles(eng, step):
            for n in range(2):
                step(n % 2, True, n > 0, False, n - 2)
            with eng.Fori(0, (NT - 2) // 2) as i:
                for s in range(2):
                    step(s, True, True, True, i * 2 + s)
            for n in range(NT, NT + 2):
                step(n % 2, False, n == NT, True, n - 2)

        @block.sync
        def _(sp):
            sp.dma_start(bias[:, :], gnn_b.rearrange("(a n) -> a n", a=1).broadcast_to([TR, D])).then_inc(s_nb, 16)

            def load_a(s, t):
                sp.dma_start(a_raw[s][:, :, :, :].rearrange("p w j d -> p w (j d)"),
                             at_scr[bass.ds(t * WPT, WPT), :, :].rearrange("w p n -> p w n")).then_inc(s_a[s], 16)

            def load_x(s, t):
                sp.dma_start(xin[s][:, :], x1_scr[bass.ds(t, 1), :, :].rearrange("a p n -> p (a n)")).then_inc(s_x[s], 16)

            for s in range(2):
                load_a(s, s)
                load_x(s, s)
            for s in range(2):
                sp.sem_inc(s_st[s], 16)

            def step(s, edges, gate_up, down, b):
                if edges:
                    nxt = (b + 4) % NT if isinstance(b, int) else sp.snap((b + 4) % NT)
                    sp.wait_ge(s_al, b + 3)
                    load_a(s, nxt)
                    sp.wait_ge(s_ln, b * LN_STEPS + 2 * LN_STEPS + 3)
                    load_x(s, nxt)
                if down:
                    sp.wait_ge(s_o, b * 2 + 2)
                    sp.dma_start(out[bass.ds(b * TR, TR), :], o[s][:, :]).then_inc(s_st[s], 16)

            tiles(sp, step)
            for s in range(2):
                sp.wait_ge(s_a[s], 16 * (NT // 2 + 1))
                sp.wait_ge(s_x[s], 16 * (NT // 2 + 1))
                sp.wait_ge(s_st[s], 16 * (NT // 2 + 1))

        @block.gpsimd
        def _(pool):
            nc.gpsimd.memset(eps[:, :], LN_EPS).then_inc(s_c, 1)
            nc.gpsimd.memset(rnd[:, 0:1], ROUND).then_inc(s_c, 1)
            nc.gpsimd.memset(rnd[:, 1:2], -ROUND).then_inc(s_c, 1)

        @block.scalar
        def _(act):
            def a_high(s, b, peeled):
                act.wait_ge(s_a[s], b * 8 + 32 - 8 * s)
                if not peeled:
                    act.wait_ge(s_agg, b * 2 + 2)
                nc.scalar.activation(ah[s][:, :, :].rearrange("p j (w d) -> p w j d", w=WPT),
                                     a_raw[s][:, :, :, :], ACT.Copy).then_inc(s_ah, 1)

            act.wait_ge(s_c, 3)
            a_high(0, -2, True)
            def step(s, edges, gate_up, down, b):
                if edges:
                    a_high(1 - s, b + 1, isinstance(b, int) and b < -1)
                if down:
                    act.wait_ge(s_hv, b * H_STEPS + 4)
                    nc.scalar.activation(hr[:, :], h[:, :], ACT.Identity, bias=rnd[:, 0:1],
                                         scale=hmax[:, 1:2]).then_inc(s_ha, 1)
                    act.wait_ge(s_hv, b * H_STEPS + 6)
                    nc.scalar.activation(hq[:, :], hr[:, :], ACT.Identity, bias=rnd[:, 1:2]).then_inc(s_ha, 1)
                    act.wait_ge(s_htp, b + 1)
                    nc.scalar.activation(hqt[:, :, 0:TR], ps_h[:, 0:KI * P].rearrange("p (k n) -> p k n", k=KI)[:, :, 0:TR],
                                         ACT.Copy).then_inc(s_ht, 1)
                if gate_up:
                    act.wait_ge(s_qtp, b + 2)
                    nc.scalar.activation(qt[:, :, 0:TR], ps_q[:, :].rearrange("p (k n) -> p k n", k=KD)[:, :, 0:TR],
                                         ACT.Copy).then_inc(s_qt, 1)
                if edges:
                    act.wait_ge(s_ln, b * LN_STEPS + 2 * LN_STEPS + 6)
                    nc.scalar.activation(std[:, :], mv[:, 1:2], ACT.Sqrt, bias=eps[:, 0:1]).then_inc(s_lna, 1)
                    act.wait_ge(s_ln, b * LN_STEPS + 2 * LN_STEPS + 12)
                    nc.scalar.activation(xn[:, :], x1[s][:, :], ACT.Identity, bias=lnw[:, 3:4],
                                         scale=lnw[:, 0:1]).then_inc(s_lna, 1)
                if gate_up:
                    act.wait_ge(s_gu, b + 2)
                    nc.scalar.activation(gate[:, :], ps_g[:, :], ACT.Silu, scale=dq[1 - s][:, 0:1]).then_inc(s_ha, 1)
                if edges:
                    act.wait_ge(s_ln, b * LN_STEPS + 2 * LN_STEPS + 15)
                    nc.scalar.activation(z[:, :], xn[:, :], ACT.Identity, bias=rnd[:, 0:1],
                                         scale=amax[s][:, 1:2]).then_inc(s_lna, 1)
                    act.wait_ge(s_ln, b * LN_STEPS + 2 * LN_STEPS + 17)
                    nc.scalar.activation(q[:, :], z[:, :], ACT.Identity, bias=rnd[:, 1:2]).then_inc(s_lna, 1)

            tiles(act, step)

        @block.vector
        def _(dve):
            def a_low(s, b):
                dve.wait_ge(s_ah, b + 3)
                view = "p j (w d) -> p w j d"
                nc.vector.tensor_tensor(al[s][:, :, :].rearrange(view, w=WPT), a_raw[s][:, :, :, :],
                                        ah[s][:, :, :].rearrange(view, w=WPT).bitcast(F32), ALU.subtract).then_inc(s_al, 1)

            dve.wait_ge(s_nb, 16)
            a_low(0, -2)
            def step(s, edges, gate_up, down, b):
                k = [0]
                kh = [0]

                def ln(ins):
                    k[0] += 1
                    ins.then_inc(s_ln, 1)
                    if k[0] not in (4, 5):
                        dve.wait_ge(s_ln, b * LN_STEPS + 2 * LN_STEPS + k[0])

                def hs(ins):
                    kh[0] += 1
                    ins.then_inc(s_hv, 1)
                    dve.wait_ge(s_hv, b * H_STEPS + H_STEPS + kh[0])

                def last_h(ins):
                    ins.then_inc(s_hv, 1)

                if edges:
                    a_low(1 - s, b + 1)
                if down:
                    dve.wait_ge(s_ha, b * 3 + 2)
                    last_h(nc.vector.tensor_scalar(hr[:, :], hr[:, :], ROUND + Q_MIN, ROUND + Q_MAX, ALU.max, ALU.min))
                if edges:
                    if not isinstance(b, int) or b >= -1:
                        dve.wait_ge(s_lna, b * 4 + 8)
                    for m in range(2):
                        dve.wait_ge(s_agg, b * 2 + 5 + m)
                        ln(nc.vector.scalar_tensor_tensor(
                            out=z[:, m * 512:(m + 1) * 512], in0=ps_a[m][:, :],
                            scalar=norm[:, b + 2, 1:2] if isinstance(b, int) else norm[:, bass.ds(b + 2, 1), 1],
                            in1=bias[:, m * 512:(m + 1) * 512], op0=ALU.mult, op1=ALU.add))
                if down:
                    dve.wait_ge(s_st[s], b * 8 + 16 - 8 * s)
                    for m in range(2):
                        dve.wait_ge(s_dn, b * 2 + 1 + m)
                        nc.vector.scalar_tensor_tensor(out=o[s][:, m * 512:(m + 1) * 512], in0=ps_d[m][:, :],
                                                       scalar=dqh[:, 0:1], in1=x1[s][:, m * 512:(m + 1) * 512],
                                                       op0=ALU.mult, op1=ALU.add).then_inc(s_o, 1)
                    if edges or gate_up:
                        dve.wait_ge(s_o, b * 2 + 2)
                if edges:
                    dve.wait_ge(s_x[s], b * 8 + 32 - 8 * s)
                    ln(nc.vector.scalar_tensor_tensor(out=x1[s][:, :], in0=z[:, :], scalar=0.0, in1=xin[s][:, :],
                                                      op0=ALU.max, op1=ALU.add))
                    for m in range(2):
                        ln(nc.vector.bn_stats(bn[:, m, :], x1[s][:, m * 512:(m + 1) * 512]))
                    dve.drain()
                    ln(nc.vector.bn_aggr(mv[:, :], bn[:, :, :].rearrange("p a b -> p (a b)")))
                    dve.wait_ge(s_lna, b * 4 + 9)
                    ln(nc.vector.reciprocal(lnw[:, 0:1], std[:, :]))
                    ln(nc.vector.tensor_tensor(lnw[:, 1:2], lnw[:, 0:1], lnw[:, 0:1], ALU.mult))
                    ln(nc.vector.scalar_tensor_tensor(out=lnw[:, 1:2], in0=mv[:, 1:2], scalar=LN_EPS,
                                                      in1=lnw[:, 1:2], op0=ALU.add, op1=ALU.mult))
                    ln(nc.vector.tensor_scalar(lnw[:, 1:2], lnw[:, 1:2], -0.5, 1.5, ALU.mult, ALU.add))
                    ln(nc.vector.tensor_tensor(lnw[:, 0:1], lnw[:, 0:1], lnw[:, 1:2], ALU.mult))
                    ln(nc.vector.scalar_tensor_tensor(out=lnw[:, 3:4], in0=mv[:, 0:1], scalar=-1.0,
                                                      in1=lnw[:, 0:1], op0=ALU.mult, op1=ALU.mult))
                    dve.wait_ge(s_lna, b * 4 + 10)
                    ln(nc.vector.tensor_reduce(amax[s][:, 0:1], xn[:, :], axis=AX.X, op=ALU.max,
                                               apply_absolute_value=True))
                    ln(nc.vector.tensor_scalar(amax[s][:, 0:1], amax[s][:, 0:1], Q_EPS, 1.0 / Q_MAX, ALU.max, ALU.mult))
                    ln(nc.vector.reciprocal(amax[s][:, 1:2], amax[s][:, 0:1]))
                    ln(nc.vector.tensor_scalar(dq[s][:, :], wsc[0:TR, 0:2], amax[s][:, 0:1], None, ALU.mult))
                if gate_up:
                    dve.wait_ge(s_ha, b * 3 + 4)
                    hs(nc.vector.scalar_tensor_tensor(out=h[:, :], in0=ps_u[:, :], scalar=dq[1 - s][:, 1:2],
                                                      in1=gate[:, :], op0=ALU.mult, op1=ALU.mult))
                    hs(nc.vector.tensor_reduce(hmax[:, 0:1], h[:, :], axis=AX.X, op=ALU.max,
                                               apply_absolute_value=True))
                    hs(nc.vector.tensor_scalar(hmax[:, 0:1], hmax[:, 0:1], Q_EPS, 1.0 / Q_MAX, ALU.max, ALU.mult))
                    hs(nc.vector.reciprocal(hmax[:, 1:2], hmax[:, 0:1]))
                    hs(nc.vector.tensor_scalar(dqh[:, 0:1], hmax[:, 0:1], wsc[0:TR, 2:3], None, ALU.mult))
                if edges:
                    dve.wait_ge(s_lna, b * 4 + 11)
                    ln(nc.vector.tensor_scalar(z[:, :], z[:, :], ROUND + Q_MIN, ROUND + Q_MAX, ALU.max, ALU.min))
                    assert k[0] == LN_STEPS
                if gate_up:
                    assert kh[0] == H_STEPS - 1

            tiles(dve, step)

        @block.tensor
        def _(pe):
            def edge_sums(s, b, m, peeled):
                if m == 0:
                    pe.wait_ge(s_al, b + 3)
                if not peeled:
                    pe.wait_ge(s_ln, b * LN_STEPS + LN_STEPS + 1 + m)
                for a, (pa, py) in enumerate(((ah, yh), (ah, yl), (al, yh))):
                    for j in range(NT):
                        ins = nc.tensor.matmul(ps_a[m][:, :], pa[s][:, j, :], py[:, j, m * 512:(m + 1) * 512],
                                               start=(a == 0 and j == 0), stop=(a == 2 and j == NT - 1))
                ins.then_inc(s_agg, 1)

            def step(s, edges, gate_up, down, b):
                peeled = isinstance(b, int) and b < -1
                if edges:
                    edge_sums(s, b, 0, peeled)
                    edge_sums(s, b, 1, peeled)
                if down:
                    pe.wait_ge(s_ha, b * 3 + 3)
                    for k in range(KI):
                        ins = nc.tensor.transpose(ps_h[:, k * P:k * P + TR], hq[:, k * P:(k + 1) * P],
                                                  ident[0:TR, 0:TR])
                    ins.then_inc(s_htp, 1)
                    pe.wait_ge(s_ht, b + 1)
                    if not isinstance(b, int) or b >= 1:
                        pe.wait_ge(s_o, b * 2)
                    for m in range(2):
                        for k in range(KI):
                            ins = nc.tensor.matmul(ps_d[m][:, :], hqt[:, k, 0:TR], wdt[:, k, m * 512:(m + 1) * 512],
                                                   start=(k == 0), stop=(k == KI - 1))
                        ins.then_inc(s_dn, 1)
                if gate_up:
                    pe.wait_ge(s_lna, b * 4 + 8)
                    for k in range(KD):
                        ins = nc.tensor.transpose(ps_q[:, k * P:k * P + TR], q[:, k * P:(k + 1) * P],
                                                  ident[0:TR, 0:TR])
                    ins.then_inc(s_qtp, 1)
                    pe.wait_ge(s_qt, b + 2)
                    if down:
                        pe.wait_ge(s_hv, b * H_STEPS + 1)
                    for w, ps in ((wgt, ps_g), (wut, ps_u)):
                        for k in range(KD):
                            ins = nc.tensor.matmul(ps[:, :], qt[:, k, 0:TR], w[:, k, :], start=(k == 0), stop=(k == KD - 1))
                    ins.then_inc(s_gu, 1)

            tiles(pe, step)


_INS = ("x", "src", "dst", "edge_weight", "L0_gnn_W", "L0_gnn_b", "L0_mix_wq", "L0_mix_wk", "L0_mix_wv", "L0_mix_wo",
        "L0_mix_rf", "L0_ffn_w_gate", "L0_ffn_w_up", "L0_ffn_w_down")


def graph_layer(nc, x, src, dst, edge_weight, gnn_w, gnn_b, wq, wk, wv, wo, rf, w_gate, w_up, w_down, out):
    def scratch(name, shape):
        return nc.dram_tensor(name, shape, F32, kind="Internal").ap()

    y_scr = scratch("y_scr", (NT, TR, D))
    xt_scr = scratch("xt_scr", (NT, P, 2 * KD * TR))
    at_scr = scratch("at_scr", (NW, TR, NT * WIN))
    edge_scr = scratch("edge_scr", (TR, 3, NC))
    o_scr = scratch("o_scr", (KD, P, N))
    x1_scr = scratch("x1_scr", (NT, TR, D))
    norm_scr = scratch("norm_scr", (TR, NT, 2))
    node_stage(nc, x, src, dst, edge_weight, gnn_w, y_scr, xt_scr, at_scr, edge_scr)
    attention_stage(nc, xt_scr, wq, wk, wv, rf, o_scr)
    output_stage(nc, o_scr, wo, x, edge_scr, x1_scr, norm_scr)
    feed_forward_stage(nc, y_scr, at_scr, norm_scr, x1_scr, gnn_b, w_gate, w_up, w_down, out)


def kernel(**inputs):
    import numpy as _np
    import concourse.bacc as _bacc
    from concourse import mybir as _mybir
    from concourse.bass_utils import run_bass_kernel_spmd as _run

    nc = _bacc.Bacc("TRN2", target_bir_lowering=False, num_devices=1)
    arrays, args = {}, []
    for name in _INS:
        a = _np.ascontiguousarray(inputs[name])
        arrays[f"in_{name}_dram"] = a
        args.append(nc.dram_tensor(f"in_{name}_dram", a.shape, _mybir.dt.from_np(a.dtype), kind="ExternalInput").ap())
    args.append(nc.dram_tensor("out_0_dram", (N, D), F32, kind="ExternalOutput").ap())
    graph_layer(nc, *args)
    r = _run(nc, [arrays], core_ids=[0])
    return r.results[0]["out_0_dram"]
```

```python
import concourse.bass as bass
from concourse import mybir
from contextlib import ExitStack
import numpy as np

F32 = mybir.dt.float32
F32R = mybir.dt.float32r
BF16 = mybir.dt.bfloat16
I32 = mybir.dt.int32
I16 = mybir.dt.int16
ACT = mybir.ActivationFunctionType
ALU = mybir.AluOpType
AX = mybir.AxisListType

N = 1250
D = 1024
E = 20000
P = 128
TR = 125
NT = N // TR
KD = D // P
NC = E // TR
CR = NC // 2
WIN = 25
NW = N // WIN
NWT = NW + 1
WPT = TR // WIN
PARTS = 3
OHW = (NT - 1) * TR + P
PREP_STEPS = 34
VC = 4
NCP = NC + VC
ROUND = 1.5 * 2.0 ** 23
RANGE_BITS = 8
RANGE = 2 ** RANGE_BITS
RANGE_WORDS = 2 ** 30
LN_EPS = 1e-5


def node_stage(nc, x, src, dst, edge_weight, gnn_w, y_scr, xt_scr, at_scr, edge_scr):
    with ExitStack() as ctx:
        def sb(name, shape, dt):
            return ctx.enter_context(nc.sbuf_tensor(name, shape, dt))

        def pb(name, shape, dt=F32):
            return ctx.enter_context(nc.psum_tensor(name, shape, dt))

        def sem(name):
            return ctx.enter_context(nc.semaphore(name))

        ident = sb("n_ident", [P, P], F32)
        xin = [sb(f"n_xin{s}", [TR, D], F32) for s in range(2)]
        xn = [sb(f"n_xn{s}", [TR, D], F32) for s in range(2)]
        xt = [sb(f"n_xt{s}", [P, 2, KD, TR], F32R) for s in range(2)]
        xraw = [sb(f"n_xraw{s}", [P, KD, TR], F32) for s in range(2)]
        w_raw = [sb(f"n_wraw{s}", [P, D], F32) for s in range(2)]
        w_hi = sb("n_whi", [P, KD, D], F32R)
        w_lo = sb("n_wlo", [P, KD, D], F32R)
        ysb = [sb(f"n_y{s}", [TR, D], F32) for s in range(2)]
        bn = [sb(f"n_bn{s}", [TR, 2, 6], F32) for s in range(2)]
        mv = [sb(f"n_mv{s}", [TR, 2], F32) for s in range(2)]
        std = [sb(f"n_std{s}", [TR, 1], F32) for s in range(2)]
        rstd = [sb(f"n_rstd{s}", [TR, 1], F32) for s in range(2)]
        nmr = [sb(f"n_nmr{s}", [TR, 1], F32) for s in range(2)]
        eps = sb("n_eps", [TR, 1], F32)
        src_r = sb("n_srcr", [CR, 2, TR], I32)
        dst_r = sb("n_dstr", [CR, 2, TR], I32)
        w_r = sb("n_wr", [CR, 2, TR], F32)
        src_f = sb("n_srcf", [CR, 2, TR], F32)
        dst_f = sb("n_dstf", [CR, 2, TR], F32)
        dmm = sb("n_dmm", [CR, 2, 2], F32)
        dmm_b = sb("n_dmmb", [CR, 2, 2, NWT], F32)
        edge_t = sb("n_edget", [TR, 3, NCP], F32)
        wrest = sb("n_wrest", [TR, 2, NCP], F32)
        wpart = sb("n_wpart", [TR, NCP, PARTS], BF16)
        wfirst = [sb(f"n_wfirst{s}", [TR, 1], F32) for s in range(2)]
        iota_s = sb("n_iotas", [TR, OHW + 3], I16)
        iota_d = sb("n_iotad", [TR, PARTS, WIN], I16)
        nodes = [sb(f"n_nodes{s}", [TR, PARTS, WIN], F32) for s in range(2)]
        oh_s = [sb(f"n_ohs{par}", [TR, VC, OHW + 3], BF16) for par in range(2)]
        oh_d = [sb(f"n_ohd{par}", [TR, VC, PARTS * WIN], BF16) for par in range(2)]
        zero = sb("n_zero", [1, P], BF16)
        sums = [sb(f"n_sums{s}", [TR, NT, PARTS, WIN], F32) for s in range(2)]
        at = [sb(f"n_at{s}", [TR, NT, WIN], F32) for s in range(2)]
        wlo = sb("n_wlo_v", [NWT, 2], F32)
        iota_w = sb("n_iotaw", [NWT, 2], I32)
        cnum = sb("n_cnum", [NWT, 2, NC], F32)
        cnum_i = sb("n_cnumi", [NWT, 2, NC], I32)
        inwin = sb("n_inwin", [NWT, NC], F32)
        cand = sb("n_cand", [NWT, 2, NC], F32)
        rng = sb("n_rng", [NWT, 4], F32)
        tri = sb("n_tri", [NWT, NWT], F32)
        even_i = sb("n_eveni", [NWT, NWT], I32)
        even = sb("n_even", [NWT, NWT], F32)
        table4 = sb("n_table4", [1, 4 * NWT], I32)
        table = sb("n_table", [1, NWT], I32)
        wbase_i = sb("n_wbasei", [TR, NWT + 1], I32)
        wbase = sb("n_wbase", [TR, NWT + 1], F32)

        ps_t = [pb(f"n_pst{s}", [P, 512]) for s in range(2)]
        ps_y = [pb(f"n_psy{s}", [TR, 512]) for s in range(2)]
        ps_a = [[pb(f"n_psa{s}{b}", [P, 512]) for b in range(2)] for s in range(2)]

        s_edge = sem("n_edge_loaded")
        s_x = [sem(f"n_x_loaded{s}") for s in range(2)]
        s_w = [sem(f"n_w_loaded{s}") for s in range(2)]
        s_ident = sem("n_const")
        s_split = sem("n_w_high")
        s_wlow = [sem("n_w_low_first"), sem("n_w_low_second")]
        s_prep = sem("n_prep")
        s_prep_pe = sem("n_prep_pe")
        s_stat = sem("n_stat")
        s_std = sem("n_std")
        s_xn = sem("n_xn")
        s_tp = sem("n_transposed")
        s_hi = sem("n_xt_high")
        s_lo = sem("n_xt_low")
        s_yp = sem("n_y_product")
        s_ye = sem("n_y_evacuated")
        s_ys = [sem(f"n_y_stored{s}") for s in range(2)]
        s_xr = sem("n_xt_copied")
        s_xs = [sem(f"n_xt_stored{s}") for s in range(2)]
        s_ohr = [sem(f"n_onehot_ready{par}") for par in range(2)]
        s_nodes = sem("n_window_nodes")
        s_ohu = [sem(f"n_onehot_used{par}") for par in range(2)]
        s_wr = sem("n_window_ready")
        s_we = sem("n_window_evacuated")
        s_at = sem("n_window_parts_added")
        s_as = [sem(f"n_window_stored{s}") for s in range(2)]

        def window_range(eng, w):
            word = eng.value_load(table[0:1, bass.ds(w, 1)], min_val=0, max_val=RANGE_WORDS - 1)
            return (eng.snap(word % RANGE % NC), eng.snap(word // RANGE % RANGE), eng.snap(word // (RANGE * RANGE)))

        PS = 5
        block = ctx.enter_context(nc.Block())

        @block.sync
        def _(sp):
            half = "(t r e) -> r t e"
            sp.dma_start(src_r[:, :, :], src.rearrange(half, t=2, r=CR)).then_inc(s_edge, 16)
            sp.dma_start(dst_r[:, :, :], dst.rearrange(half, t=2, r=CR)).then_inc(s_edge, 16)
            sp.dma_start(w_r[:, :, :], edge_weight.rearrange(half, t=2, r=CR)).then_inc(s_edge, 16)
            for s in range(2):
                sp.dma_start(xin[s][:, :], x[s * TR:(s + 1) * TR, :]).then_inc(s_x[s], 16)
            for k in range(KD):
                if k >= 2:
                    sp.wait_ge(s_wlow[(k - 2) // (KD // 2)], (k - 2) % (KD // 2) + 1)
                sp.dma_start(w_raw[k % 2][:, :], gnn_w[k * P:(k + 1) * P, :]).then_inc(s_w[k % 2], 16)
            for s in range(2):
                sp.sem_inc(s_as[s], 16)
                sp.sem_inc(s_ys[s], 16)
                sp.sem_inc(s_xs[s], 16)
            sp.wait_ge(s_prep, 9)
            sp.dma_start(edge_scr, edge_t[:, :, 0:NC]).then_inc(s_edge, 16)
            with sp.Fori(0, NT // 2) as i:
                for s in range(2):
                    sp.wait_ge(s_xr, (i * 2 + s) * 2 + 4)
                    sp.dma_start(xt_scr[bass.ds(i * 2 + s, 1), :, :].rearrange("a p n -> p (a n)"),
                                 xraw[s][:, :, :].rearrange("p k n -> p (k n)")).then_inc(s_xs[s], 16)
                    nxt = sp.snap((i * 2 + s + 2) % NT)
                    sp.wait_ge(s_xn, i * 2 + s + 1)
                    sp.dma_start(xin[s][:, :], x[bass.ds(nxt * TR, TR), :]).then_inc(s_x[s], 16)
                    for q in range(WPT):
                        w = (i * 2 + s) * WPT + q
                        sp.wait_ge(s_at, w + 3)
                        sp.dma_start(at_scr[bass.ds(w, 1), :, :].rearrange("a p n -> p (a n)"),
                                     at[(s * WPT + q) % 2][:, :, :].rearrange("p j d -> p (j d)")
                                     ).then_inc(s_as[(s * WPT + q) % 2], 16)
                    sp.wait_ge(s_ye, (i * 2 + s + 1) * 2 + 2)
                    sp.dma_start(y_scr[bass.ds(i * 2 + s, 1), :, :].rearrange("a p n -> p (a n)"),
                                 ysb[s][:, :]).then_inc(s_ys[s], 16)
            sp.wait_ge(s_x[0], (NT // 2 + 1) * 16)
            sp.wait_ge(s_x[1], (NT // 2 + 1) * 16)
            for s in range(2):
                sp.wait_ge(s_xs[s], (NT // 2 + 1) * 16)
                sp.wait_ge(s_as[s], (NW // 2 + 1) * 16)
                sp.wait_ge(s_ys[s], (NT // 2 + 1) * 16)
            sp.wait_ge(s_edge, 64)

        @block.gpsimd
        def _(pool):
            nc.gpsimd.memset(ident[:, :], 0.0).then_inc(s_ident, 1)
            nc.gpsimd.memset(tri[:, :], 0.0).then_inc(s_ident, 1)
            nc.gpsimd.memset(zero[:, :], 0.0).then_inc(s_ident, 1)
            nc.gpsimd.memset(eps[:, :], LN_EPS).then_inc(s_ident, 1)
            nc.gpsimd.iota(iota_s[:, :], pattern=[[1, OHW + 3]], base=0, channel_multiplier=0).then_inc(s_ident, 1)
            nc.gpsimd.iota(iota_d[:, :, :], pattern=[[0, PARTS], [1, WIN]], base=0,
                           channel_multiplier=0).then_inc(s_ident, 1)
            nc.gpsimd.iota(iota_w[:, :], pattern=[[WIN, 2]], base=0, channel_multiplier=WIN).then_inc(s_ident, 1)
            nc.gpsimd.iota(cnum_i[:, 0, :], pattern=[[1, NC]], base=1, channel_multiplier=0).then_inc(s_ident, 1)
            nc.gpsimd.iota(cnum_i[:, 1, :], pattern=[[-1, NC]], base=NC, channel_multiplier=0).then_inc(s_ident, 1)
            nc.gpsimd.iota(wbase_i[:, :], pattern=[[WIN, NWT + 1]], base=0, channel_multiplier=0).then_inc(s_ident, 1)
            nc.gpsimd.memset(edge_t[:, :, NC:NCP], -1.0).then_inc(s_ident, 1)
            nc.gpsimd.iota(even_i[:, :], pattern=[[1, NWT]], base=2 * (NWT // 2) + 3, channel_multiplier=-1
                           ).then_inc(s_ident, 1)
            pool.wait_ge(s_ident, 12)
            nc.gpsimd.affine_select(out=ident[:, :], in_=ident[:, :], compare_op=ALU.not_equal, fill=1.0,
                                    base=0, pattern=[[-1, P]], channel_multiplier=1).then_inc(s_ident, 1)
            nc.gpsimd.affine_select(out=tri[:, :], in_=tri[:, :], compare_op=ALU.is_ge, fill=1.0,
                                    base=0, pattern=[[-1, NWT]], channel_multiplier=1).then_inc(s_ident, 1)

            for k in range(KD // 2):
                pool.wait_ge(s_split, k + 1)
                nc.gpsimd.tensor_tensor(w_lo[:, k, :], w_raw[k % 2][:, :], w_hi[:, k, :].bitcast(F32),
                                        ALU.subtract).then_inc(s_wlow[0], 1)
            pool.wait_ge(s_prep, PREP_STEPS)

            def window_nodes(par, w):
                nc.gpsimd.tensor_copy(wfirst[par][:, :], wbase[:, bass.ds(w, 1)])
                pool.drain()
                nc.gpsimd.tensor_scalar(nodes[par][:, :, :], iota_d[:, :, :], wfirst[par][:, 0:1], None,
                                        ALU.add).then_inc(s_nodes, 1)

            for w in range(2):
                window_nodes(w, w)
            with pool.Fori(0, NW // 2) as i:
                for par in range(2):
                    w = i * 2 + par
                    pool.wait_ge(s_we, w + 3)
                    window_nodes(par, w + 2)
                    pool.wait_ge(s_as[par], i * 16 + 16)
                    nc.gpsimd.tensor_tensor(at[par][:, :, :], sums[par][:, :, 2, :], sums[par][:, :, 1, :], ALU.add)
                    pool.drain()
                    nc.gpsimd.tensor_tensor(at[par][:, :, :], at[par][:, :, :], sums[par][:, :, 0, :], ALU.add
                                            ).then_inc(s_at, 1)

        @block.scalar
        def _(act):
            def normalise(s, count):
                act.wait_ge(s_stat, count * PS + 3)
                nc.scalar.activation(std[s][:, :], mv[s][:, 1:2], ACT.Sqrt, bias=eps[:, 0:1]).then_inc(s_std, 1)
                act.wait_ge(s_stat, count * PS + 5)
                nc.scalar.activation(xn[s][:, :], xin[s][:, :], ACT.Identity, bias=nmr[s][:, 0:1],
                                     scale=rstd[s][:, 0:1]).then_inc(s_xn, 1)

            act.wait_ge(s_ident, 14)
            normalise(0, 0)
            for k in range(KD):
                act.wait_ge(s_w[k % 2], (k // 2 + 1) * 16)
                nc.scalar.activation(w_hi[:, k, :], w_raw[k % 2][:, :], ACT.Copy).then_inc(s_split, 1)
            with act.Fori(0, NT // 2) as i:
                for s in range(2):
                    t = i * 2 + s
                    act.wait_ge(s_xs[s], (i + 1) * 16)
                    for b in range(2):
                        act.wait_ge(s_tp, t * 2 + b + 1)
                        nc.scalar.activation(
                            xt[s][:, 0, 4 * b:4 * b + 4, :],
                            ps_t[b][:, 0:4 * TR].rearrange("p (k n) -> p k n", k=4), ACT.Copy).then_inc(s_hi, 1)
                        nc.scalar.activation(
                            xraw[s][:, 4 * b:4 * b + 4, :],
                            ps_t[b][:, 0:4 * TR].rearrange("p (k n) -> p k n", k=4), ACT.Copy).then_inc(s_xr, 1)
                    act.wait_ge(s_ys[s], (i + 1) * 16)
                    for q in range(WPT):
                        par = (s * WPT + q) % 2
                        act.wait_ge(s_at, t * WPT + q + 1)
                        act.wait_ge(s_wr, t * WPT + q + 1)
                        for b in range(2):
                            ins = nc.scalar.activation(
                                sums[par][:, 5 * b:5 * b + 5, :, :].rearrange("p j m d -> p (j m d)"),
                                ps_a[par][b][0:TR, 0:5 * PARTS * WIN], ACT.Copy)
                        ins.then_inc(s_we, 1)
                        if q == 0:
                            normalise(1 - s, t + 1)
                        if q == 3:
                            act.wait_ge(s_yp, t * 2 + 1)
                            nc.scalar.activation(ysb[s][:, 0:512], ps_y[0][:, :], ACT.Copy).then_inc(s_ye, 1)
                    act.wait_ge(s_yp, t * 2 + 2)
                    nc.scalar.activation(ysb[s][:, 512:1024], ps_y[1][:, :], ACT.Copy).then_inc(s_ye, 1)

        @block.vector
        def _(dve):
            prep = [0]

            def step(ins):
                prep[0] += 1
                ins.then_inc(s_prep, 1)
                dve.wait_ge(s_prep, prep[0])

            def statistics(s, count, loaded):
                dve.wait_ge(s_x[s], loaded)
                nc.vector.bn_stats(bn[s][:, 0, :], xin[s][:, 0:512]).then_inc(s_stat, 1)
                nc.vector.bn_stats(bn[s][:, 1, :], xin[s][:, 512:1024]).then_inc(s_stat, 1)
                dve.drain()
                nc.vector.bn_aggr(mv[s][:, :], bn[s][:, :, :].rearrange("p a b -> p (a b)")).then_inc(s_stat, 1)
                dve.wait_ge(s_std, count + 1)
                nc.vector.reciprocal(rstd[s][:, :], std[s][:, :]).then_inc(s_stat, 1)
                dve.wait_ge(s_stat, count * PS + 4)
                nc.vector.scalar_tensor_tensor(out=nmr[s][:, :], in0=mv[s][:, 0:1], scalar=-1.0,
                                               in1=rstd[s][:, :], op0=ALU.mult, op1=ALU.mult).then_inc(s_stat, 1)

            statistics(0, 0, 16)
            dve.wait_ge(s_edge, 48)
            step(nc.vector.tensor_copy(src_f[:, :, :], src_r[:, :, :]))
            step(nc.vector.tensor_copy(dst_f[:, :, :], dst_r[:, :, :]))
            step(nc.vector.tensor_reduce(dmm[:, :, 0:1], dst_f[:, :, :], axis=AX.X, op=ALU.min))
            step(nc.vector.tensor_reduce(dmm[:, :, 1:2], dst_f[:, :, :], axis=AX.X, op=ALU.max))
            step(nc.vector.tensor_copy(dmm_b[:, :, :, :],
                                       dmm[:, :, :].unsqueeze(3).broadcast_to([CR, 2, 2, NWT])))
            dve.wait_ge(s_ident, 14)
            step(nc.vector.tensor_copy(wlo[:, :], iota_w[:, :]))
            step(nc.vector.tensor_copy(cnum[:, :, :], cnum_i[:, :, :]))
            step(nc.vector.tensor_copy(wbase[:, :], wbase_i[:, :]))
            dve.wait_ge(s_prep_pe, 1)
            step(nc.vector.tensor_copy(edge_t[:, :, 0:NC], ps_t[0][0:TR, 0:3 * NC].rearrange(
                "p (a c) -> p a c", a=3)))
            step(nc.vector.tensor_copy(wpart[:, :, 0], edge_t[:, 2, :]))
            step(nc.vector.tensor_tensor(wrest[:, 0, :], edge_t[:, 2, :], wpart[:, :, 0], ALU.subtract))
            step(nc.vector.tensor_copy(wpart[:, :, 1], wrest[:, 0, :]))
            step(nc.vector.tensor_tensor(wrest[:, 1, :], wrest[:, 0, :], wpart[:, :, 1], ALU.subtract))
            step(nc.vector.tensor_copy(wpart[:, :, 2], wrest[:, 1, :]))
            step(nc.vector.tensor_scalar(even_i[:, :], even_i[:, :], 1, None, ALU.bitwise_and))
            step(nc.vector.tensor_copy(even[:, :], even_i[:, :]))
            step(nc.vector.tensor_tensor(tri[:, :], tri[:, :], even[:, :], ALU.mult))
            dve.wait_ge(s_prep_pe, 2)
            lows = ps_t[1][0:NWT, 0:2 * NC].rearrange("v (m c) -> v m c", m=2)
            step(nc.vector.tensor_scalar(inwin[:, :], lows[:, 0, :], wlo[:, 1:2], None, ALU.is_lt))
            step(nc.vector.scalar_tensor_tensor(out=inwin[:, :], in0=lows[:, 1, :], scalar=wlo[:, 0:1],
                                                in1=inwin[:, :], op0=ALU.is_ge, op1=ALU.mult))
            step(nc.vector.tensor_tensor(cand[:, :, :], cnum[:, :, :],
                                         inwin[:, :].unsqueeze(1).broadcast_to([NWT, 2, NC]), ALU.mult))
            step(nc.vector.tensor_reduce(rng[:, 0:2], cand[:, :, :], axis=AX.X, op=ALU.max))
            step(nc.vector.tensor_scalar(rng[:, 2:3], rng[:, 1:2], -1.0, float(NC), ALU.mult, ALU.add))
            step(nc.vector.tensor_tensor(rng[:, 3:4], rng[:, 0:1], rng[:, 2:3], ALU.subtract))
            step(nc.vector.tensor_scalar(rng[:, 3:4], rng[:, 3:4], 1.0 / VC, 0.5 - 0.5 / VC, ALU.mult, ALU.add))
            step(nc.vector.tensor_scalar(rng[:, 3:4], rng[:, 3:4], ROUND, ROUND, ALU.add, ALU.subtract))
            step(nc.vector.tensor_scalar(rng[:, 3:4], rng[:, 3:4], 1.0, None, ALU.max))
            step(nc.vector.tensor_copy(rng[:, 1:2], rng[:, 3:4]))
            step(nc.vector.tensor_scalar(rng[:, 0:1], rng[:, 2:3], float(NC - 1), None, ALU.min))
            dve.wait_ge(s_prep_pe, 3)
            step(nc.vector.tensor_copy(rng[:, 2:3], ps_y[0][0:NWT, 0:1]))
            dve.wait_ge(s_prep_pe, 4)
            step(nc.vector.tensor_copy(table4[:, :], ps_y[1][0:1, 0:4 * NWT]))
            step(nc.vector.tensor_scalar(table4[:, NWT:2 * NWT], table4[:, NWT:2 * NWT], RANGE_BITS, None,
                                         ALU.logical_shift_left))
            step(nc.vector.tensor_scalar(table4[:, 2 * NWT:3 * NWT], table4[:, 2 * NWT:3 * NWT], 2 * RANGE_BITS, None,
                                         ALU.logical_shift_left))
            step(nc.vector.tensor_tensor(table[:, :], table4[:, NWT:2 * NWT], table4[:, 0:NWT], ALU.bitwise_or))
            step(nc.vector.tensor_tensor(table[:, :], table4[:, 2 * NWT:3 * NWT], table[:, :], ALU.bitwise_or))
            assert prep[0] == PREP_STEPS

            def build(par, w):
                first, visits, before = window_range(dve, w)
                with dve.Fori(0, visits) as v:
                    done = dve.snap((before + v) * VC)
                    for h in range(VC):
                        c = dve.snap((first + v * VC) % NC + h) if h else dve.snap((first + v * VC) % NC)
                        dve.wait_ge(s_ohu[par], done + h + 1)
                        nc.vector.tensor_scalar(oh_s[par][:, h, :], iota_s[:, :], edge_t[:, 0, bass.ds(c, 1)],
                                                None, ALU.is_equal)
                        dve.wait_ge(s_nodes, w + 1)
                        nc.vector.scalar_tensor_tensor(
                            out=oh_d[par][:, h, :].rearrange("p (m d) -> p m d", m=PARTS),
                            in0=nodes[par][:, :, :], scalar=edge_t[:, 1, bass.ds(c, 1)],
                            in1=wpart[:, bass.ds(c, 1), :].rearrange("p a m -> p (a m)").unsqueeze(2)
                            .broadcast_to([TR, PARTS, WIN]),
                            op0=ALU.is_equal, op1=ALU.mult).then_inc(s_ohr[par], 1)

            build(0, 0)
            for k in range(KD // 2, KD):
                dve.wait_ge(s_split, k + 1)
                nc.vector.tensor_tensor(w_lo[:, k, :], w_raw[k % 2][:, :], w_hi[:, k, :].bitcast(F32),
                                        ALU.subtract).then_inc(s_wlow[1], 1)
            with dve.Fori(0, NT // 2) as i:
                for s in range(2):
                    t = i * 2 + s
                    for b in range(2):
                        dve.wait_ge(s_hi, t * 2 + b + 1)
                        dve.wait_ge(s_xr, t * 2 + b + 3)
                        nc.vector.tensor_tensor(
                            xt[s][:, 1, 4 * b:4 * b + 4, :],
                            ps_t[b][:, 0:4 * TR].rearrange("p (k n) -> p k n", k=4),
                            xt[s][:, 0, 4 * b:4 * b + 4, :].bitcast(F32), ALU.subtract
                        ).then_inc(s_lo, 1)
                    statistics(1 - s, t + 1, (i + 1 + s) * 16)
                    for q in range(WPT):
                        build((s * WPT + q + 1) % 2, dve.snap(t * WPT + q + 1))

        @block.tensor
        def _(pe):
            pe.wait_ge(s_ident, 14)
            pe.wait_ge(s_prep, 2)
            for a, rows in enumerate((src_f, dst_f, w_r)):
                for h in range(2):
                    ins = nc.tensor.transpose(ps_t[0][0:TR, a * NC + h * CR:a * NC + (h + 1) * CR],
                                              rows[:, h, :], ident[0:CR, 0:CR])
            ins.then_inc(s_prep_pe, 1)
            pe.wait_ge(s_prep, 5)
            for m in range(2):
                for h in range(2):
                    ins = nc.tensor.matmul(ps_t[1][0:NWT, m * NC + h * CR:m * NC + (h + 1) * CR],
                                           dmm_b[:, h, m, :], ident[0:CR, 0:CR], start=True, stop=True)
            ins.then_inc(s_prep_pe, 1)
            pe.wait_ge(s_prep, PREP_STEPS - 8)
            nc.tensor.matmul(ps_y[0][0:NWT, 0:1], tri[:, :], rng[:, 3:4], start=True, stop=True).then_inc(s_prep_pe, 1)
            pe.wait_ge(s_prep, PREP_STEPS - 5)
            for q in range(4):
                ins = nc.tensor.matmul(ps_y[1][0:1, q * NWT:(q + 1) * NWT], rng[:, q:q + 1], ident[0:NWT, 0:NWT],
                                       start=True, stop=True)
            ins.then_inc(s_prep_pe, 1)
            pe.wait_ge(s_prep, PREP_STEPS)
            for par in range(2):
                pe.sem_inc(s_ohu[par], VC)
            pe.sem_inc(s_we, 2)
            pe.sem_inc(s_at, 2)
            pe.sem_inc(s_ye, 2)
            pe.sem_inc(s_lo, 2)
            pe.sem_inc(s_xr, 2)

            PIECES = 2 * 3 * KD

            def product(s, t, lo, hi):
                for n in range(lo, hi):
                    b, m, k = n // (3 * KD), n // KD % 3, n % KD
                    part, w = ((0, w_hi), (0, w_lo), (1, w_hi))[m]
                    if n == 0:
                        pe.wait_ge(s_wlow[0], KD // 2)
                        pe.wait_ge(s_wlow[1], KD // 2)
                    if n % (3 * KD) == 0:
                        pe.wait_ge(s_ye, t * 2 + b + 1)
                    ins = nc.tensor.matmul(ps_y[b][:, :], xt[s][:, part, k, :], w[:, k, b * 512:(b + 1) * 512],
                                           start=(m == 0 and k == 0), stop=(m == 2 and k == KD - 1))
                    if n % (3 * KD) == 3 * KD - 1:
                        ins.then_inc(s_yp, 1)

            def window(t, s, q):
                w = pe.snap(t * WPT + q)
                par = (s * WPT + q) % 2
                _, visits, before = window_range(pe, w)
                pe.wait_ge(s_we, w + 1)
                for b in range(2):
                    nc.tensor.matmul(ps_a[par][b][:, 511:512], zero[:, :], zero[:, 0:1], start=True, stop=False,
                                     skip_group_check=True)
                with pe.Fori(0, visits) as v:
                    done = pe.snap((before + v) * VC)
                    for h in range(VC):
                        pe.wait_ge(s_ohr[par], done + h + 1)
                        for j in range(NT):
                            ins = nc.tensor.matmul(
                                ps_a[par][j // 5][:, (j % 5) * PARTS * WIN:(j % 5 + 1) * PARTS * WIN],
                                oh_s[par][:, h, j * TR:j * TR + P], oh_d[par][:, h, :],
                                start=False, stop=False, skip_group_check=True)
                        ins.then_inc(s_ohu[par], 1)
                for b in range(2):
                    ins = nc.tensor.matmul(ps_a[par][b][:, 511:512], zero[:, :], zero[:, 0:1], start=False,
                                           stop=True, skip_group_check=True)
                ins.then_inc(s_wr, 1)

            with pe.Fori(0, NT // 2) as i:
                for s in range(2):
                    t = i * 2 + s
                    pe.wait_ge(s_xn, t + 1)
                    for b in range(2):
                        pe.wait_ge(s_lo, t * 2 + b + 1)
                        pe.wait_ge(s_xr, t * 2 + b + 1)
                        for k in range(4):
                            ins = nc.tensor.transpose(ps_t[b][:, k * TR:(k + 1) * TR],
                                                      xn[s][:, (4 * b + k) * P:(4 * b + k + 1) * P],
                                                      ident[0:TR, 0:TR])
                        ins.then_inc(s_tp, 1)
                    window(t, s, 0)
                    pe.wait_ge(s_lo, t * 2 + 4)
                    for q in range(WPT):
                        product(s, t, q * PIECES // WPT, (q + 1) * PIECES // WPT)
                        if q < WPT - 1:
                            window(t, s, q + 1)


NH = 16
DH = D // NH
M = 256
JP = D // P
NF = 2 * M // P
DV = DH + 1
CH = [(0, 4), (4, 4), (8, 2)]
TWO_PI = 6.28318501
ROUND = 1.5 * 2.0 ** 23
Z_MIN = 1e-6


def attention_stage(nc, xt_scr, wq, wk, wv, rf, o_scr):
    with ExitStack() as ctx:
        def sb(name, shape, dt):
            return ctx.enter_context(nc.sbuf_tensor(name, shape, dt))

        def sem(name):
            return ctx.enter_context(nc.semaphore(name))

        xa = sb("a_x", [P, 2, KD, N], F32R)
        w_raw = sb("a_wraw", [P, 3, D], F32)
        wt = sb("a_wt", [P, 3, 2, KD, P], F32R)
        qt = sb("a_qt", [P, 2, N], F32R)
        kt = sb("a_kt", [P, 2, N], F32R)
        vt = sb("a_vt", [P, N], F32)
        sq = sb("a_sq", [P, N], F32)
        bd = sb("a_bd", [P, 2, 2 * M], F32R)
        ub = [sb(f"a_u{s}", [P, 512], F32) for s in range(2)]
        rb = [sb(f"a_r{s}", [P, 512], F32) for s in range(2)]
        kl = [sb(f"a_kl{s}", [TR, 2, 2 * M], F32R) for s in range(2)]
        kh = [sb(f"a_kh{s}", [TR, 2, 2 * M], F32R) for s in range(2)]
        qf = sb("a_qf", [P, 2, NF, 500], F32)
        rf_in = qf[:, 0, 0, 0:4 * DH].rearrange("p (m a d) -> p m a d", m=2, a=2)
        bd32 = qf[:, 1, :, :].rearrange("p f n -> p (f n)")[:, 0:2 * M]
        kf = [qf[0:TR, s, :, :].rearrange("p f n -> p (f n)")[:, 0:4 * M].rearrange("p (f n) -> p f n", f=2)
              for s in range(2)]
        x_in = [qf[:, s, 2:4, :].rearrange("p f n -> p (f n)") for s in range(2)] + [vt[:, 0:KD * TR]]
        vl = sb("a_vl", [TR, NT, 2, DV], F32R)
        vh = sb("a_vh", [TR, NT, 2, DV], F32R)
        kv = sb("a_kv", [P, 2, NF, DV], F32)
        kvt = vt[0:DV, 0:4 * M].rearrange("v (h n) -> v h n", h=2)
        ob = sb("a_o", [TR, 4, P], F32)
        ot = sb("a_ot", [P, N], F32)
        es = sb("a_exp", [TR, 2, NT, 2], F32)
        zt = sb("a_z", [TR, 4, 4], F32)
        ident = sb("a_ident", [P, P], F32)
        hsel = sb("a_hsel", [P, 2], F32)
        c_round = sb("a_cround", [P, 1], F32)
        c_quarter = sb("a_cquarter", [P, 1], F32)
        c_ln = sb("a_cln", [P, 1], F32)

        gen = [ctx.enter_context(nc.psum_tensor(f"a_psg{s}", [P, 512], F32)) for s in range(3)]
        fea = [ctx.enter_context(nc.psum_tensor(f"a_psf{s}", [P, 512], F32)) for s in range(3)]
        acc = [ctx.enter_context(nc.psum_tensor(f"a_psa{s}", [P, 512], F32)) for s in range(2)]

        s_x = [sem(f"a_x_loaded{s}") for s in range(3)]
        s_xh = sem("a_x_high")
        s_xl = sem("a_x_low")
        s_rf = sem("a_rf_loaded")
        s_raw = [sem(f"a_weights_loaded{m}") for m in range(3)]
        s_cst = sem("a_const")
        s_bd = sem("a_bd")
        s_gen = sem("a_gen")
        s_fea = sem("a_fea")
        s_whi = sem("a_w_high")
        s_wlo = sem("a_w_low")
        s_hi = [sem("a_q_high"), sem("a_k_high")]
        s_lo = [sem("a_q_low"), sem("a_k_low")]
        s_sq = [sem("a_q_squared"), sem("a_k_squared")]
        s_vt = sem("a_v_copied")
        s_exp = [sem("a_q_exp"), sem("a_k_exp")]
        s_vs = sem("a_v_scaled")
        s_v1 = sem("a_v_ones")
        s_u = sem("a_rounded")
        s_r = sem("a_remainder")
        s_abs = sem("a_abs")
        s_sc = sem("a_sincos")
        s_vh = sem("a_v_high")
        s_vl = sem("a_v_low")
        s_kh = sem("a_k_features_high")
        s_kl = sem("a_k_features_low")
        s_kv = sem("a_kv_tile")
        s_kvc = sem("a_kv_copied")
        s_kvt = sem("a_kv_transposed")
        s_kve = sem("a_kv_evacuated")
        s_out = sem("a_out_product")
        s_z = sem("a_z_step")
        s_norm = sem("a_out_scaled")
        s_ot = sem("a_out_transposed")
        s_st = sem("a_stored")

        MM = 3 * KD
        K_PLAN = [[("p", 0, 0, 0, 6)], [("p", 0, 0, 6, 12)], [("p", 0, 0, 12, 18)], [("p", 0, 0, 18, MM)],
                  [("p", 0, 1, 0, 6)], [("p", 0, 1, 6, 12)], [("p", 0, 1, 12, 18)], [("p", 0, 1, 18, MM)],
                  [("p", 0, 2, 0, 12)], [("p", 0, 2, 12, MM), ("w", 1, 0)],
                  [("w", 1, 1), ("n", 0)], [("w", 2, 0), ("w", 2, 1)]]
        Q_PLAN = [[("p", 1, 0, 0, 12)],
                  [("p", 1, 0, 12, MM)],
                  [("p", 1, 1, 0, MM)],
                  [("p", 1, 2, 0, MM), ("o", 0)],
                  [("n", 1), ("p", 2, 0, 0, MM)],
                  [("p", 2, 1, 0, 12), ("o", 1)],
                  [("p", 2, 1, 12, MM), ("v", 0), ("w", 0, 0)],
                  [("p", 2, 2, 0, MM), ("v", 1), ("w", 0, 1), ("v", 2), ("o", 2)]]
        START = [("w", 1, 0), ("w", 1, 1), ("w", 2, 0), ("w", 2, 1), ("w", 0, 0), ("w", 0, 1),
                 ("p", 1, 0, 0, MM), ("p", 1, 1, 0, MM), ("p", 1, 2, 0, MM), ("n", 1),
                 ("p", 2, 0, 0, MM), ("p", 2, 1, 0, MM), ("p", 2, 2, 0, MM), ("v", 0), ("v", 1), ("v", 2)]

        def readers(pieces):
            found = []
            for piece in pieces:
                if piece[0] == "w":
                    found.append((s_wlo, 6, (4, 0, 2)[piece[1]] + piece[2]))
                elif piece[0] == "p" and piece[4] == MM:
                    found.append((s_vt, 3, piece[2]) if piece[1] == 2 else (s_lo[piece[1]], 3, piece[2]))
                elif piece[0] == "v":
                    found.append((s_vs, 3, piece[1]))
                elif piece[0] == "o":
                    found.append((s_ot, 3, piece[1]))
            return found

        READ = readers(piece for step in K_PLAN + Q_PLAN for piece in step)
        NG = len(READ)
        START_READ = readers(START)
        NS = len(START_READ)
        FREAD = [(s_r, NT + 12, 0)]
        for t in range(NT + 2):
            FREAD += [(s_r, NT + 12, t + 1)] if t + 1 < NT else []
            FREAD += [(s_exp[x[1]], 1, 0) for x in K_PLAN[t] if x[0] == "n"]
        for i in range(6):
            FREAD += [(s_r, NT + 12, NT + 2 * i), (s_r, NT + 12, NT + 2 * i + 1)]
            FREAD += [(s_exp[x[1]], 1, 0) for x in Q_PLAN[i] if x[0] == "n"]
        NU = NT + 12
        NE = len(FREAD)
        FS = 3
        assert NG % 3 == 0 and NS % 3 == 0 and NE % 3 == 0 and NU % 2 == 0
        UNIT = [f for f in range(NE) if FREAD[f][0] is s_r]
        NORM = {m: [f for f in range(NE) if FREAD[f][0] is s_exp[m]][0] for m in range(2)}

        def use(piece):
            key = {"w": lambda: (s_wlo, (4, 0, 2)[piece[1]] + piece[2]),
                   "p": lambda: (s_vt, piece[2]) if piece[1] == 2 else (s_lo[piece[1]], piece[2]),
                   "v": lambda: (s_vs, piece[1]), "o": lambda: (s_ot, piece[1])}[piece[0]]()
            where = [[g for g, r in enumerate(table) if r[0] is key[0] and r[2] == key[1]]
                     for table in (READ, START_READ)]
            return where[0][0], (where[1][0] if where[1] else None)

        def chunk(c):
            first, number = CH[c]
            return first * TR, number * TR

        def filled(eng, j, piece):
            g, g0 = use(piece)
            eng.wait_ge(s_gen, g0 + 1 if j is None else j * NG + NS + g + 1)
            return gen[(g0 if j is None else g) % 3]

        block = ctx.enter_context(nc.Block())

        def units():
            return [(c, h, m) for c in range(3) for h in range(2) for m in range(2)]

        @block.sync
        def _(sp):
            for m in (1, 2, 0):
                sp.dma_start(w_raw[:, m, :], (wq, wk, wv)[m][0:P, :]).then_inc(s_raw[m], 16)
            sp.dma_start(rf_in[:, :, 0, :], rf.rearrange("(m p) d -> p m d", p=P)).then_inc(s_rf, 16)
            sp.dma_start(rf_in[:, :, 1, :], rf.rearrange("(m p) d -> p m d", p=P)).then_inc(s_rf, 16)
            for t in range(NT):
                if t >= 3:
                    sp.wait_ge(s_xl, t - 2)
                sp.dma_start(x_in[t % 3], xt_scr[t, :, :]).then_inc(s_x[t % 3], 16)
            sp.wait_ge(s_gen, 6)
            for m in (1, 2, 0):
                sp.dma_start(w_raw[:, m, :], (wq, wk, wv)[m][P:2 * P, :]).then_inc(s_raw[m], 16)
            with sp.Fori(0, JP) as j:
                nxt = sp.snap((j + 2) % JP)
                for m in (1, 2, 0):
                    sp.wait_ge(s_gen, j * NG + NS + use(("w", m, 1))[0] + 1)
                    sp.dma_start(w_raw[:, m, :], (wq, wk, wv)[m][bass.ds(nxt * P, P), :]).then_inc(s_raw[m], 16)
                sp.wait_ge(s_ot, j * 3 + 6)
                sp.dma_start(o_scr[bass.ds(j, 1), :, :].rearrange("a p n -> p (a n)"), ot[:, :]).then_inc(s_st, 16)
            for m in range(3):
                sp.wait_ge(s_raw[m], 16 * (JP + 2))
            sp.wait_ge(s_st, 16 * (JP + 1))

        @block.gpsimd
        def _(pool):
            nc.gpsimd.memset(ident[:, :], 0.0).then_inc(s_cst, 1)
            nc.gpsimd.memset(hsel[:, :], 0.0).then_inc(s_cst, 1)
            nc.gpsimd.memset(bd32[:, :], 0.0).then_inc(s_cst, 1)
            nc.gpsimd.memset(c_round[:, :], ROUND).then_inc(s_cst, 1)
            nc.gpsimd.memset(c_quarter[:, :], float(np.float32(np.pi / 2))).then_inc(s_cst, 1)
            nc.gpsimd.memset(c_ln[:, :], -float(np.log(np.sqrt(M)))).then_inc(s_cst, 1)
            pool.wait_ge(s_cst, 6)
            nc.gpsimd.affine_select(out=ident[:, :], in_=ident[:, :], compare_op=ALU.not_equal, fill=1.0,
                                    base=0, pattern=[[-1, P]], channel_multiplier=1).then_inc(s_cst, 1)
            pool.wait_ge(s_cst, 7)
            nc.gpsimd.memset(hsel[0:DH, 0:1], 1.0).then_inc(s_cst, 1)
            pool.wait_ge(s_cst, 8)
            nc.gpsimd.memset(hsel[DH:P, 1:2], 1.0).then_inc(s_cst, 1)
            pool.sem_inc(s_lo[0], 3)
            pool.sem_inc(s_ot, 3)
            pool.sem_inc(s_exp[0], 1)
            pool.sem_inc(s_r, NU)
            pool.sem_inc(s_norm, 6)
            pool.sem_inc(s_sc, 2)
            pool.sem_inc(s_st, 16)

        @block.scalar
        def _(act):
            act.wait_ge(s_cst, 9)

            def read(j, piece):
                kind = piece[0]
                if kind == "n":
                    m = piece[1]
                    act.wait_ge(s_fea, 2 if j is None else j * NE + FS + NORM[m] + 1)
                    nc.scalar.activation(es[:, m, :, :], fea[1 if j is None else NORM[m] % 3][0:TR, 0:2 * NT].rearrange(
                        "p (t h) -> p t h", h=2), ACT.Exp, bias=c_ln[0:TR, 0:1], scale=-0.5).then_inc(s_exp[m], 1)
                elif kind == "w":
                    m, b = piece[1:]
                    bank = filled(act, j, piece)
                    nc.scalar.activation(wt[:, m, 0, 4 * b:4 * b + 4, :],
                                         bank[:, :].rearrange("p (k n) -> p k n", k=4), ACT.Copy).then_inc(s_whi, 1)
                elif kind == "p" and piece[4] == MM:
                    m, c = piece[1:3]
                    o, size = chunk(c)
                    bank = filled(act, j, piece)
                    if m < 2:
                        nc.scalar.activation((qt, kt)[m][:, 0, o:o + size], bank[:, 0:size], ACT.Copy
                                             ).then_inc(s_hi[m], 1)
                        nc.scalar.activation(sq[:, o:o + size], bank[:, 0:size], ACT.Square).then_inc(s_sq[m], 1)
                    else:
                        nc.scalar.activation(vt[:, o:o + size], bank[:, 0:size], ACT.Copy).then_inc(s_vt, 1)
                elif kind == "o":
                    c = piece[1]
                    o, size = chunk(c)
                    if c == 0:
                        act.wait_ge(s_st, (j + 1) * 16)
                    bank = filled(act, j, piece)
                    nc.scalar.activation(ot[:, o:o + size], bank[:, 0:size], ACT.Copy).then_inc(s_ot, 1)

            for n in range(6):
                read(None, START[n])
            act.wait_ge(s_bd, 1)
            nc.scalar.activation(bd[:, 0, :], bd32[:, :], ACT.Copy).then_inc(s_bd, 1)
            for t in range(NT):
                act.wait_ge(s_x[t % 3], 16 * (t // 3 + 1))
                nc.scalar.activation(xa[:, 0, :, t * TR:(t + 1) * TR], x_in[t % 3].rearrange("p (k n) -> p k n", k=KD),
                                     ACT.Copy).then_inc(s_xh, 1)
            for piece in START[6:]:
                read(None, piece)

            with act.Fori(0, JP) as j:
                def rounded(n, rows, size):
                    act.wait_ge(s_sc, j * NU + n + 1)
                    act.wait_ge(s_fea, j * NE + FS + UNIT[n] + 1)
                    nc.scalar.activation(ub[n % 2][0:rows, 0:size], fea[UNIT[n] % 3][0:rows, 0:size],
                                         ACT.Identity, bias=c_round[0:rows, 0:1]).then_inc(s_u, 1)

                def sincos(n, rows, size, sin_out, cos_out):
                    act.wait_ge(s_abs, j * NU + n + 1)
                    nc.scalar.activation(sin_out, rb[n % 2][0:rows, 0:size], ACT.Sin, scale=-TWO_PI)
                    nc.scalar.activation(cos_out, ub[n % 2][0:rows, 0:size], ACT.Sin,
                                         bias=c_quarter[0:rows, 0:1], scale=-TWO_PI).then_inc(s_sc, 1)

                for t in range(NT + 2):
                    if t < NT:
                        rounded(t, TR, 512)
                    if 0 < t <= NT:
                        k = (t - 1) % 2
                        if t - 1 >= 2:
                            act.wait_ge(s_kv, j * NT + t - 2)
                        sincos(t - 1, TR, 512, kf[k][:, 1, :], kf[k][:, 0, :])
                    for piece in K_PLAN[t]:
                        read(j, piece)

                act.wait_ge(s_kl, j * NT + NT)
                def q_sincos(n):
                    c, h, m = units()[n]
                    size = chunk(c)[1]
                    if c > 0:
                        act.wait_ge(s_out, j * 6 + 2 * (c - 1) + h + 1)
                    sincos(NT + n, P, size, qf[:, h, 2 + m, 0:size], qf[:, h, m, 0:size])

                for i in range(8):
                    for n in (2 * i, 2 * i + 1):
                        if n < 12:
                            rounded(NT + n, P, chunk(units()[n][0])[1])
                        if 0 < n < 13:
                            q_sincos(n - 1)
                    for piece in Q_PLAN[i]:
                        read(j, piece)

        @block.vector
        def _(dve):
            def read(j, piece):
                kind = piece[0]
                if kind == "w":
                    m, b = piece[1:]
                    n = (4, 0, 2)[m] + b
                    g, g0 = use(piece)
                    dve.wait_ge(s_whi, n + 1 if j is None else j * 6 + 6 + n + 1)
                    nc.vector.tensor_tensor(wt[:, m, 1, 4 * b:4 * b + 4, :],
                                            gen[(g0 if j is None else g) % 3][:, :].rearrange("p (k n) -> p k n", k=4),
                                            wt[:, m, 0, 4 * b:4 * b + 4, :].bitcast(F32), ALU.subtract
                                            ).then_inc(s_wlo, 1)
                elif kind == "p" and piece[4] == MM and piece[1] < 2:
                    m, c = piece[1:3]
                    o, size = chunk(c)
                    x = (qt, kt)[m]
                    g, g0 = use(piece)
                    dve.wait_ge(s_hi[m], c + 1 if j is None else j * 3 + (0, 3)[m] + c + 1)
                    dve.wait_ge(s_sq[m], c + 1 if j is None else j * 3 + (0, 3)[m] + c + 1)
                    nc.vector.tensor_tensor(x[:, 1, o:o + size], gen[(g0 if j is None else g) % 3][:, 0:size],
                                            x[:, 0, o:o + size].bitcast(F32), ALU.subtract).then_inc(s_lo[m], 1)
                elif kind == "v":
                    c = piece[1]
                    t0, nt = CH[c]
                    bank = filled(dve, j, piece)
                    dve.wait_ge(s_exp[1], 1 if j is None else j + 2)
                    n = c + 1 if j is None else j * 3 + 3 + c + 1
                    if c == 0:
                        e = es[:, 1, :, :]
                        k = 1 if j is None else j * 2 + 3
                        nc.vector.tensor_copy(vh[:, :, :, DH], e).then_inc(s_v1, 1)
                        dve.wait_ge(s_v1, k)
                        nc.vector.tensor_tensor(vl[:, :, :, DH], e, vh[:, :, :, DH].bitcast(F32), ALU.subtract
                                                ).then_inc(s_v1, 1)
                        if j is not None:
                            dve.wait_ge(s_sc, j * NU + NU + 2)
                    if c == 2:
                        dve.wait_ge(s_vl, n - 2)
                    raw = rb[c % 2][0:TR, 0:nt * P].rearrange("p (t h d) -> p t h d", t=nt, h=2)
                    nc.vector.tensor_tensor(raw, bank[0:TR, 0:nt * P].rearrange("p (t h d) -> p t h d", t=nt, h=2),
                                            es[:, 1, t0:t0 + nt, :].unsqueeze(3).broadcast_to([TR, nt, 2, DH]),
                                            ALU.mult).then_inc(s_vs, 1)
                    dve.wait_ge(s_vs, n)
                    nc.vector.tensor_copy(vh[:, t0:t0 + nt, :, 0:DH], raw).then_inc(s_vh, 1)
                    dve.wait_ge(s_vh, n)
                    nc.vector.tensor_tensor(vl[:, t0:t0 + nt, :, 0:DH], raw,
                                            vh[:, t0:t0 + nt, :, 0:DH].bitcast(F32), ALU.subtract).then_inc(s_vl, 1)

            for piece in START[:6]:
                read(None, piece)
            dve.wait_ge(s_cst, 9)
            dve.wait_ge(s_fea, 1)
            for h in range(2):
                for m in range(2):
                    ins = nc.vector.tensor_scalar(
                        bd32[DH * h:DH * h + DH, M * h + P * m:M * h + P * m + P],
                        fea[0][DH * h:DH * h + DH, P * m:P * m + P], float(1 / (2 * np.pi)), None, ALU.mult)
            ins.then_inc(s_bd, 1)
            dve.wait_ge(s_bd, 2)
            nc.vector.tensor_tensor(bd[:, 1, :], bd32[:, :], bd[:, 0, :].bitcast(F32), ALU.subtract).then_inc(s_bd, 1)
            for t in range(NT):
                dve.wait_ge(s_xh, t + 1)
                nc.vector.tensor_tensor(xa[:, 1, :, t * TR:(t + 1) * TR], x_in[t % 3].rearrange("p (k n) -> p k n", k=KD),
                                        xa[:, 0, :, t * TR:(t + 1) * TR].bitcast(F32), ALU.subtract).then_inc(s_xl, 1)
            for piece in START[6:]:
                read(None, piece)

            with dve.Fori(0, JP) as j:
                def remainder(n, rows, size):
                    u, r = ub[n % 2][0:rows, 0:size], rb[n % 2][0:rows, 0:size]
                    dve.wait_ge(s_sc, j * NU + n + 1)
                    dve.wait_ge(s_u, j * NU + n + 1)
                    nc.vector.scalar_tensor_tensor(out=r, in0=u, scalar=ROUND, in1=fea[UNIT[n] % 3][0:rows, 0:size],
                                                   op0=ALU.subtract, op1=ALU.subtract).then_inc(s_r, 1)
                    dve.wait_ge(s_r, j * NU + NU + n + 1)
                    nc.vector.tensor_scalar(u.bitcast(I32), r.bitcast(I32), 0x7fffffff, None,
                                            ALU.bitwise_and).then_inc(s_abs, 1)

                def scaled(c, h):
                    t0, nt = CH[c]
                    prod = acc[h][0:TR, 0:nt * DV].rearrange("p (t v) -> p t v", v=DV)
                    scale = es[:, 0, t0:t0 + nt, h]
                    first = (2 * c + h) * 4
                    dve.wait_ge(s_out, j * 6 + 2 * c + h + 1)
                    nc.vector.tensor_tensor(zt[:, 0, 0:nt], prod[:, :, DH], scale, ALU.mult).then_inc(s_z, 1)
                    dve.wait_ge(s_z, j * 24 + first + 1)
                    nc.vector.tensor_scalar(zt[:, 1, 0:nt], zt[:, 0, 0:nt], Z_MIN, None, ALU.max).then_inc(s_z, 1)
                    dve.wait_ge(s_z, j * 24 + first + 2)
                    nc.vector.reciprocal(zt[:, 2, 0:nt], zt[:, 1, 0:nt]).then_inc(s_z, 1)
                    dve.wait_ge(s_z, j * 24 + first + 3)
                    nc.vector.tensor_tensor(zt[:, 3, 0:nt], zt[:, 2, 0:nt], scale, ALU.mult).then_inc(s_z, 1)
                    dve.wait_ge(s_z, j * 24 + first + 4)
                    nc.vector.tensor_tensor(ob[:, 0:nt, DH * h:DH * h + DH], prod[:, :, 0:DH],
                                            zt[:, 3, 0:nt].unsqueeze(2).broadcast_to([TR, nt, DH]),
                                            ALU.mult).then_inc(s_norm, 1)

                dve.wait_ge(s_vl, j * 3 + 3)
                for t in range(NT + 2):
                    if t < NT:
                        remainder(t, TR, 512)
                    if 0 < t <= NT:
                        k = (t - 1) % 2
                        dve.wait_ge(s_sc, j * NU + t + 2)
                        nc.vector.tensor_copy(kh[k][:, :, :], kf[k]).then_inc(s_kh, 1)
                        dve.wait_ge(s_kh, j * NT + t)
                        nc.vector.tensor_tensor(kl[k][:, :, :], kf[k],
                                                kh[k][:, :, :].bitcast(F32), ALU.subtract).then_inc(s_kl, 1)
                    for piece in K_PLAN[t]:
                        read(j, piece)
                dve.wait_ge(s_kv, j * NT + NT)
                for h in range(2):
                    ins = nc.vector.tensor_copy(kvt[:, h, :], acc[h][0:DV, :])
                ins.then_inc(s_kvc, 1)
                for i in range(8):
                    if i < 6:
                        remainder(NT + 2 * i, P, chunk(i // 2)[1])
                    if i >= 2:
                        scaled(i // 2 - 1, i % 2)
                    if i < 6:
                        remainder(NT + 2 * i + 1, P, chunk(i // 2)[1])
                    if i == 0:
                        dve.wait_ge(s_kvt, j + 1)
                        for h in range(2):
                            ins = nc.vector.tensor_copy(kv[:, h, :, :].rearrange("p f v -> p (f v)"),
                                                        acc[h][:, 0:NF * DV])
                        ins.then_inc(s_kve, 1)
                    for piece in Q_PLAN[i]:
                        read(j, piece)

        @block.tensor
        def _(pe):
            def free(j, g):
                if j is None:
                    if g >= 3:
                        sem_, _, n = START_READ[g - 3]
                        pe.wait_ge(sem_, n + 1)
                elif g < 3:
                    sem_, per, n = READ[(g - 3) % NG]
                    pe.wait_ge(sem_, j * per + n + 1)
                    pe.wait_ge(s_vs, j * 3 + 3)
                else:
                    sem_, per, n = READ[g - 3]
                    pe.wait_ge(sem_, j * per + per + n + 1)

            def free_fea(j, f):
                sem_, per, n = FREAD[(f - 3) % NE]
                pe.wait_ge(sem_, j * per + n + 1 + (per if f >= 3 else 0))

            PASSES = ((0, 0), (0, 1), (1, 0))

            def do(j, piece):
                kind = piece[0]
                if kind == "n":
                    m = piece[1]
                    if j is None:
                        bank = fea[1]
                        pe.wait_ge(s_sq[m], 3)
                    else:
                        free_fea(j, NORM[m])
                        bank = fea[NORM[m] % 3]
                        pe.wait_ge(s_sq[m], j * 3 + 3 + (0, 3)[m])
                    for t in range(NT):
                        ins = nc.tensor.matmul(bank[0:TR, 2 * t:2 * t + 2], sq[:, t * TR:(t + 1) * TR], hsel[:, :],
                                               start=True, stop=True)
                    ins.then_inc(s_fea, 1)
                    return
                g, g0 = use(piece)
                bank = gen[(g0 if j is None else g) % 3]
                if kind != "p" or piece[3] == 0:
                    free(j, g0 if j is None else g)
                if kind == "w":
                    m, b = piece[1:]
                    if b == 0:
                        pe.wait_ge(s_raw[m], 16 if j is None else j * 16 + 32)
                    for k in range(4):
                        ins = nc.tensor.transpose(bank[:, k * P:(k + 1) * P],
                                                  w_raw[:, m, (4 * b + k) * P:(4 * b + k + 1) * P], ident[:, :])
                    ins.then_inc(s_gen, 1)
                elif kind == "p":
                    m, c, first, end = piece[1:]
                    o, size = chunk(c)
                    if c == 0 and first == 0:
                        last = (6, 2, 4)[m]
                        pe.wait_ge(s_wlo, last if j is None else j * 6 + last + (0, 6, 6)[m])
                    if j is None and m == 1:
                        pe.wait_ge(s_xl, CH[c][0] + CH[c][1])
                    for n in range(first, end):
                        a, k = n // KD, n % KD
                        pw, px = PASSES[a]
                        ins = nc.tensor.matmul(bank[:, 0:size], wt[:, m, pw, k, :], xa[:, px, k, o:o + size],
                                               start=(n == 0), stop=(n == MM - 1))
                    if end == MM:
                        ins.then_inc(s_gen, 1)
                elif kind == "v":
                    c = piece[1]
                    t0, nt = CH[c]
                    pe.wait_ge(s_vt, c + 1 if j is None else j * 3 + 3 + c + 1)
                    for i in range(nt):
                        ins = nc.tensor.transpose(bank[0:TR, i * P:(i + 1) * P],
                                                  vt[:, (t0 + i) * TR:(t0 + i + 1) * TR], ident[:, :])
                    ins.then_inc(s_gen, 1)
                else:
                    c = piece[1]
                    pe.wait_ge(s_norm, j * 6 + 6 + 2 * c + 2)
                    for i in range(CH[c][1]):
                        ins = nc.tensor.transpose(bank[:, i * TR:(i + 1) * TR], ob[:, i, :], ident[0:TR, 0:TR])
                    ins.then_inc(s_gen, 1)

            pe.wait_ge(s_cst, 9)
            for piece in START[:6]:
                do(None, piece)
            pe.wait_ge(s_rf, 32)
            for m in range(2):
                ins = nc.tensor.transpose(fea[0][:, m * P:(m + 1) * P], rf_in[:, m, :, :].rearrange("p a d -> p (a d)"),
                                          ident[:, :])
            ins.then_inc(s_fea, 1)
            for piece in START[6:]:
                do(None, piece)
            pe.sem_inc(s_fea, 1)
            pe.wait_ge(s_bd, 3)
            pe.wait_ge(s_exp[1], 1)
            with pe.Fori(0, JP) as j:
                pe.wait_ge(s_lo[1], j * 3 + 3)
                def k_angles(t):
                    free_fea(j, UNIT[t])
                    for a, (pk, pr) in enumerate(PASSES):
                        ins = nc.tensor.matmul(fea[UNIT[t] % 3][0:TR, :], kt[:, pk, t * TR:(t + 1) * TR],
                                               bd[:, pr, :], start=(a == 0), stop=(a == 2))
                    ins.then_inc(s_fea, 1)

                k_angles(0)
                for t in range(NT + 2):
                    if t + 1 < NT:
                        k_angles(t + 1)
                    if t >= 2:
                        s = t - 2
                        if s == 0:
                            pe.wait_ge(s_v1, j * 2 + 2)
                            pe.wait_ge(s_vl, j * 3 + 3)
                            pe.wait_ge(s_norm, j * 6 + 6)
                        pe.wait_ge(s_kl, j * NT + s + 1)
                        for h in range(2):
                            for a, (pv, pk) in enumerate(((vh, kh), (vh, kl), (vl, kh))):
                                ins = nc.tensor.matmul(acc[h][0:DV, :], pv[:, s, h, :],
                                                       pk[s % 2][:, :, h * M:(h + 1) * M],
                                                       start=(s == 0 and a == 0), stop=(s == NT - 1 and a == 2))
                        ins.then_inc(s_kv, 1)
                    for piece in K_PLAN[t]:
                        do(j, piece)

                def angles(c, h):
                    o, size = chunk(c)
                    for m in range(2):
                        n = NT + 4 * c + 2 * h + m
                        free_fea(j, UNIT[n])
                        for a, (pr, pq) in enumerate(PASSES):
                            ins = nc.tensor.matmul(fea[UNIT[n] % 3][:, 0:size],
                                                   bd[:, pr, h * M + m * P:h * M + m * P + P], qt[:, pq, o:o + size],
                                                   start=(a == 0), stop=(a == 2))
                        ins.then_inc(s_fea, 1)

                def output(c, h):
                    nt = CH[c][1]
                    if c == 0:
                        pe.wait_ge(s_kve, j + 1)
                    else:
                        pe.wait_ge(s_norm, j * 6 + 6 + 2 * (c - 1) + h + 1)
                    pe.wait_ge(s_sc, j * NU + NT + 4 * c + 2 * h + 4)
                    for i in range(nt):
                        for f in range(NF):
                            ins = nc.tensor.matmul(acc[h][0:TR, i * DV:(i + 1) * DV], qf[:, h, f, i * TR:(i + 1) * TR],
                                                   kv[:, h, f, :], start=(f == 0), stop=(f == NF - 1))
                    ins.then_inc(s_out, 1)

                pe.wait_ge(s_lo[0], j * 3 + 6)
                for i in range(8):
                    if i >= 2:
                        output(i // 2 - 1, i % 2)
                    if i < 6:
                        angles(i // 2, i % 2)
                    for piece in Q_PLAN[i]:
                        do(j, piece)
                    if i == 0:
                        pe.wait_ge(s_kvc, j + 1)
                        for h in range(2):
                            for f in range(NF):
                                ins = nc.tensor.transpose(acc[h][:, f * DV:(f + 1) * DV], kvt[:, h, f * P:(f + 1) * P],
                                                          ident[0:DV, 0:DV])
                        ins.then_inc(s_kvt, 1)


FI = 512
KI = FI // P


def output_stage(nc, o_scr, wo, x, edge_scr, y_scr, y_sb, x1_scr, norm):
    CPT = NC // NT
    with ExitStack() as ctx:
        def sb(name, shape, dt):
            return ctx.enter_context(nc.sbuf_tensor(name, shape, dt))

        def sem(name):
            return ctx.enter_context(nc.semaphore(name))

        ident = sb("o_ident", [P, P], F32)
        zero = sb("o_zero", [1, TR], BF16)
        w_raw = [sb(f"o_wraw{s}", [P, D], F32) for s in range(4)]
        wt = sb("o_wt", [P, 2, KD, D], F32R)
        of = [sb(f"o_of{s}", [P, KD, TR], F32) for s in range(2)]
        oh = [sb(f"o_oh{s}", [P, 2, KD, TR], F32R) for s in range(2)]
        xin = [sb(f"o_x{s}", [TR, D], F32) for s in range(2)]
        xout = [sb(f"o_xo{s}", [TR, D], F32) for s in range(2)]
        edge_t = sb("o_edge", [TR, 3, NC], F32)
        tile_f = sb("o_tile", [TR, 2, NC], F32)
        row_f = sb("o_row", [TR, 2, NC], F32)
        wrest = sb("o_wrest", [TR, 2, NC], F32)
        wpart = sb("o_wpart", [TR, NC, 4], BF16)
        iota_t = sb("o_iotat", [TR, CPT, NT], F32)
        iota_p = sb("o_iotap", [TR, CPT, TR], F32)
        oh_t = [sb(f"o_oht{s}", [TR, 2, CPT, NT], BF16) for s in range(2)]
        rhs = [sb(f"o_rhs{s}", [TR, 2, CPT, 4, NT], BF16) for s in range(2)]
        oh_p = [sb(f"o_ohp{s}", [TR, 2, CPT, TR + 1], BF16) for s in range(2)]
        sums = sb("o_sums", [TR, 2, 4 * NT], F32)
        nrm = sb("o_nrm", [TR, 2, 6, NT], F32)

        ps_t = [ctx.enter_context(nc.psum_tensor(f"o_pst{s}", [P, 512], F32)) for s in range(4)]
        ps_o = [ps[0:TR, :] for ps in ps_t]
        ps_h = [ctx.enter_context(nc.psum_tensor(f"o_psh{s}", [TR, 512], F32)) for s in range(2)]

        s_w = [sem(f"o_w_loaded{s}") for s in range(4)]
        s_o = [sem(f"o_o_loaded{s}") for s in range(2)]
        s_x = [sem(f"o_x_loaded{s}") for s in range(2)]
        s_e = sem("o_edge_loaded")
        s_cst = sem("o_const")
        s_tp = sem("o_transposed")
        s_whi = sem("o_w_high")
        s_wlo = sem("o_w_low")
        s_ohi = sem("o_o_high")
        s_olo = sem("o_o_low")
        s_pr = sem("o_product")
        s_add = sem("o_added")
        s_st = [sem(f"o_stored{s}") for s in range(2)]
        s_hp = sem("o_hist_step")
        s_ht = sem("o_hist_tile_onehot")
        s_hr = sem("o_hist_onehot")
        s_hu = sem("o_hist_used")
        s_sq = sem("o_hist_sqrt")
        s_y = sem("o_y_loaded")
        block = ctx.enter_context(nc.Block())

        @block.sync
        def _(sp):
            for k in range(KD):
                if k >= 4:
                    sp.wait_ge(s_tp, 2 * (k - 3))
                sp.dma_start(w_raw[k % 4][:, :], wo[k * P:(k + 1) * P, :]).then_inc(s_w[k % 4], 16)
                if k == KD - 1:
                    sp.dma_start(edge_t[:, :, :], edge_scr).then_inc(s_e, 16)
                    for s in range(2):
                        sp.dma_start(of[s][:, :, :], o_scr[:, :, s * TR:(s + 1) * TR].rearrange("j p n -> p j n")
                                     ).then_inc(s_o[s], 16)
                        sp.dma_start(xin[s][:, :], x[s * TR:(s + 1) * TR, :]).then_inc(s_x[s], 16)
            for j in range(NT):
                sp.dma_start(y_sb[:, j, :].bitcast(F32), y_scr[j]).then_inc(s_y, 16)
            for s in range(2):
                sp.sem_inc(s_st[s], 16)
            with sp.Fori(0, NT // 2) as i:
                for s in range(2):
                    nxt = sp.snap((i * 2 + s + 2) % NT)
                    sp.wait_ge(s_olo, i * 2 + s + 1)
                    sp.dma_start(of[s][:, :, :], o_scr[:, :, bass.ds(nxt * TR, TR)].rearrange("j p n -> p j n")
                                 ).then_inc(s_o[s], 16)
                    sp.wait_ge(s_add, (i * 2 + s) * 2 + 6)
                    sp.dma_start(xin[s][:, :], x[bass.ds(nxt * TR, TR), :]).then_inc(s_x[s], 16)
                    sp.dma_start(x1_scr[bass.ds(i * 2 + s, 1), :, :].rearrange("a p n -> p (a n)"),
                                 xout[s][:, :]).then_inc(s_st[s], 16)
            sp.wait_ge(s_hp, HIST_STEPS)
            sp.wait_ge(s_y, 16 * NT)
            for s in range(2):
                sp.wait_ge(s_st[s], 16 * (NT // 2 + 1))
                sp.wait_ge(s_o[s], 16 * (NT // 2 + 1))
                sp.wait_ge(s_x[s], 16 * (NT // 2 + 1))

        @block.gpsimd
        def _(pool):
            nc.gpsimd.memset(ident[:, :], 0.0).then_inc(s_cst, 1)
            nc.gpsimd.memset(zero[:, :], 0.0).then_inc(s_cst, 1)
            nc.gpsimd.iota(iota_t[:, :, :].bitcast(I32), pattern=[[0, CPT], [1, NT]], base=0,
                           channel_multiplier=0).then_inc(s_cst, 1)
            nc.gpsimd.iota(iota_p[:, :, :].bitcast(I32), pattern=[[0, CPT], [1, TR]], base=0,
                           channel_multiplier=0).then_inc(s_cst, 1)
            nc.gpsimd.memset(wpart[:, :, 0], 1.0).then_inc(s_cst, 1)
            pool.wait_ge(s_cst, 5)
            nc.gpsimd.affine_select(out=ident[:, :], in_=ident[:, :], compare_op=ALU.not_equal, fill=1.0,
                                    base=0, pattern=[[-1, P]], channel_multiplier=1).then_inc(s_cst, 1)
            nc.gpsimd.tensor_copy(iota_t[:, :, :], iota_t[:, :, :].bitcast(I32)).then_inc(s_cst, 1)
            nc.gpsimd.tensor_copy(iota_p[:, :, :], iota_p[:, :, :].bitcast(I32)).then_inc(s_cst, 1)

        @block.scalar
        def _(act):
            for n in range(2 * KD):
                m, b = n // 2, n % 2
                act.wait_ge(s_tp, n + 1)
                nc.scalar.activation(wt[:, 0, 4 * b:4 * b + 4, m * P:(m + 1) * P],
                                     ps_t[n % 4][:, :].rearrange("p (k n) -> p k n", k=4), ACT.Copy).then_inc(s_whi, 1)

            def high(s, i, t):
                act.wait_ge(s_o[s], i * 16 + 16)
                act.wait_ge(s_pr, t * 2 + 2)
                nc.scalar.activation(oh[s][:, 0, :, :], of[s][:, :, :], ACT.Copy).then_inc(s_ohi, 1)

            high(0, 0, 0)
            with act.Fori(0, NT // 2) as i:
                for s in range(2):
                    high(1 - s, i + s, i * 2 + s + 1)
            act.wait_ge(s_hp, HIST_SQRT)
            nc.scalar.activation(nrm[:, :, 4, :], nrm[:, :, 3, :], ACT.Sqrt).then_inc(s_sq, 1)

        @block.vector
        def _(dve):
            steps = [0]

            def step(ins):
                steps[0] += 1
                ins.then_inc(s_hp, 1)
                dve.wait_ge(s_hp, steps[0])

            for n in range(2 * KD):
                m, b = n // 2, n % 2
                dve.wait_ge(s_whi, n + 1)
                nc.vector.tensor_tensor(wt[:, 1, 4 * b:4 * b + 4, m * P:(m + 1) * P],
                                        ps_t[n % 4][:, :].rearrange("p (k n) -> p k n", k=4),
                                        wt[:, 0, 4 * b:4 * b + 4, m * P:(m + 1) * P].bitcast(F32),
                                        ALU.subtract).then_inc(s_wlo, 1)
            dve.wait_ge(s_e, 16)
            dve.wait_ge(s_cst, 8)
            step(nc.vector.tensor_scalar(tile_f[:, :, :], edge_t[:, 0:2, :], 1.0 / TR, -0.5 + 0.5 / TR, ALU.mult, ALU.add))
            step(nc.vector.tensor_scalar(tile_f[:, :, :], tile_f[:, :, :], ROUND, ROUND, ALU.add, ALU.subtract))
            step(nc.vector.scalar_tensor_tensor(out=row_f[:, :, :], in0=tile_f[:, :, :], scalar=-float(TR),
                                                in1=edge_t[:, 0:2, :], op0=ALU.mult, op1=ALU.add))
            step(nc.vector.tensor_copy(wpart[:, :, 1], edge_t[:, 2, :]))
            step(nc.vector.tensor_tensor(wrest[:, 0, :], edge_t[:, 2, :], wpart[:, :, 1], ALU.subtract))
            step(nc.vector.tensor_copy(wpart[:, :, 2], wrest[:, 0, :]))
            step(nc.vector.tensor_tensor(wrest[:, 1, :], wrest[:, 0, :], wpart[:, :, 2], ALU.subtract))
            step(nc.vector.tensor_copy(wpart[:, :, 3], wrest[:, 1, :]))

            def low(s, t):
                dve.wait_ge(s_ohi, t + 1)
                nc.vector.tensor_tensor(oh[s][:, 1, :, :], of[s][:, :, :], oh[s][:, 0, :, :].bitcast(F32),
                                        ALU.subtract).then_inc(s_olo, 1)

            low(0, 0)
            with dve.Fori(0, NT // 2) as i:
                for s in range(2):
                    t = i * 2 + s
                    low(1 - s, t + 1)
                    dve.wait_ge(s_hu, t + 1)
                    edges = bass.ds(t * CPT, CPT)
                    for e in range(2):
                        nc.vector.tensor_tensor(oh_p[s][:, e, :, 0:TR], iota_p[:, :, :],
                                                row_f[:, e, edges].unsqueeze(2).broadcast_to([TR, CPT, TR]), ALU.is_equal)
                        nc.vector.tensor_tensor(oh_t[s][:, e, :, :], iota_t[:, :, :],
                                                tile_f[:, e, edges].unsqueeze(2).broadcast_to([TR, CPT, NT]),
                                                ALU.is_equal).then_inc(s_ht, 1)
                    for e in range(2):
                        dve.wait_ge(s_ht, t * 2 + e + 1)
                        ins = nc.vector.tensor_tensor(rhs[s][:, e, :, :, :],
                                                      oh_t[s][:, e, :, :].unsqueeze(2).broadcast_to([TR, CPT, 4, NT]),
                                                      wpart[:, edges, :].unsqueeze(3).broadcast_to([TR, CPT, 4, NT]),
                                                      ALU.mult)
                    ins.then_inc(s_hr, 1)
                    dve.wait_ge(s_x[s], i * 16 + 16)
                    dve.wait_ge(s_st[s], i * 16 + 16)
                    for b in range(2):
                        dve.wait_ge(s_pr, t * 2 + b + 5)
                        nc.vector.tensor_tensor(xout[s][:, b * 512:(b + 1) * 512], ps_o[2 * s + b],
                                                xin[s][:, b * 512:(b + 1) * 512], ALU.add).then_inc(s_add, 1)
            dve.wait_ge(s_hu, NT + 2)
            for e in range(2):
                step(nc.vector.tensor_copy(sums[:, e, :], ps_h[e][:, 0:4 * NT]))
            sv = sums[:, :, :].rearrange("p e (m t) -> p e m t", m=4)
            step(nc.vector.tensor_scalar(nrm[:, :, 0, :], sv[:, :, 0, :], 1.0, None, ALU.max))
            step(nc.vector.tensor_tensor(nrm[:, :, 1, :], sv[:, :, 1, :], sv[:, :, 2, :], ALU.add))
            step(nc.vector.tensor_tensor(nrm[:, :, 1, :], nrm[:, :, 1, :], sv[:, :, 3, :], ALU.add))
            step(nc.vector.scalar_tensor_tensor(out=nrm[:, :, 2, :], in0=sv[:, :, 0, :], scalar=0.0,
                                                in1=nrm[:, :, 1, :], op0=ALU.is_equal, op1=ALU.add))
            step(nc.vector.tensor_tensor(nrm[:, :, 3, :], nrm[:, :, 2, :], nrm[:, :, 0, :], ALU.mult))
            assert steps[0] == HIST_SQRT
            dve.wait_ge(s_sq, 1)
            step(nc.vector.reciprocal(nrm[:, :, 5, :], nrm[:, :, 4, :]))
            step(nc.vector.tensor_tensor(nrm[:, :, 4, :], nrm[:, :, 5, :], nrm[:, :, 5, :], ALU.mult))
            step(nc.vector.tensor_tensor(nrm[:, :, 4, :], nrm[:, :, 4, :], nrm[:, :, 3, :], ALU.mult))
            step(nc.vector.tensor_scalar(nrm[:, :, 4, :], nrm[:, :, 4, :], -0.5, 1.5, ALU.mult, ALU.add))
            step(nc.vector.tensor_tensor(norm[:, :, :], nrm[:, :, 4, :].rearrange("p e t -> p t e"),
                                         nrm[:, :, 5, :].rearrange("p e t -> p t e"), ALU.mult))
            assert steps[0] == HIST_STEPS

        @block.tensor
        def _(pe):
            pe.sem_inc(s_hu, 2)
            pe.sem_inc(s_pr, 4)
            pe.sem_inc(s_add, 4)
            pe.wait_ge(s_cst, 6)
            for n in range(2 * KD):
                m, b = n // 2, n % 2
                if b == 0:
                    pe.wait_ge(s_w[m % 4], (m // 4 + 1) * 16)
                if n >= 4:
                    pe.wait_ge(s_wlo, n - 3)
                for k in range(4):
                    ins = nc.tensor.transpose(ps_t[n % 4][:, k * P:(k + 1) * P],
                                              w_raw[m % 4][:, (4 * b + k) * P:(4 * b + k + 1) * P], ident[:, :])
                ins.then_inc(s_tp, 1)
            pe.wait_ge(s_wlo, 2 * KD)
            for e in range(2):
                nc.tensor.matmul(ps_h[e][:, 511:512], zero[:, :], zero[:, 0:1], start=True, stop=False,
                                 skip_group_check=True)
            with pe.Fori(0, NT // 2) as i:
                for s in range(2):
                    t = i * 2 + s
                    pe.wait_ge(s_olo, t + 1)
                    for b in range(2):
                        pe.wait_ge(s_add, t * 2 + b + 1)
                        for a, (po, pw) in enumerate(((0, 0), (0, 1), (1, 0))):
                            for k in range(KD):
                                ins = nc.tensor.matmul(ps_o[2 * s + b], oh[s][:, po, k, :],
                                                       wt[:, pw, k, b * 512:(b + 1) * 512],
                                                       start=(a == 0 and k == 0), stop=(a == 2 and k == KD - 1))
                        ins.then_inc(s_pr, 1)
                    pe.wait_ge(s_hr, t + 1)
                    for q in range(CPT):
                        for e in range(2):
                            ins = nc.tensor.matmul(ps_h[e][:, 0:4 * NT], oh_p[s][:, e, q, 0:TR],
                                                   rhs[s][:, e, q, :, :].rearrange("p m t -> p (m t)"),
                                                   start=False, stop=False, skip_group_check=True)
                    ins.then_inc(s_hu, 1)


HIST_SQRT = 8 + 2 + 5
HIST_STEPS = HIST_SQRT + 5


HO = FI // P
LN_STEPS = 17
H_STEPS = 6
Q_MAX = 127.0
Q_MIN = -128.0
Q_EPS = 1e-5


def feed_forward_stage(nc, yl, at_scr, norm, x1_scr, gnn_b, w_gate, w_up, w_down, out):
    with ExitStack() as outer:
        wgt = outer.enter_context(nc.sbuf_tensor("f_wgt", [P, KD, FI], BF16))
        wut = outer.enter_context(nc.sbuf_tensor("f_wut", [P, KD, FI], BF16))
        wdt = outer.enter_context(nc.sbuf_tensor("f_wdt", [P, KI, D], BF16))
        ident = outer.enter_context(nc.sbuf_tensor("f_ident", [P, P], BF16))
        wsc = outer.enter_context(nc.sbuf_tensor("f_wsc", [P, 3], F32))
        yh = outer.enter_context(nc.sbuf_tensor("f_yh", [TR, NT, D], F32R))
        bias = outer.enter_context(nc.sbuf_tensor("f_bias", [TR, D], F32))
        a_raw = [outer.enter_context(nc.sbuf_tensor(f"f_araw{s}", [TR, WPT, NT, WIN], F32)) for s in range(2)]
        s_nb = outer.enter_context(nc.semaphore("f_bias_loaded"))
        s_a = [outer.enter_context(nc.semaphore(f"f_a_loaded{s}")) for s in range(2)]
        first_loads = (at_scr, gnn_b, bias, a_raw, s_nb, s_a)
        feed_forward_operands(nc, first_loads, w_gate, w_up, w_down, wgt, wut, wdt, ident, wsc, norm, yh, yl)
        feed_forward_tiles(nc, first_loads, x1_scr, wgt, wut, wdt, ident, wsc, norm, yh, yl, out)


def feed_forward_operands(nc, first_loads, w_gate, w_up, w_down, wgt, wut, wdt, ident, wsc, norm, yh, yl):
    at_scr, gnn_b, bias, a_raw, s_nb, s_a = first_loads
    with ExitStack() as ctx:
        def sb(name, shape, dt):
            return ctx.enter_context(nc.sbuf_tensor(name, shape, dt))

        def sem(name):
            return ctx.enter_context(nc.semaphore(name))

        WN = FI * D // P
        raw = [sb(f"t_raw{m}", [P, WN], F32) for m in range(3)]
        tern = [sb(f"t_tern{m}", [P, WN], BF16) for m in range(3)]
        part = sb("t_part", [P, 2, 3], F32)
        scale = sb("t_scale", [P, 3], F32)
        ones = sb("t_ones", [P, P], F32)
        neg_round = sb("t_nround", [P, 1], F32)
        ps_s = [ctx.enter_context(nc.psum_tensor(f"t_pss{m}", [P, 512], F32)) for m in range(3)]
        ps_t = [ctx.enter_context(nc.psum_tensor(f"t_pst{s}", [P, 1024], BF16)) for s in range(2)]
        s_w = [sem(f"t_loaded{m}") for m in range(3)]
        s_c = sem("t_const")
        s_yh = sem("t_y_high")
        s_yl = sem("t_y_low")
        s_v = sem("t_vector")
        s_sum = sem("t_summed")
        s_abs = sem("t_abs_summed")
        s_tern = sem("t_ternary")
        s_tp = sem("t_transposed")
        s_ev = sem("t_evacuated")
        VS = 6
        BEFORE = ((0, 1, 2, 3), (4, 5, 6), (7, 8, 9))
        block = ctx.enter_context(nc.Block())

        @block.sync
        def _(sp):
            for m, w in enumerate((w_gate, w_up, w_down)):
                sp.dma_start(raw[m][:, :], w.rearrange("(a p) n -> p a n", p=P)).then_inc(s_w[m], 16)
            sp.dma_start(bias[:, :], gnn_b.rearrange("(a n) -> a n", a=1).broadcast_to([TR, D])).then_inc(s_nb, 16)
            for s in range(2):
                sp.dma_start(a_raw[s][:, :, :, :].rearrange("p w j d -> p w (j d)"),
                             at_scr[s * WPT:(s + 1) * WPT, :, :].rearrange("w p n -> p w n")).then_inc(s_a[s], 16)
            sp.wait_ge(s_yl, NT)

        @block.gpsimd
        def _(pool):
            nc.gpsimd.memset(ident[:, :], 0.0).then_inc(s_c, 1)
            nc.gpsimd.memset(ones[:, :], 1.0).then_inc(s_c, 1)
            nc.gpsimd.memset(neg_round[:, :], -ROUND).then_inc(s_c, 1)
            pool.wait_ge(s_c, 3)
            nc.gpsimd.affine_select(out=ident[:, :], in_=ident[:, :], compare_op=ALU.not_equal, fill=1.0,
                                    base=0, pattern=[[-1, P]], channel_multiplier=1).then_inc(s_c, 1)

        @block.vector
        def _(dve):
            steps = [0]

            def step(ins):
                steps[0] += 1
                ins.then_inc(s_v, 1)
                dve.wait_ge(s_v, steps[0])

            for m in range(3):
                for j in BEFORE[m]:
                    dve.wait_ge(s_yh, j + 1)
                    nc.vector.scalar_tensor_tensor(out=yl[:, j, :], in0=yl[:, j, :].bitcast(F32),
                                                   scalar=norm[:, j, 0:1], in1=yh[:, j, :].bitcast(F32),
                                                   op0=ALU.mult, op1=ALU.subtract).then_inc(s_yl, 1)
                dve.wait_ge(s_w[m], 16)
                step(nc.vector.tensor_reduce(part[:, 0, m:m + 1], raw[m][:, 0:WN // 2], axis=AX.X, op=ALU.add,
                                             apply_absolute_value=True))
                dve.wait_ge(s_sum, m + 1)
                step(nc.vector.tensor_scalar(wsc[:, m:m + 1], ps_s[m][:, 0:1], 1.0 / (FI * D), Q_EPS, ALU.mult, ALU.max))
                step(nc.vector.reciprocal(scale[:, m:m + 1], wsc[:, m:m + 1]))
                step(nc.vector.tensor_scalar(raw[m][:, :], raw[m][:, :], scale[:, m:m + 1], 1.0, ALU.mult, ALU.min))
                step(nc.vector.tensor_scalar(raw[m][:, :], raw[m][:, :], -1.0, ROUND, ALU.max, ALU.add))
                step(nc.vector.tensor_scalar(tern[m][:, 0:WN // 2], raw[m][:, 0:WN // 2], ROUND, None, ALU.subtract))

        @block.tensor
        def _(pe):
            pe.wait_ge(s_c, 4)
            n = 0
            for m in range(3):
                pe.wait_ge(s_v, VS * m + 1)
                pe.wait_ge(s_abs, m + 1)
                for e in range(2):
                    ins = nc.tensor.matmul(ps_s[m][:, 0:1], ones[:, :], part[:, e, m:m + 1], start=(e == 0), stop=(e == 1))
                ins.then_inc(s_sum, 1)
                pe.wait_ge(s_tern, m + 1)
                pe.wait_ge(s_v, VS * m + VS)
                rows, cols = (HO, KD) if m < 2 else (KD, KI)
                for c in range(4):
                    if n >= 2:
                        pe.wait_ge(s_ev, n - 1)
                    for b in range(8):
                        blk = 8 * c + b
                        k, a = blk // rows, blk % rows
                        ins = nc.tensor.transpose(ps_t[n % 2][:, b * P:(b + 1) * P],
                                                  tern[m][:, a * cols * P + k * P:a * cols * P + (k + 1) * P], ident[:, :])
                    ins.then_inc(s_tp, 1)
                    n += 1

        @block.scalar
        def _(act):
            act.wait_ge(s_c, 4)

            def y_high(m):
                for j in BEFORE[m]:
                    nc.scalar.activation(yh[:, j, :], yl[:, j, :].bitcast(F32), ACT.Copy,
                                         scale=norm[:, j, 0:1]).then_inc(s_yh, 1)

            def abs_sum(m):
                act.wait_ge(s_w[m], 16)
                nc.scalar.activation(tern[m][:, WN // 2:WN], raw[m][:, WN // 2:WN], ACT.Abs,
                                     accum_out=part[:, 1, m:m + 1]).then_inc(s_abs, 1)

            y_high(0)
            abs_sum(0)
            for n in range(12):
                m, c = n // 4, n % 4
                if c == 0:
                    if m < 2:
                        y_high(m + 1)
                    act.wait_ge(s_v, VS * m + VS - 1)
                    nc.scalar.activation(tern[m][:, WN // 2:WN], raw[m][:, WN // 2:WN], ACT.Identity,
                                         bias=neg_round[:, 0:1]).then_inc(s_tern, 1)
                    if m < 2:
                        abs_sum(m + 1)
                wt = (wgt, wut, wdt)[m]
                act.wait_ge(s_tp, n + 1)
                nc.scalar.activation(wt[:, :, :].rearrange("p k n -> p (k n)")[:, c * 1024:(c + 1) * 1024],
                                     ps_t[n % 2][:, :], ACT.Copy).then_inc(s_ev, 1)


def feed_forward_tiles(nc, first_loads, x1_scr, wgt, wut, wdt, ident, wsc, norm, yh, yl, out):
    at_scr, _, bias, a_raw, s_nb, s_a = first_loads
    with ExitStack() as ctx:
        def sb(name, shape, dt):
            return ctx.enter_context(nc.sbuf_tensor(name, shape, dt))

        def sem(name):
            return ctx.enter_context(nc.semaphore(name))

        ah = [sb(f"f_ah{s}", [TR, NT, TR], F32R) for s in range(2)]
        al = [sb(f"f_al{s}", [TR, NT, TR], F32R) for s in range(2)]
        xin = [sb(f"f_xin{s}", [TR, D], F32) for s in range(2)]
        x1 = [sb(f"f_x1{s}", [TR, D], F32) for s in range(2)]
        z = sb("f_z", [TR, D], F32)
        xn = sb("f_xn", [TR, D], F32)
        q = sb("f_q", [TR, D], BF16)
        qt = sb("f_qt", [P, KD, P], BF16)
        gate = sb("f_gate", [TR, FI], F32)
        h = sb("f_h", [TR, FI], F32)
        hr = sb("f_hr", [TR, FI], F32)
        hq = sb("f_hq", [TR, FI], BF16)
        hqt = sb("f_hqt", [P, KI, P], BF16)
        o = [sb(f"f_out{s}", [TR, D], F32) for s in range(2)]
        eps = sb("f_eps", [TR, 1], F32)
        rnd = sb("f_round", [TR, 2], F32)
        bn = sb("f_bn", [TR, 2, 6], F32)
        mv = sb("f_mv", [TR, 2], F32)
        std = sb("f_std", [TR, 1], F32)
        lnw = sb("f_lnw", [TR, 4], F32)
        amax = [sb(f"f_amax{s}", [TR, 2], F32) for s in range(2)]
        dq = [sb(f"f_dq{s}", [TR, 2], F32) for s in range(2)]
        hmax = sb("f_hmax", [TR, 2], F32)
        dqh = sb("f_dqh", [TR, 1], F32)

        ps_a = [ctx.enter_context(nc.psum_tensor(f"f_psa{b}", [TR, 512], F32)) for b in range(2)]
        ps_q = ctx.enter_context(nc.psum_tensor("f_psq", [P, 1024], BF16))
        ps_h = ctx.enter_context(nc.psum_tensor("f_psh", [P, 1024], BF16))
        ps_g = ctx.enter_context(nc.psum_tensor("f_psg", [TR, 512], F32))
        ps_u = ctx.enter_context(nc.psum_tensor("f_psu", [TR, 512], F32))
        ps_d = [ctx.enter_context(nc.psum_tensor(f"f_psd{b}", [TR, 512], F32)) for b in range(2)]

        s_x = [sem(f"f_x_loaded{s}") for s in range(2)]
        s_st = [sem(f"f_stored{s}") for s in range(2)]
        s_c = sem("f_const")
        s_ah = sem("f_a_high")
        s_al = sem("f_a_low")
        s_agg = sem("f_edges_summed")
        s_ln = sem("f_ln")
        s_lna = sem("f_ln_scalar")
        s_qtp = sem("f_q_transposed")
        s_qt = sem("f_qt_ready")
        s_gu = sem("f_gate_up")
        s_hv = sem("f_h")
        s_ha = sem("f_h_scalar")
        s_htp = sem("f_h_transposed")
        s_ht = sem("f_ht_ready")
        s_dn = sem("f_down")
        s_o = sem("f_out_ready")
        block = ctx.enter_context(nc.Block())

        def tiles(eng, step):
            for n in range(2):
                step(n % 2, True, n > 0, False, n - 2)
            with eng.Fori(0, (NT - 2) // 2) as i:
                for s in range(2):
                    step(s, True, True, True, i * 2 + s)
            for n in range(NT, NT + 2):
                step(n % 2, False, n == NT, True, n - 2)

        @block.sync
        def _(sp):
            def load_a(s, t):
                sp.dma_start(a_raw[s][:, :, :, :].rearrange("p w j d -> p w (j d)"),
                             at_scr[bass.ds(t * WPT, WPT), :, :].rearrange("w p n -> p w n")).then_inc(s_a[s], 16)

            def load_x(s, t):
                sp.dma_start(xin[s][:, :], x1_scr[bass.ds(t, 1), :, :].rearrange("a p n -> p (a n)")).then_inc(s_x[s], 16)

            for s in range(2):
                load_x(s, s)
            for s in range(2):
                sp.sem_inc(s_st[s], 16)

            def step(s, edges, gate_up, down, b):
                if edges:
                    nxt = (b + 4) % NT if isinstance(b, int) else sp.snap((b + 4) % NT)
                    sp.wait_ge(s_al, b + 3)
                    load_a(s, nxt)
                    sp.wait_ge(s_ln, b * LN_STEPS + 2 * LN_STEPS + 3)
                    load_x(s, nxt)
                if down:
                    sp.wait_ge(s_o, b * 2 + 2)
                    sp.dma_start(out[bass.ds(b * TR, TR), :], o[s][:, :]).then_inc(s_st[s], 16)

            tiles(sp, step)
            for s in range(2):
                sp.wait_ge(s_a[s], 16 * (NT // 2 + 1))
                sp.wait_ge(s_x[s], 16 * (NT // 2 + 1))
                sp.wait_ge(s_st[s], 16 * (NT // 2 + 1))

        @block.gpsimd
        def _(pool):
            nc.gpsimd.memset(eps[:, :], LN_EPS).then_inc(s_c, 1)
            nc.gpsimd.memset(rnd[:, 0:1], ROUND).then_inc(s_c, 1)
            nc.gpsimd.memset(rnd[:, 1:2], -ROUND).then_inc(s_c, 1)

        @block.scalar
        def _(act):
            def a_high(s, b, peeled):
                act.wait_ge(s_a[s], b * 8 + 32 - 8 * s)
                if not peeled:
                    act.wait_ge(s_agg, b * 2 + 2)
                nc.scalar.activation(ah[s][:, :, :].rearrange("p j (w d) -> p w j d", w=WPT),
                                     a_raw[s][:, :, :, :], ACT.Copy).then_inc(s_ah, 1)

            act.wait_ge(s_c, 3)
            a_high(0, -2, True)
            def step(s, edges, gate_up, down, b):
                if edges:
                    a_high(1 - s, b + 1, isinstance(b, int) and b < -1)
                if down:
                    act.wait_ge(s_hv, b * H_STEPS + 4)
                    nc.scalar.activation(hr[:, :], h[:, :], ACT.Identity, bias=rnd[:, 0:1],
                                         scale=hmax[:, 1:2]).then_inc(s_ha, 1)
                    act.wait_ge(s_hv, b * H_STEPS + 6)
                    nc.scalar.activation(hq[:, :], hr[:, :], ACT.Identity, bias=rnd[:, 1:2]).then_inc(s_ha, 1)
                    act.wait_ge(s_htp, b + 1)
                    nc.scalar.activation(hqt[:, :, 0:TR], ps_h[:, 0:KI * P].rearrange("p (k n) -> p k n", k=KI)[:, :, 0:TR],
                                         ACT.Copy).then_inc(s_ht, 1)
                if gate_up:
                    act.wait_ge(s_qtp, b + 2)
                    nc.scalar.activation(qt[:, :, 0:TR], ps_q[:, :].rearrange("p (k n) -> p k n", k=KD)[:, :, 0:TR],
                                         ACT.Copy).then_inc(s_qt, 1)
                if edges:
                    act.wait_ge(s_ln, b * LN_STEPS + 2 * LN_STEPS + 6)
                    nc.scalar.activation(std[:, :], mv[:, 1:2], ACT.Sqrt, bias=eps[:, 0:1]).then_inc(s_lna, 1)
                    act.wait_ge(s_ln, b * LN_STEPS + 2 * LN_STEPS + 12)
                    nc.scalar.activation(xn[:, :], x1[s][:, :], ACT.Identity, bias=lnw[:, 3:4],
                                         scale=lnw[:, 0:1]).then_inc(s_lna, 1)
                if gate_up:
                    act.wait_ge(s_gu, b + 2)
                    nc.scalar.activation(gate[:, :], ps_g[:, :], ACT.Silu, scale=dq[1 - s][:, 0:1]).then_inc(s_ha, 1)
                if edges:
                    act.wait_ge(s_ln, b * LN_STEPS + 2 * LN_STEPS + 15)
                    nc.scalar.activation(z[:, :], xn[:, :], ACT.Identity, bias=rnd[:, 0:1],
                                         scale=amax[s][:, 1:2]).then_inc(s_lna, 1)
                    act.wait_ge(s_ln, b * LN_STEPS + 2 * LN_STEPS + 17)
                    nc.scalar.activation(q[:, :], z[:, :], ACT.Identity, bias=rnd[:, 1:2]).then_inc(s_lna, 1)

            tiles(act, step)

        @block.vector
        def _(dve):
            def a_low(s, b):
                dve.wait_ge(s_ah, b + 3)
                view = "p j (w d) -> p w j d"
                nc.vector.tensor_tensor(al[s][:, :, :].rearrange(view, w=WPT), a_raw[s][:, :, :, :],
                                        ah[s][:, :, :].rearrange(view, w=WPT).bitcast(F32), ALU.subtract).then_inc(s_al, 1)

            dve.wait_ge(s_nb, 16)
            a_low(0, -2)
            def step(s, edges, gate_up, down, b):
                k = [0]
                kh = [0]

                def ln(ins):
                    k[0] += 1
                    ins.then_inc(s_ln, 1)
                    if k[0] not in (4, 5):
                        dve.wait_ge(s_ln, b * LN_STEPS + 2 * LN_STEPS + k[0])

                def hs(ins):
                    kh[0] += 1
                    ins.then_inc(s_hv, 1)
                    dve.wait_ge(s_hv, b * H_STEPS + H_STEPS + kh[0])

                def last_h(ins):
                    ins.then_inc(s_hv, 1)

                if edges:
                    a_low(1 - s, b + 1)
                if down:
                    dve.wait_ge(s_ha, b * 3 + 2)
                    last_h(nc.vector.tensor_scalar(hr[:, :], hr[:, :], ROUND + Q_MIN, ROUND + Q_MAX, ALU.max, ALU.min))
                if edges:
                    if not isinstance(b, int) or b >= -1:
                        dve.wait_ge(s_lna, b * 4 + 8)
                    for m in range(2):
                        dve.wait_ge(s_agg, b * 2 + 5 + m)
                        ln(nc.vector.scalar_tensor_tensor(
                            out=z[:, m * 512:(m + 1) * 512], in0=ps_a[m][:, :],
                            scalar=norm[:, b + 2, 1:2] if isinstance(b, int) else norm[:, bass.ds(b + 2, 1), 1],
                            in1=bias[:, m * 512:(m + 1) * 512], op0=ALU.mult, op1=ALU.add))
                if down:
                    dve.wait_ge(s_st[s], b * 8 + 16 - 8 * s)
                    for m in range(2):
                        dve.wait_ge(s_dn, b * 2 + 1 + m)
                        nc.vector.scalar_tensor_tensor(out=o[s][:, m * 512:(m + 1) * 512], in0=ps_d[m][:, :],
                                                       scalar=dqh[:, 0:1], in1=x1[s][:, m * 512:(m + 1) * 512],
                                                       op0=ALU.mult, op1=ALU.add).then_inc(s_o, 1)
                    if edges or gate_up:
                        dve.wait_ge(s_o, b * 2 + 2)
                if edges:
                    dve.wait_ge(s_x[s], b * 8 + 32 - 8 * s)
                    ln(nc.vector.scalar_tensor_tensor(out=x1[s][:, :], in0=z[:, :], scalar=0.0, in1=xin[s][:, :],
                                                      op0=ALU.max, op1=ALU.add))
                    for m in range(2):
                        ln(nc.vector.bn_stats(bn[:, m, :], x1[s][:, m * 512:(m + 1) * 512]))
                    dve.drain()
                    ln(nc.vector.bn_aggr(mv[:, :], bn[:, :, :].rearrange("p a b -> p (a b)")))
                    dve.wait_ge(s_lna, b * 4 + 9)
                    ln(nc.vector.reciprocal(lnw[:, 0:1], std[:, :]))
                    ln(nc.vector.tensor_tensor(lnw[:, 1:2], lnw[:, 0:1], lnw[:, 0:1], ALU.mult))
                    ln(nc.vector.scalar_tensor_tensor(out=lnw[:, 1:2], in0=mv[:, 1:2], scalar=LN_EPS,
                                                      in1=lnw[:, 1:2], op0=ALU.add, op1=ALU.mult))
                    ln(nc.vector.tensor_scalar(lnw[:, 1:2], lnw[:, 1:2], -0.5, 1.5, ALU.mult, ALU.add))
                    ln(nc.vector.tensor_tensor(lnw[:, 0:1], lnw[:, 0:1], lnw[:, 1:2], ALU.mult))
                    ln(nc.vector.scalar_tensor_tensor(out=lnw[:, 3:4], in0=mv[:, 0:1], scalar=-1.0,
                                                      in1=lnw[:, 0:1], op0=ALU.mult, op1=ALU.mult))
                    dve.wait_ge(s_lna, b * 4 + 10)
                    ln(nc.vector.tensor_reduce(amax[s][:, 0:1], xn[:, :], axis=AX.X, op=ALU.max,
                                               apply_absolute_value=True))
                    ln(nc.vector.tensor_scalar(amax[s][:, 0:1], amax[s][:, 0:1], Q_EPS, 1.0 / Q_MAX, ALU.max, ALU.mult))
                    ln(nc.vector.reciprocal(amax[s][:, 1:2], amax[s][:, 0:1]))
                    ln(nc.vector.tensor_scalar(dq[s][:, :], wsc[0:TR, 0:2], amax[s][:, 0:1], None, ALU.mult))
                if gate_up:
                    dve.wait_ge(s_ha, b * 3 + 4)
                    hs(nc.vector.scalar_tensor_tensor(out=h[:, :], in0=ps_u[:, :], scalar=dq[1 - s][:, 1:2],
                                                      in1=gate[:, :], op0=ALU.mult, op1=ALU.mult))
                    hs(nc.vector.tensor_reduce(hmax[:, 0:1], h[:, :], axis=AX.X, op=ALU.max,
                                               apply_absolute_value=True))
                    hs(nc.vector.tensor_scalar(hmax[:, 0:1], hmax[:, 0:1], Q_EPS, 1.0 / Q_MAX, ALU.max, ALU.mult))
                    hs(nc.vector.reciprocal(hmax[:, 1:2], hmax[:, 0:1]))
                    hs(nc.vector.tensor_scalar(dqh[:, 0:1], hmax[:, 0:1], wsc[0:TR, 2:3], None, ALU.mult))
                if edges:
                    dve.wait_ge(s_lna, b * 4 + 11)
                    ln(nc.vector.tensor_scalar(z[:, :], z[:, :], ROUND + Q_MIN, ROUND + Q_MAX, ALU.max, ALU.min))
                    assert k[0] == LN_STEPS
                if gate_up:
                    assert kh[0] == H_STEPS - 1

            tiles(dve, step)

        @block.tensor
        def _(pe):
            def edge_sums(s, b, m, peeled):
                if m == 0:
                    pe.wait_ge(s_al, b + 3)
                if not peeled:
                    pe.wait_ge(s_ln, b * LN_STEPS + LN_STEPS + 1 + m)
                for a, (pa, py) in enumerate(((ah, yh), (ah, yl), (al, yh))):
                    for j in range(NT):
                        ins = nc.tensor.matmul(ps_a[m][:, :], pa[s][:, j, :], py[:, j, m * 512:(m + 1) * 512],
                                               start=(a == 0 and j == 0), stop=(a == 2 and j == NT - 1))
                ins.then_inc(s_agg, 1)

            def step(s, edges, gate_up, down, b):
                peeled = isinstance(b, int) and b < -1
                if edges:
                    edge_sums(s, b, 0, peeled)
                    edge_sums(s, b, 1, peeled)
                if down:
                    pe.wait_ge(s_ha, b * 3 + 3)
                    for k in range(KI):
                        ins = nc.tensor.transpose(ps_h[:, k * P:k * P + TR], hq[:, k * P:(k + 1) * P],
                                                  ident[0:TR, 0:TR])
                    ins.then_inc(s_htp, 1)
                    pe.wait_ge(s_ht, b + 1)
                    if not isinstance(b, int) or b >= 1:
                        pe.wait_ge(s_o, b * 2)
                    for m in range(2):
                        for k in range(KI):
                            ins = nc.tensor.matmul(ps_d[m][:, :], hqt[:, k, 0:TR], wdt[:, k, m * 512:(m + 1) * 512],
                                                   start=(k == 0), stop=(k == KI - 1))
                        ins.then_inc(s_dn, 1)
                if gate_up:
                    pe.wait_ge(s_lna, b * 4 + 8)
                    for k in range(KD):
                        ins = nc.tensor.transpose(ps_q[:, k * P:k * P + TR], q[:, k * P:(k + 1) * P],
                                                  ident[0:TR, 0:TR])
                    ins.then_inc(s_qtp, 1)
                    pe.wait_ge(s_qt, b + 2)
                    if down:
                        pe.wait_ge(s_hv, b * H_STEPS + 1)
                    for w, ps in ((wgt, ps_g), (wut, ps_u)):
                        for k in range(KD):
                            ins = nc.tensor.matmul(ps[:, :], qt[:, k, 0:TR], w[:, k, :], start=(k == 0), stop=(k == KD - 1))
                    ins.then_inc(s_gu, 1)

            tiles(pe, step)


_INS = ("x", "src", "dst", "edge_weight", "L0_gnn_W", "L0_gnn_b", "L0_mix_wq", "L0_mix_wk", "L0_mix_wv", "L0_mix_wo",
        "L0_mix_rf", "L0_ffn_w_gate", "L0_ffn_w_up", "L0_ffn_w_down")


def graph_layer(nc, x, src, dst, edge_weight, gnn_w, gnn_b, wq, wk, wv, wo, rf, w_gate, w_up, w_down, out):
    def scratch(name, shape):
        return nc.dram_tensor(name, shape, F32, kind="Internal").ap()

    y_scr = scratch("y_scr", (NT, TR, D))
    xt_scr = scratch("xt_scr", (NT, P, KD * TR))
    at_scr = scratch("at_scr", (NW, TR, NT * WIN))
    edge_scr = scratch("edge_scr", (TR, 3, NC))
    o_scr = scratch("o_scr", (KD, P, N))
    x1_scr = scratch("x1_scr", (NT, TR, D))
    node_stage(nc, x, src, dst, edge_weight, gnn_w, y_scr, xt_scr, at_scr, edge_scr)
    attention_stage(nc, xt_scr, wq, wk, wv, rf, o_scr)
    with nc.sbuf_tensor("y_sb", [TR, NT, D], F32R) as y_sb, nc.sbuf_tensor("norm_sb", [TR, NT, 2], F32) as norm:
        output_stage(nc, o_scr, wo, x, edge_scr, y_scr, y_sb, x1_scr, norm)
        feed_forward_stage(nc, y_sb, at_scr, norm, x1_scr, gnn_b, w_gate, w_up, w_down, out)


def kernel(**inputs):
    import numpy as _np
    import concourse.bacc as _bacc
    from concourse import mybir as _mybir
    from concourse.bass_utils import run_bass_kernel_spmd as _run

    nc = _bacc.Bacc("TRN2", target_bir_lowering=False, num_devices=1)
    arrays, args = {}, []
    for name in _INS:
        a = _np.ascontiguousarray(inputs[name])
        arrays[f"in_{name}_dram"] = a
        args.append(nc.dram_tensor(f"in_{name}_dram", a.shape, _mybir.dt.from_np(a.dtype), kind="ExternalInput").ap())
    args.append(nc.dram_tensor("out_0_dram", (N, D), F32, kind="ExternalOutput").ap())
    graph_layer(nc, *args)
    r = _run(nc, [arrays], core_ids=[0])
    return r.results[0]["out_0_dram"]
```
